# Optimizing a Trainium2 kernel written in Bass

```python
import numpy as np
import jax
import jax.numpy as jnp

def _softmax(x, axis=-1):
    return jax.nn.softmax(x, axis=axis)

def _gelu(x):
    return jax.nn.gelu(x, approximate=True)

def _silu(x):
    return jax.nn.silu(x)

def _sigmoid(x):
    return jax.nn.sigmoid(x)

def _layernorm(x, axis=-1, eps=1e-05):
    m = jnp.mean(x, axis=axis, keepdims=True)
    v = jnp.var(x, axis=axis, keepdims=True)
    return (x - m) / jnp.sqrt(v + eps)

def _scatter_add(tgt, idx, src, axis=0):
    return tgt.at[idx].add(src)

def _segment_sum(src, seg, n):
    return jax.ops.segment_sum(src, seg, n)
kernel_name = 'mk_pixart_seq_d2_seqx_r2_ecfdef'

def setup_inputs(seed: int=0):
    np.random.seed(seed)
    _w = jnp.asarray

    def _rec_inputs():
        import jax
        import jax.numpy as jnp
        _rk = jax.random.key(seed)
        x = -0.0003929 + 0.9999 * jax.random.normal(jax.random.fold_in(_rk, 1), (2, 2048, 512), jnp.float32)
        _lenS = 2048 - jax.random.randint(jax.random.fold_in(_rk, 7), (2,), 0, max(1, 2048 // 4) + 1, jnp.int32)
        _lenS2 = 77 - jax.random.randint(jax.random.fold_in(_rk, 8), (2,), 0, max(1, 77 // 4) + 1, jnp.int32)
        _ctx_1024P = jax.random.normal(jax.random.fold_in(_rk, 11), (2, 16, 512), jnp.float32)
        _ctx_1024c = jax.random.dirichlet(jax.random.fold_in(_rk, 511), 0.3 * jnp.ones((16,), jnp.float32), (2, 77))
        _ctx_1024t = jnp.einsum('bsk,bkd->bsd', _ctx_1024c, _ctx_1024P)
        _ctx_1024t = _ctx_1024t * jax.lax.rsqrt(jnp.mean(jnp.square(_ctx_1024t)) + 1e-12) * 0.953939
        ctx_1024 = -1.39393e-06 + 0.999914 * (_ctx_1024t + 0.3 * jax.random.normal(jax.random.fold_in(_rk, 611), (2, 77, 512), jnp.float32))
        cond_1024 = -0.00920427 + 1.00102 * jax.random.normal(jax.random.fold_in(_rk, 12), (2, 512), jnp.float32)
        return (x, ctx_1024, cond_1024)
    x, ctx_1024, cond_1024 = _rec_inputs()

    def _L0_xcond_setup():
        import jax, jax.numpy as jnp
        import numpy as np
        EPS = 1e-05

        def _ada_ln(x, c, W_ss, b_ss):
            mu = jnp.mean(x, axis=-1, keepdims=True)
            var = jnp.mean((x - mu) ** 2, axis=-1, keepdims=True)
            h = (x - mu) / jnp.sqrt(var + EPS)
            ss = jax.nn.silu(c) @ W_ss + b_ss
            scale, bias = jnp.split(ss, 2, axis=-1)
            return (1.0 + scale)[:, None, :] * h + bias[:, None, :]
        key = jax.random.key(seed)
        ks = jax.random.split(key, 12)
        B, Lq, Lkv, H = (8, 1024, 256, 512)
        s = 0.02
        return {'x_q': jax.random.normal(ks[0], (B, Lq, H), jnp.float32), 'x_kv': jax.random.normal(ks[1], (B, Lkv, H), jnp.float32), 't_vec': jax.random.normal(ks[2], (B, H), jnp.float32), 'Wq': jax.random.normal(ks[3], (H, H), jnp.float32) * s, 'bq': jnp.zeros((H,), jnp.float32), 'Wkv': jax.random.normal(ks[4], (H, 2 * H), jnp.float32) * s, 'bkv': jnp.zeros((2 * H,), jnp.float32), 'Wp': jax.random.normal(ks[5], (H, H), jnp.float32) * s, 'bp': jnp.zeros((H,), jnp.float32), 'Wss_q': jax.random.normal(ks[6], (H, 2 * H), jnp.float32) * s, 'bss_q': jnp.zeros((2 * H,), jnp.float32), 'Wss_kv': jax.random.normal(ks[7], (H, 2 * H), jnp.float32) * s, 'bss_kv': jnp.zeros((2 * H,), jnp.float32)}
    _L0_xcond_all = _L0_xcond_setup()
    _L0_xcond_in = {k: v for k, v in _L0_xcond_all.items() if k in ('Wq', 'bq', 'Wkv', 'bkv', 'Wp', 'bp', 'Wss_q', 'bss_q', 'Wss_kv', 'bss_kv')}
    del _L0_xcond_all

    def _L1_xcond_setup():
        import jax, jax.numpy as jnp
        import numpy as np
        EPS = 1e-06
        H = 16

        def layer_norm(x, gamma=None, beta=None):
            x32 = x.astype(jnp.float32)
            mu = jnp.mean(x32, axis=-1, keepdims=True)
            var = jnp.var(x32, axis=-1, keepdims=True)
            y = (x32 - mu) * jax.lax.rsqrt(var + EPS)
            if gamma is not None:
                y = y * gamma + beta
            return y.astype(x.dtype)

        def mha(q, k, v):
            B, Nq, C = q.shape
            d = C // H
            qh = q.reshape(B, Nq, H, d)
            kh = k.reshape(B, k.shape[1], H, d)
            vh = v.reshape(B, v.shape[1], H, d)
            scores = jnp.einsum('bqhd,bkhd->bhqk', qh, kh) / jnp.sqrt(jnp.asarray(d, q.dtype))
            attn = jax.nn.softmax(scores, axis=-1)
            out = jnp.einsum('bhqk,bkhd->bqhd', attn, vh)
            return out.reshape(B, Nq, C)
        key = jax.random.key(seed)
        ks = jax.random.split(key, 24)
        B, N, C, M, Cc = (4, 1024, 512, 512, 512)
        hid = 4 * C
        s = 0.02
        return {'x': jax.random.normal(ks[0], (B, N, C), jnp.float32), 'mod': jax.random.normal(ks[1], (B, C), jnp.float32), 'context': jax.random.normal(ks[2], (B, M, Cc), jnp.float32), 'ada_w': jax.random.normal(ks[3], (C, 6 * C), jnp.float32) * s, 'ada_b': jnp.zeros((6 * C,), jnp.float32), 'qkv_w': jax.random.normal(ks[4], (C, 3 * C), jnp.float32) * s, 'qkv_b': jnp.zeros((3 * C,), jnp.float32), 'self_o_w': jax.random.normal(ks[5], (C, C), jnp.float32) * s, 'self_o_b': jnp.zeros((C,), jnp.float32), 'norm2_g': jnp.ones((C,), jnp.float32), 'norm2_b': jnp.zeros((C,), jnp.float32), 'q_w': jax.random.normal(ks[6], (C, C), jnp.float32) * s, 'q_b': jnp.zeros((C,), jnp.float32), 'kv_w': jax.random.normal(ks[7], (Cc, 2 * C), jnp.float32) * s, 'kv_b': jnp.zeros((2 * C,), jnp.float32), 'cross_o_w': jax.random.normal(ks[8], (C, C), jnp.float32) * s, 'cross_o_b': jnp.zeros((C,), jnp.float32), 'mlp_w1': jax.random.normal(ks[9], (C, hid), jnp.float32) * s, 'mlp_b1': jnp.zeros((hid,), jnp.float32), 'mlp_w2': jax.random.normal(ks[10], (hid, C), jnp.float32) * s, 'mlp_b2': jnp.zeros((C,), jnp.float32)}
    _L1_xcond_all = _L1_xcond_setup()
    _L1_xcond_in = {k: v for k, v in _L1_xcond_all.items() if k in ('ada_w', 'ada_b', 'qkv_w', 'qkv_b', 'self_o_w', 'self_o_b', 'norm2_g', 'norm2_b', 'q_w', 'q_b', 'kv_w', 'kv_b', 'cross_o_w', 'cross_o_b', 'mlp_w1', 'mlp_b1', 'mlp_w2', 'mlp_b2')}
    del _L1_xcond_all
    return {'x': x, 'ctx_1024': ctx_1024, 'cond_1024': cond_1024, 'L0_xcond_Wq': _L0_xcond_in['Wq'], 'L0_xcond_bq': _L0_xcond_in['bq'], 'L0_xcond_Wkv': _L0_xcond_in['Wkv'], 'L0_xcond_bkv': _L0_xcond_in['bkv'], 'L0_xcond_Wp': _L0_xcond_in['Wp'], 'L0_xcond_bp': _L0_xcond_in['bp'], 'L0_xcond_Wss_q': _L0_xcond_in['Wss_q'], 'L0_xcond_bss_q': _L0_xcond_in['bss_q'], 'L0_xcond_Wss_kv': _L0_xcond_in['Wss_kv'], 'L0_xcond_bss_kv': _L0_xcond_in['bss_kv'], 'L1_xcond_ada_w': _L1_xcond_in['ada_w'], 'L1_xcond_ada_b': _L1_xcond_in['ada_b'], 'L1_xcond_qkv_w': _L1_xcond_in['qkv_w'], 'L1_xcond_qkv_b': _L1_xcond_in['qkv_b'], 'L1_xcond_self_o_w': _L1_xcond_in['self_o_w'], 'L1_xcond_self_o_b': _L1_xcond_in['self_o_b'], 'L1_xcond_norm2_g': _L1_xcond_in['norm2_g'], 'L1_xcond_norm2_b': _L1_xcond_in['norm2_b'], 'L1_xcond_q_w': _L1_xcond_in['q_w'], 'L1_xcond_q_b': _L1_xcond_in['q_b'], 'L1_xcond_kv_w': _L1_xcond_in['kv_w'], 'L1_xcond_kv_b': _L1_xcond_in['kv_b'], 'L1_xcond_cross_o_w': _L1_xcond_in['cross_o_w'], 'L1_xcond_cross_o_b': _L1_xcond_in['cross_o_b'], 'L1_xcond_mlp_w1': _L1_xcond_in['mlp_w1'], 'L1_xcond_mlp_b1': _L1_xcond_in['mlp_b1'], 'L1_xcond_mlp_w2': _L1_xcond_in['mlp_w2'], 'L1_xcond_mlp_b2': _L1_xcond_in['mlp_b2']}

def reference(x, ctx_1024, cond_1024, L0_xcond_Wq, L0_xcond_bq, L0_xcond_Wkv, L0_xcond_bkv, L0_xcond_Wp, L0_xcond_bp, L0_xcond_Wss_q, L0_xcond_bss_q, L0_xcond_Wss_kv, L0_xcond_bss_kv, L1_xcond_ada_w, L1_xcond_ada_b, L1_xcond_qkv_w, L1_xcond_qkv_b, L1_xcond_self_o_w, L1_xcond_self_o_b, L1_xcond_norm2_g, L1_xcond_norm2_b, L1_xcond_q_w, L1_xcond_q_b, L1_xcond_kv_w, L1_xcond_kv_b, L1_xcond_cross_o_w, L1_xcond_cross_o_b, L1_xcond_mlp_w1, L1_xcond_mlp_b1, L1_xcond_mlp_w2, L1_xcond_mlp_b2):
    import jax
    import jax.numpy as jnp

    def _L0_xcond_ref(x_q, x_kv, t_vec, Wq, bq, Wkv, bkv, Wp, bp, Wss_q, bss_q, Wss_kv, bss_kv):
        import jax, jax.numpy as jnp
        import numpy as np
        EPS = 1e-05

        def _ada_ln(x, c, W_ss, b_ss):
            mu = jnp.mean(x, axis=-1, keepdims=True)
            var = jnp.mean((x - mu) ** 2, axis=-1, keepdims=True)
            h = (x - mu) / jnp.sqrt(var + EPS)
            ss = jax.nn.silu(c) @ W_ss + b_ss
            scale, bias = jnp.split(ss, 2, axis=-1)
            return (1.0 + scale)[:, None, :] * h + bias[:, None, :]
        B, Lq, H = x_q.shape
        Lkv = x_kv.shape[1]
        nh = 16
        dh = H // nh
        xq = _ada_ln(x_q, t_vec, Wss_q, bss_q)
        xkv = _ada_ln(x_kv, t_vec, Wss_kv, bss_kv)
        q = (xq @ Wq + bq).reshape(B, Lq, nh, dh)
        kv = (xkv @ Wkv + bkv).reshape(B, Lkv, 2, nh, dh)
        k = kv[:, :, 0]
        v = kv[:, :, 1]
        scores = jnp.einsum('bqhd,bkhd->bhqk', q, k) / jnp.sqrt(jnp.float32(dh))
        attn = jax.nn.softmax(scores, axis=-1)
        out = jnp.einsum('bhqk,bkhd->bqhd', attn, v).reshape(B, Lq, H)
        return x_q + (out @ Wp + bp)

    def _L1_xcond_ref(x, mod, context, ada_w, ada_b, qkv_w, qkv_b, self_o_w, self_o_b, norm2_g, norm2_b, q_w, q_b, kv_w, kv_b, cross_o_w, cross_o_b, mlp_w1, mlp_b1, mlp_w2, mlp_b2):
        import jax, jax.numpy as jnp
        import numpy as np
        EPS = 1e-06
        H = 16

        def layer_norm(x, gamma=None, beta=None):
            x32 = x.astype(jnp.float32)
            mu = jnp.mean(x32, axis=-1, keepdims=True)
            var = jnp.var(x32, axis=-1, keepdims=True)
            y = (x32 - mu) * jax.lax.rsqrt(var + EPS)
            if gamma is not None:
                y = y * gamma + beta
            return y.astype(x.dtype)

        def mha(q, k, v):
            B, Nq, C = q.shape
            d = C // H
            qh = q.reshape(B, Nq, H, d)
            kh = k.reshape(B, k.shape[1], H, d)
            vh = v.reshape(B, v.shape[1], H, d)
            scores = jnp.einsum('bqhd,bkhd->bhqk', qh, kh) / jnp.sqrt(jnp.asarray(d, q.dtype))
            attn = jax.nn.softmax(scores, axis=-1)
            out = jnp.einsum('bhqk,bkhd->bqhd', attn, vh)
            return out.reshape(B, Nq, C)
        C = x.shape[-1]
        m = jax.nn.silu(mod) @ ada_w + ada_b
        shift_msa, scale_msa, gate_msa, shift_mlp, scale_mlp, gate_mlp = [c[:, None, :] for c in jnp.split(m, 6, axis=-1)]
        h = layer_norm(x)
        h = h * (1.0 + scale_msa) + shift_msa
        qkv = h @ qkv_w + qkv_b
        q, k, v = jnp.split(qkv, 3, axis=-1)
        h = mha(q, k, v) @ self_o_w + self_o_b
        x = x + h * gate_msa
        h = layer_norm(x, norm2_g, norm2_b)
        q = h @ q_w + q_b
        kv = context @ kv_w + kv_b
        k, v = jnp.split(kv, 2, axis=-1)
        h = mha(q, k, v) @ cross_o_w + cross_o_b
        x = x + h
        h = layer_norm(x)
        h = h * (1.0 + scale_mlp) + shift_mlp
        h = jax.nn.gelu(h @ mlp_w1 + mlp_b1) @ mlp_w2 + mlp_b2
        x = x + h * gate_mlp
        return x
    x = _L0_xcond_ref(x, ctx_1024, cond_1024, L0_xcond_Wq, L0_xcond_bq, L0_xcond_Wkv, L0_xcond_bkv, L0_xcond_Wp, L0_xcond_bp, L0_xcond_Wss_q, L0_xcond_bss_q, L0_xcond_Wss_kv, L0_xcond_bss_kv)
    x = _L1_xcond_ref(x, cond_1024, ctx_1024, L1_xcond_ada_w, L1_xcond_ada_b, L1_xcond_qkv_w, L1_xcond_qkv_b, L1_xcond_self_o_w, L1_xcond_self_o_b, L1_xcond_norm2_g, L1_xcond_norm2_b, L1_xcond_q_w, L1_xcond_q_b, L1_xcond_kv_w, L1_xcond_kv_b, L1_xcond_cross_o_w, L1_xcond_cross_o_b, L1_xcond_mlp_w1, L1_xcond_mlp_b1, L1_xcond_mlp_w2, L1_xcond_mlp_b2)
    return x

_drawn_inputs = setup_inputs


def setup_inputs(seed=0):
    import zlib

    import numpy as np

    out = dict(_drawn_inputs(seed))
    spreads = {'L0_xcond_bq': (0.0, 2.0),
     'L0_xcond_bkv': (0.0, 0.1),
     'L0_xcond_bp': (0.0, 0.1),
     'L0_xcond_bss_q': (0.0, 0.8),
     'L0_xcond_bss_kv': (0.0, 0.343),
     'L1_xcond_ada_b': (0.0, 0.1),
     'L1_xcond_qkv_b': (0.0, 0.606),
     'L1_xcond_self_o_b': (0.0, 0.28),
     'L1_xcond_norm2_g': (1.0, 0.6),
     'L1_xcond_norm2_b': (0.0, 0.8),
     'L1_xcond_q_b': (0.0, 2.0),
     'L1_xcond_kv_b': (0.0, 0.1),
     'L1_xcond_cross_o_b': (0.0, 0.1),
     'L1_xcond_mlp_b1': (0.0, 0.545),
     'L1_xcond_mlp_b2': (0.0, 0.276)}
    factors = {'L0_xcond_Wq': 6.137, 'L0_xcond_Wss_q': 8.0, 'L1_xcond_qkv_w': 2.687, 'L1_xcond_q_w': 6.68}
    for name, (base, spread) in spreads.items():
        noise = np.random.default_rng([zlib.crc32(name.encode()), seed]).standard_normal(out[name].shape)
        drawn = base * np.exp(spread * noise) if base else spread * noise
        out[name] = jnp.asarray(drawn.astype(out[name].dtype))
    for name, factor in factors.items():
        out[name] = (out[name] * factor).astype(out[name].dtype)
    return out
```

```python
from contextlib import ExitStack

import numpy as np

import concourse.bass as bass
from concourse import mybir

F32 = mybir.dt.float32
F32R = mybir.dt.float32r
ALU = mybir.AluOpType
ACT = mybir.ActivationFunctionType
AX = mybir.AxisListType

P = 128
B, T, C = 2, 2048, 512
S = 77
HEADS, DH = 16, 32
HID = 4 * C
KT = C // P
HT = HID // P
W = 512
CHUNKS = T // W
TT = W // P
GH = P // DH
GROUPS = HEADS // GH
SCALE = DH ** -0.5
PARTS = [(0, 0), (0, 1), (1, 0)]
DMA = 16
MODS = (2 + 2 + 6 + 1) * KT


def channels(ap):
    return ap.rearrange("(t p) n -> p t n", p=P)


def column(ap):
    return ap.rearrange("(t p) -> p t", p=P)


def chunk_after(i, b):
    return (i, 1) if b == 0 else (i + 1, 0)


def conditioning(nc, d, mod, gates, kv):
    NS, NA = 2 * C // P, 6 * C // P
    with nc.cleanup_on_exit(), ExitStack() as ctx:
        sb = lambda n, s, t=F32: ctx.enter_context(nc.sbuf_tensor("cn_" + n, s, t))
        sem = lambda n: nc.alloc_semaphore("cn_" + n)
        ps = ctx.enter_context(nc.psum_tensor("cn_ps", [P, 8, W], F32))
        ident = sb("ident", [P, P])
        cond = sb("cond", [P, KT, B])
        act_c = sb("act_c", [P, KT, B])
        act_row = sb("act_row", [P, KT, B, P])
        ctx_tok = sb("ctx_tok", [S, B, C])
        ctx_n = sb("ctx_n", [S, B, C])
        wss = sb("wss", [P, 2, KT, 2 * C])
        ada = sb("ada", [P, KT, 6 * C])
        wkv = sb("wkv", [P, 2, KT, 2 * C])
        bias = sb("bias", [P, 2 * NS + NA])
        kbias = sb("kbias", [P, 2, KT])
        vbias = sb("vbias", [S, 2, C])
        gbias = sb("gbias", [P, 2, C])
        gate_row = sb("gate_row", [P, 2, B, C])
        stats = sb("stats", [S, B, 6])
        mv = sb("mv", [S, B, 2])
        rstd = sb("rstd", [S, B])
        epst = sb("epst", [S, 1])
        ctxT = sb("ctxT", [P, 2, B, KT, S])
        kf = sb("kf", [P, 2, B, KT, S])
        khi = sb("khi", [P, 2, B, KT, S], F32R)
        klo = sb("klo", [P, 2, B, KT, S], F32R)
        vf = sb("vf", [S, 2, B, C])
        small_in, wss_in, ada_in, wkv_in = sem("small_in"), sem("wss_in"), sem("ada_in"), sem("wkv_in")
        silu_done, row_done, mods_done, mod_out = sem("silu_done"), sem("row_done"), sem("mods_done"), sem("mod_out")
        var_done, sqrt_done, norm_done = sem("var_done"), sem("sqrt_done"), sem("norm_done")
        turned, ctx_out, eps_set = sem("turned"), sem("ctx_out"), sem("eps_set")
        k_done, v_done, k_out, split, v_out, g_done, g_out, stored = (sem(n) for n in (
            "k_done", "v_done", "k_out", "split", "v_out", "g_done", "g_out", "stored"))
        dve_step = sem("dve_step")
        block = ctx.enter_context(nc.Block())
        SMALL = 15

        @block.sync
        def _(sp):
            with nc.allow_non_contiguous_dma(reason="short vectors, once"):
                for b in range(B):
                    sp.dma_start(cond[:, :, b], column(d["cond_1024"][b])).then_inc(small_in, DMA)
                sp.dma_start(ident[:], d["ident"]).then_inc(small_in, DMA)
                sp.dma_start(ctx_tok[:], d["ctx_1024"].rearrange("b s c -> s b c")).then_inc(small_in, DMA)
                for o, n, name in ((0, NS, "L0_xcond_bss_q"), (NS, NS, "L0_xcond_bss_kv"), (2 * NS, NA, "L1_xcond_ada_b")):
                    sp.dma_start(bias[:, o:o + n], column(d[name])).then_inc(small_in, DMA)
                for a, name in enumerate(("L0_xcond_bkv", "L1_xcond_kv_b")):
                    sp.dma_start(kbias[:, a], column(d[name][0:C])).then_inc(small_in, DMA)
                    sp.dma_start(vbias[:, a], d[name][C:2 * C].partition_broadcast(S)).then_inc(small_in, DMA)
                for g in range(2):
                    sp.dma_start(gbias[:, g], d["L1_xcond_ada_b"][(3 * g + 2) * C:(3 * g + 3) * C].partition_broadcast(P)).then_inc(small_in, DMA)
                sp.dma_start(mod[:, 2 * NS + NA:2 * NS + NA + KT, 0], column(d["L1_xcond_norm2_g"])).then_inc(small_in, DMA)
                sp.dma_start(mod[:, 2 * NS + NA:2 * NS + NA + KT, 1], column(d["L1_xcond_norm2_b"])).then_inc(small_in, DMA)
            for a, name in enumerate(("L0_xcond_Wss_q", "L0_xcond_Wss_kv")):
                sp.dma_start(wss[:, a], channels(d[name])).then_inc(wss_in, DMA)
            for a, name in enumerate(("L0_xcond_Wkv", "L1_xcond_kv_w")):
                sp.dma_start(wkv[:, a], channels(d[name])).then_inc(wkv_in, DMA)
            sp.dma_start(ada[:], channels(d["L1_xcond_ada_w"])).then_inc(ada_in, DMA)
            sp.wait_ge(split, 2)
            sp.wait_ge(v_out, 2 * B)
            for a in range(2):
                for b in range(B):
                    for part, t in ((0, khi), (1, klo)):
                        sp.dma_start(kv[a][0][part, b].rearrange("(t p) s -> p t s", p=P), t[:, a, b].bitcast(F32)).then_inc(stored, DMA)
                    sp.dma_start(kv[a][1][b], vf[:, a, b]).then_inc(stored, DMA)
            sp.wait_ge(g_out, 2 * B)
            sp.dma_start(gates.rearrange("g b c -> (g b c)").rearrange("(o n) -> o n", o=1),
                         gate_row[0:1].rearrange("p g b c -> p (g b c)")).then_inc(stored, DMA)
            sp.wait_ge(stored, DMA * (2 * B * 3 + 1))

        @block.tensor
        def _(pe):
            pe.wait_ge(small_in, DMA * SMALL)
            for b in range(B):
                for t in range(KT):
                    mm = pe.transpose(ps[:, 5 + b, t * S:(t + 1) * S], ctx_tok[:, b, t * P:(t + 1) * P], ident[0:S, 0:S])
            mm.then_inc(turned, 1)
            pe.wait_ge(norm_done, 2)
            for b in range(B):
                for t in range(KT):
                    mm = pe.transpose(ps[:, 3 + b, t * S:(t + 1) * S], ctx_n[:, b, t * P:(t + 1) * P], ident[0:S, 0:S])
            mm.then_inc(turned, 1)
            pe.wait_ge(wss_in, DMA * 2)
            pe.wait_ge(silu_done, 1)
            for j in range(2 * NS):
                for t in range(KT):
                    mm = pe.matmul(ps[:, 0, j * B:(j + 1) * B], wss[:, j // NS, t, (j % NS) * P:(j % NS + 1) * P],
                                   act_c[:, t], start=(t == 0), stop=(t == KT - 1))
            mm.then_inc(mods_done, 1)
            pe.wait_ge(wkv_in, DMA * 2)
            for n, a in enumerate((1, 0)):
                pe.wait_ge(ctx_out, 1 if a == 1 else 1 + B)
                for b in range(B):
                    if n:
                        pe.wait_ge(k_out, b + 1)
                    for m in range(KT):
                        for t in range(KT):
                            mm = pe.matmul(ps[:, 1 + b, m * S:(m + 1) * S], wkv[:, a, t, m * P:(m + 1) * P],
                                           ctxT[:, a, b, t], start=(t == 0), stop=(t == KT - 1))
                    mm.then_inc(k_done, 1)
                    if n:
                        pe.wait_ge(v_out, b + 1)
                    for t in range(KT):
                        mm = pe.matmul(ps[0:S, 6 + b, :], ctxT[:, a, b, t], wkv[:, a, t, C:2 * C],
                                       start=(t == 0), stop=(t == KT - 1))
                    mm.then_inc(v_done, 1)
            pe.wait_ge(ada_in, DMA)
            pe.wait_ge(mod_out, 1)
            for j in range(NA):
                for t in range(KT):
                    mm = pe.matmul(ps[:, 0, j * B:(j + 1) * B], ada[:, t, j * P:(j + 1) * P],
                                   act_c[:, t], start=(t == 0), stop=(t == KT - 1))
            mm.then_inc(mods_done, 1)
            pe.wait_ge(row_done, 1)
            for g in range(2):
                for b in range(B):
                    n = g * B + b
                    if n == 3:
                        pe.wait_ge(mod_out, 2)
                    for t in range(KT):
                        mm = pe.matmul(ps[:, (3, 4, 5, 0)[n], :], act_row[:, t, b], ada[:, t, (3 * g + 2) * C:(3 * g + 3) * C],
                                       start=(t == 0), stop=(t == KT - 1))
                    mm.then_inc(g_done, 1)

        @block.scalar
        def _(act):
            act.wait_ge(small_in, DMA * SMALL)
            act.activation(act_c[:], cond[:], ACT.Silu).then_inc(silu_done, 1)
            act.wait_ge(var_done, 1)
            act.wait_ge(eps_set, 1)
            act.activation(rstd[:], mv[:, :, 1], ACT.Sqrt, bias=epst[:, 0:1]).then_inc(sqrt_done, 1)
            for n, a in enumerate((1, 0)):
                for b in range(B):
                    act.wait_ge(k_done, n * B + b + 1)
                    for m in range(KT):
                        ins = act.activation(kf[:, a, b, m], ps[:, 1 + b, m * S:(m + 1) * S], ACT.Identity,
                                             bias=kbias[:, a, m:m + 1])
                    ins.then_inc(k_out, 1)

        @block.vector
        def _(dve):
            dve.memset(epst[:], 1e-5).then_inc(eps_set, 1)
            dve.wait_ge(small_in, DMA * SMALL)
            steps = 0
            for b in range(B):
                ins = dve.bn_stats(stats[:, b], ctx_tok[:, b])
            ins.then_inc(dve_step, 1)
            dve.wait_ge(dve_step, 1)
            for b in range(B):
                ins = dve.bn_aggr(mv[:, b], stats[:, b])
            ins.then_inc(var_done, 1)
            dve.wait_ge(turned, 1)
            dve.tensor_copy(ctxT[:, 1], ps[:, 5:7, 0:KT * S].rearrange("p b (t s) -> p b t s", t=KT)).then_inc(ctx_out, 1)
            dve.wait_ge(sqrt_done, 1)
            dve.reciprocal(rstd[:], rstd[:]).then_inc(dve_step, 1)
            dve.wait_ge(dve_step, 2)
            for b in range(B):
                dve.tensor_scalar(ctx_n[:, b], ctx_tok[:, b], mv[:, b, 0:1], rstd[:, b:b + 1],
                                  ALU.subtract, ALU.mult).then_inc(norm_done, 1)
            dve.wait_ge(silu_done, 1)
            for t in range(KT):
                for b in range(B):
                    ins = dve.tensor_copy(act_row[:, t, b], act_c[:, t, b:b + 1].to_broadcast([P, P]))
            ins.then_inc(row_done, 1)
            dve.wait_ge(mods_done, 1)
            dve.tensor_tensor(mod[:, 0:2 * NS], ps[:, 0, 0:2 * NS * B].rearrange("p (j b) -> p j b", b=B),
                              bias[:, 0:2 * NS].unsqueeze(2).to_broadcast([P, 2 * NS, B]), ALU.add).then_inc(mod_out, 1)
            dve.wait_ge(mod_out, 1)
            for o in (0, NS):
                ins = dve.tensor_scalar(mod[:, o:o + KT], mod[:, o:o + KT], 1.0, None, ALU.add)
            ins.then_inc(dve_step, 1)
            dve.wait_ge(dve_step, 3)
            dve.wait_ge(turned, 2)
            for b in range(B):
                for t in range(KT):
                    ins = dve.tensor_scalar(ctxT[:, 0, b, t], ps[:, 3 + b, t * S:(t + 1) * S],
                                            mod[:, NS + t, b:b + 1], mod[:, NS + KT + t, b:b + 1], ALU.mult, ALU.add)
                ins.then_inc(ctx_out, 1)
            for n, a in enumerate((1, 0)):
                for b in range(B):
                    dve.wait_ge(v_done, n * B + b + 1)
                    dve.tensor_tensor(vf[:, a, b], ps[0:S, 6 + b, :], vbias[:, a], ALU.add).then_inc(v_out, 1)
            dve.wait_ge(k_out, 2 * B)
            dve.tensor_copy(khi[:], kf[:]).then_inc(split, 1)
            dve.wait_ge(split, 1)
            dve.tensor_tensor(klo[:].rearrange("p a b t s -> p (a b t s)"), kf[:].rearrange("p a b t s -> p (a b t s)"),
                              khi[:].bitcast(F32).rearrange("p a b t s -> p (a b t s)"), ALU.subtract).then_inc(split, 1)
            dve.wait_ge(mods_done, 2)
            dve.tensor_tensor(mod[:, 2 * NS:2 * NS + NA], ps[:, 0, 0:NA * B].rearrange("p (j b) -> p j b", b=B),
                              bias[:, 2 * NS:2 * NS + NA].unsqueeze(2).to_broadcast([P, NA, B]), ALU.add).then_inc(mod_out, 1)
            dve.wait_ge(mod_out, 2)
            for o in (KT, 4 * KT):
                dve.tensor_scalar(mod[:, 2 * NS + o:2 * NS + o + KT], mod[:, 2 * NS + o:2 * NS + o + KT], 1.0, None, ALU.add)
            for g in range(2):
                for b in range(B):
                    n = g * B + b
                    dve.wait_ge(g_done, n + 1)
                    dve.tensor_tensor(gate_row[:, g, b], ps[:, (3, 4, 5, 0)[n], :], gbias[:, g], ALU.add).then_inc(g_out, 1)


def chunk_pass(nc, d, name, x_in, x_out, o_in, w_out, b_out, gate, eps, scale, shift, projections, values, plain=None):
    NM = sum(KT for _ in projections)
    TILES = NM + (TT if values else 0)
    RING = 4
    XC = 2 if gate is None else 0
    with nc.cleanup_on_exit(), ExitStack() as ctx:
        sb = lambda n, s, t=F32: ctx.enter_context(nc.sbuf_tensor(f"{name}_{n}", s, t))
        sem = lambda n: nc.alloc_semaphore(f"{name}_{n}")
        po = ctx.enter_context(nc.psum_tensor(name + "_po", [P, 2, W], F32))
        pt = ctx.enter_context(nc.psum_tensor(name + "_pt", [P, 2, W], F32))
        pp = ctx.enter_context(nc.psum_tensor(name + "_pp", [P, RING, W], F32))
        ident = sb("ident", [P, P])
        weights = ([w_out] if o_in is not None else []) + [w for w, _, _ in projections] + ([values[0]] if values else [])
        NWT = len(weights)
        wparts = sb("w", [P, max(NWT, 1), 2, KT, C], F32R)
        stage = sb("stage", [P, 2, KT, C])
        x = sb("x", [P, 2, TT, C])
        xn = sb("xn", [P, TT, C])
        u = sb("u", [P, KT, W])
        us = sb("us", [P, 2, 2, KT, W], F32R)
        stats = sb("stats", [P, TT, 6])
        mv = sb("mv", [P, TT, 2])
        rstd = sb("rstd", [P, TT])
        epst = sb("epst", [P, 1])
        if o_in is not None:
            o = sb("o", [P, KT, W])
            os_ = sb("os", [P, 2, KT, W], F32R)
            orow = sb("orow", [P, C])
            brow = sb("brow", [P, B, C])
        if gate is not None:
            grow = sb("grow", [P, B, C])
            gated = sb("gated", [P, 2, C])
        if projections:
            out = sb("out", [P, RING, 2, W], F32R)
            pbias = sb("pbias", [P, NM])
        if values:
            vout = sb("vout", [P, 2, C])
            vrow = sb("vrow", [P, C])
        small_in, stage_in = sem("small_in"), [sem("stage_in0"), sem("stage_in1")]
        w_hi, w_lo, rows_ready, rows_done = sem("w_hi"), sem("w_lo"), sem("rows_ready"), sem("rows_done")
        x_in_s, o_loaded = [sem("x_in0"), sem("x_in1")], sem("o_in")
        x_stored = [sem("x_stored0"), sem("x_stored1")]
        biased, o_hi, o_lo, oproj_done = sem("biased"), sem("o_hi"), sem("o_lo"), sem("oproj_done")
        gated_done, x_ready = sem("gated_done"), sem("x_ready")
        stats_done, var_done, std_done, rstd_done, xn_done = (sem(n) for n in (
            "stats_done", "var_done", "std_done", "rstd_done", "xn_done"))
        turned, u_done, u_hi, u_lo = sem("turned"), sem("u_done"), sem("u_hi"), sem("u_lo")
        proj_done, proj_hi, proj_out = sem("proj_done"), sem("proj_hi"), sem("proj_out")
        out_stored = [sem(f"out_stored{r}") for r in range(RING)]
        v_stored = [sem("v_stored0"), sem("v_stored1")]
        passed, aggregating = sem("passed"), sem("aggregating")
        u_stored = [sem("u_stored0"), sem("u_stored1")]
        block = ctx.enter_context(nc.Block())
        small = [(ident[:], d["ident"])]
        if o_in is not None:
            small.append((orow[:], b_out.partition_broadcast(P)))
        if gate is not None:
            small += [(grow[:, b], gate[b].partition_broadcast(P)) for b in range(B)]
        if values:
            small.append((vrow[:], values[1].partition_broadcast(P)))
        m = 0
        for _, bias, _ in projections:
            small.append((pbias[:, m:m + KT], column(bias)))
            m += KT
        N = CHUNKS * B

        @block.sync
        def _(sp):
            with nc.allow_non_contiguous_dma(reason="short vectors, once"):
                for dst, src in small:
                    sp.dma_start(dst, src).then_inc(small_in, DMA)

            def load_weight(k):
                if k >= 2:
                    sp.wait_ge(w_lo, k - 1)
                sp.dma_start(stage[:, k % 2], channels(weights[k])).then_inc(stage_in[k % 2], DMA)

            def load_x(i, b, first=False):
                if not first:
                    sp.wait_ge(xn_done, (2 * (i - 1) + b + 1) * TT)
                    if x_out is not None:
                        sp.sem_inc(passed, 1)
                        sp.wait_ge(x_stored[b], DMA * i)
                    sp.sem_inc(passed, 1)
                sp.dma_start(x[:, b], x_in[b, bass.ds(i * W, W), :].rearrange("(t p) c -> p t c", p=P)).then_inc(x_in_s[b], DMA)

            def load_o(i, b):
                sp.wait_ge(o_lo, 2 * i + b + 1)
                sp.sem_inc(passed, 1)
                sp.dma_start(o[:], o_in[b, :, bass.ds(i * W, W)].rearrange("(t p) w -> p t w", p=P)).then_inc(o_loaded, DMA)

            def store_x(i, b):
                sp.wait_ge(x_ready, (2 * i + b + 1) * TT + XC)
                sp.sem_inc(passed, 1)
                sp.dma_start(x_out[b, bass.ds(i * W, W), :].rearrange("(t p) c -> p t c", p=P), x[:, b]).then_inc(x_stored[b], DMA)

            def store_outputs(i, b):
                for t in range(TILES):
                    sp.wait_ge(proj_out, (2 * i + b) * TILES + t + 1 + RING)
                    sp.sem_inc(passed, 1)
                    if t < NM:
                        dst = projections[t // KT][2]
                        sp.dma_start(dst[:, b, t % KT * P:(t % KT + 1) * P, bass.ds(i * W, W)].rearrange("s p w -> p s w"),
                                     out[:, t % RING].bitcast(F32)).then_inc(out_stored[t % RING], DMA)
                    else:
                        sp.dma_start(values[2][b, bass.ds(i * W + (t - NM) * P, P)], vout[:, t % 2]).then_inc(v_stored[t % 2], DMA)
                if plain is not None:
                    sp.wait_ge(u_lo, 2 * i + b + 2)
                    sp.sem_inc(passed, 1)
                    sp.dma_start(plain[0, b, :, bass.ds(i * W, W)].rearrange("(t p) w -> p t w", p=P), us[:, b, 0].bitcast(F32)).then_inc(u_stored[b], DMA)
                    sp.dma_start(plain[1, b, :, bass.ds(i * W, W)].rearrange("(t p) w -> p t w", p=P), us[:, b, 1].bitcast(F32)).then_inc(u_stored[b], DMA)

            def superstep(i, b, left):
                if left > 2:
                    if o_in is not None:
                        load_o(i + 1, b)
                    if x_out is None:
                        load_x(i + 1, b)
                if left > 1 and x_out is not None:
                    store_x(*chunk_after(i, b))
                store_outputs(i, b)
                if left > 2 and x_out is not None:
                    load_x(i + 1, b)

            for s in (out_stored if projections else []) + (v_stored if values else []):
                sp.sem_inc(s, DMA)
            for s in u_stored if plain is not None else []:
                sp.sem_inc(s, 2 * DMA)
            load_x(0, 0, True)
            if o_in is not None:
                load_o(0, 0)
            load_weight(0) if NWT else None
            load_x(0, 1, True)
            for k in range(1, NWT):
                load_weight(k)
            if o_in is not None:
                load_o(0, 1)
                store_x(0, 0)
            with sp.Fori(0, CHUNKS - 1) as i:
                for b in range(B):
                    superstep(i, b, 3)
            for b in range(B):
                superstep(CHUNKS - 1, b, B - b)
            for b in range(2):
                if x_out is not None:
                    sp.wait_ge(x_stored[b], DMA * CHUNKS)
                if values:
                    sp.wait_ge(v_stored[b], DMA * (N * TT // 2 + 1))
                if plain is not None:
                    sp.wait_ge(u_stored[b], 2 * DMA * (CHUNKS + 1))
            if projections:
                for r in range(RING):
                    sp.wait_ge(out_stored[r], DMA * (N * NM // RING + 1))

        @block.tensor
        def _(pe):
            def split_matmul(out_ap, lhs, rhs):
                for t in range(KT):
                    for q, (pm, pw) in enumerate(PARTS):
                        mm = pe.matmul(out_ap, lhs(pw, t), rhs(pm, t), start=(t == 0 and q == 0),
                                       stop=(t == KT - 1 and q == 2))
                return mm

            def output_projection(i, b):
                n = 2 * i + b
                pe.wait_ge(o_lo, n + 2)
                for tt in range(TT):
                    pe.wait_ge(x_ready, n * TT + tt + 1) if gate is None else pe.wait_ge(gated_done, n * TT + tt + 1)
                    split_matmul(po[:, tt % 2], lambda s, t: os_[:, s, t, tt * P:(tt + 1) * P],
                                 lambda s, t: wparts[:, 0, s, t]).then_inc(oproj_done, 1)

            def turn(i, b):
                n = 2 * i + b
                for t in range(KT):
                    pe.wait_ge(u_done, n * KT + t + 1)
                    for tt in range(TT):
                        if t == 0:
                            pe.wait_ge(xn_done, n * TT + tt + 1)
                        mm = pe.transpose(pt[:, t % 2, tt * P:(tt + 1) * P], xn[:, tt, t * P:(t + 1) * P], ident[:])
                    mm.then_inc(turned, 1)

            def project(i, b):
                n = 2 * i + b
                pe.wait_ge(u_lo, n + 2)
                for t in range(TILES):
                    pe.wait_ge(proj_out, n * TILES + t + 1)
                    w = NWT - len(projections) - (1 if values else 0) + t // KT
                    if t < NM:
                        mm = split_matmul(pp[:, t % RING], lambda s, k: wparts[:, w, s, k, t % KT * P:(t % KT + 1) * P],
                                          lambda s, k: us[:, b, s, k])
                    else:
                        mm = split_matmul(pp[:, t % RING], lambda s, k: us[:, b, s, k, (t - NM) * P:(t - NM + 1) * P],
                                          lambda s, k: wparts[:, w, s, k])
                    mm.then_inc(proj_done, 1)

            def superstep(i, b, left):
                if left > 1 and o_in is not None:
                    output_projection(*chunk_after(i, b))
                if TILES:
                    project(i, b)
                if left > 1:
                    turn(*chunk_after(i, b))

            pe.wait_ge(small_in, DMA * len(small))
            if NWT:
                pe.wait_ge(w_lo, NWT if o_in is None else 1)
            if o_in is not None:
                output_projection(0, 0)
            turn(0, 0)
            if NWT:
                pe.wait_ge(w_lo, NWT)
            with pe.Fori(0, CHUNKS - 1) as i:
                for b in range(B):
                    superstep(i, b, 3)
            for b in range(B):
                superstep(CHUNKS - 1, b, B - b)

        @block.scalar
        def _(act):
            def split_o(i, b):
                n = 2 * i + b
                act.wait_ge(o_loaded, DMA * (n + 1))
                if gate is None:
                    act.wait_ge(x_ready, n * TT + 2)
                else:
                    act.wait_ge(gated_done, n * TT + 2)
                act.activation(os_[:, 0], o[:], ACT.Copy).then_inc(o_hi, 1)

            def std(i, b):
                act.wait_ge(var_done, 2 * i + b + 1)
                act.activation(rstd[:], mv[:, :, 1], ACT.Sqrt, bias=epst[:, 0:1]).then_inc(std_done, 1)

            def modulate(i, b):
                n = 2 * i + b
                for t in range(KT):
                    act.wait_ge(turned, n * KT + t + 1)
                    if t == 0:
                        act.wait_ge(u_lo, n + 1)
                    act.activation(u[:, t], pt[:, t % 2], ACT.Identity, bias=shift(b, t), scale=scale(b, t)).then_inc(u_done, 1)

            def evacuate(i, b):
                n = 2 * i + b
                for t in range(NM):
                    act.wait_ge(proj_done, n * TILES + t + 1)
                    act.wait_ge(out_stored[t % RING], DMA * (n * (NM // RING) + t // RING + 1))
                    act.activation(out[:, t % RING, 0], pp[:, t % RING], ACT.Identity, bias=pbias[:, t:t + 1]).then_inc(proj_hi, 1)

            def superstep(i, b, left):
                if left > 1:
                    std(*chunk_after(i, b))
                evacuate(i, b)
                if left > 1:
                    modulate(*chunk_after(i, b))
                if left > 2 and o_in is not None:
                    split_o(i + 1, b)

            act.sem_inc(u_done, 2)
            if o_in is not None:
                split_o(0, 0)
            act.wait_ge(rows_ready, 1)
            for k in range(NWT):
                act.wait_ge(stage_in[k % 2], DMA * (k // 2 + 1))
                act.activation(wparts[:, k, 0], stage[:, k % 2], ACT.Copy).then_inc(w_hi, 1)
            std(0, 0)
            modulate(0, 0)
            if o_in is not None:
                split_o(0, 1)
            with act.Fori(0, CHUNKS - 1) as i:
                for b in range(B):
                    superstep(i, b, 3)
            for b in range(B):
                superstep(CHUNKS - 1, b, B - b)

        @block.vector
        def _(dve):
            def split_o(i, b):
                n = 2 * i + b
                dve.wait_ge(o_hi, n + 1)
                dve.tensor_tensor(os_[:, 1], o[:], os_[:, 0].bitcast(F32), ALU.subtract).then_inc(o_lo, 1)

            def normalise(i, b, first=False):
                n = 2 * i + b
                dve.wait_ge(x_in_s[b], DMA * (i + 1))
                for tt in range(TT):
                    if o_in is not None:
                        dve.wait_ge(oproj_done, n * TT + tt + 1)
                        dve.wait_ge(biased, n + 1)
                        if gate is not None:
                            dve.tensor_tensor(gated[:, tt % 2], po[:, tt % 2], grow[:, b], ALU.mult).then_inc(gated_done, 1)
                            dve.wait_ge(gated_done, n * TT + tt + 3)
                            dve.tensor_tensor(x[:, b, tt], x[:, b, tt], gated[:, tt % 2], ALU.add).then_inc(x_ready, 1)
                            dve.wait_ge(x_ready, n * TT + tt + 1)
                        else:
                            dve.tensor_tensor(x[:, b, tt], po[:, tt % 2], x[:, b, tt], ALU.add).then_inc(x_ready, 1)
                            dve.wait_ge(x_ready, n * TT + tt + 3)
                    dve.bn_stats(stats[:, tt], x[:, b, tt]).then_inc(stats_done, 1)
                dve.wait_ge(stats_done, (n + 1) * TT)
                dve.sem_inc(aggregating, 1)
                for tt in range(TT):
                    ins = dve.bn_aggr(mv[:, tt], stats[:, tt])
                ins.then_inc(var_done, 1)
                dve.wait_ge(std_done, n + 1)
                dve.reciprocal(rstd[:], rstd[:]).then_inc(rstd_done, 1)
                dve.wait_ge(rstd_done, n + 1)
                if not first:
                    dve.wait_ge(turned, n * KT)
                for tt in range(TT):
                    dve.tensor_scalar(xn[:, tt], x[:, b, tt], mv[:, tt, 0:1], rstd[:, tt:tt + 1],
                                      ALU.subtract, ALU.mult).then_inc(xn_done, 1)

            def evacuate(i, b):
                n = 2 * i + b
                for t in range(NM):
                    dve.wait_ge(proj_hi, n * NM + t + 1)
                    dve.scalar_tensor_tensor(out=out[:, t % RING, 1], in0=pp[:, t % RING], scalar=pbias[:, t:t + 1],
                                             in1=out[:, t % RING, 0].bitcast(F32), op0=ALU.add, op1=ALU.subtract).then_inc(proj_out, 1)
                for t in range(NM, TILES):
                    dve.wait_ge(proj_done, n * TILES + t + 1)
                    dve.wait_ge(v_stored[t % 2], DMA * (n * (TT // 2) + (t - NM) // 2 + 1))
                    dve.tensor_tensor(vout[:, t % 2], pp[:, t % RING], vrow[:], ALU.add).then_inc(proj_out, 1)

            def split_u(i, b):
                n = 2 * i + b
                dve.wait_ge(u_done, (n + 1) * KT + 2)
                if plain is not None:
                    dve.wait_ge(u_stored[b], 2 * DMA * (i + 1))
                dve.tensor_copy(us[:, b, 0], u[:]).then_inc(u_hi, 1)
                dve.wait_ge(u_hi, n + 1)
                dve.tensor_tensor(us[:, b, 1], u[:], us[:, b, 0].bitcast(F32), ALU.subtract).then_inc(u_lo, 1)

            def superstep(i, b, left):
                if left > 1:
                    normalise(*chunk_after(i, b))
                evacuate(i, b)
                if left > 1:
                    split_u(*chunk_after(i, b))
                if left > 2 and o_in is not None:
                    split_o(i + 1, b)

            dve.memset(epst[:], eps).then_inc(rows_ready, 1)
            dve.sem_inc(proj_out, RING)
            dve.sem_inc(u_lo, 1)
            if o_in is not None:
                dve.sem_inc(o_lo, 1)
                dve.sem_inc(gated_done if gate is not None else x_ready, 2)
                split_o(0, 0)
            for k in range(NWT):
                dve.wait_ge(w_hi, k + 1)
                dve.tensor_tensor(wparts[:, k, 1], stage[:, k % 2], wparts[:, k, 0].bitcast(F32), ALU.subtract).then_inc(w_lo, 1)
            normalise(0, 0, True)
            split_u(0, 0)
            if o_in is not None:
                split_o(0, 1)
            with dve.Fori(0, CHUNKS - 1) as i:
                for b in range(B):
                    superstep(i, b, 3)
            for b in range(B):
                superstep(CHUNKS - 1, b, B - b)

        if o_in is not None:
            @block.gpsimd
            def _(pool):
                pool.wait_ge(small_in, DMA * len(small))
                if gate is not None:
                    for b in range(B):
                        ins = pool.tensor_tensor(brow[:, b], orow[:], grow[:, b], ALU.mult)
                    ins.then_inc(rows_done, 1)
                    pool.wait_ge(rows_done, 1)

                def add_bias(i, b):
                    row = orow[:] if gate is None else brow[:, b]
                    pool.wait_ge(x_in_s[b], DMA * (i + 1))
                    pool.tensor_tensor(x[:, b], x[:, b], row.unsqueeze(1).to_broadcast([P, TT, C]), ALU.add).then_inc(biased, 1)

                with pool.Fori(0, CHUNKS) as i:
                    for b in range(B):
                        add_bias(i, b)


def attention(nc, d, name, q_in, k_in, v_in, o_out, keys):
    NKT = -(-keys // P)
    KR = keys // NKT
    KC = -(-keys // W)
    KW = keys // KC
    KE = KW + KW % 2
    AHEAD = 1 if NKT > 1 else 2
    if KC > 1:
        UNITS = [(h, [qt], kc) for h in range(GH) for qt in range(TT) for kc in range(KC)]
    else:
        UNITS = [(h, list(range(TT)), 0) for h in range(GH)]
    U = len(UNITS) + 1
    PER = -(-len(UNITS) // max(NKT - 3, 1))
    QR = 4
    STEPS = B * GROUPS * CHUNKS
    BODY = 2 * CHUNKS
    SETUP = 4 + KW % 2
    with nc.cleanup_on_exit(), ExitStack() as ctx:
        sb = lambda n, s, t=F32: ctx.enter_context(nc.sbuf_tensor(f"{name}_{n}", s, t))
        sem = lambda n: nc.alloc_semaphore(f"{name}_{n}")
        sm = ctx.enter_context(nc.psum_tensor(name + "_sm", [P, 2, W], F32))
        st = ctx.enter_context(nc.psum_tensor(name + "_st", [P, 2, 2, W], F32))
        acc = ctx.enter_context(nc.psum_tensor(name + "_acc", [P, W], F32))
        den = ctx.enter_context(nc.psum_tensor(name + "_den", [P, W], F32))
        ident = sb("ident", [P, P])
        mask = sb("mask", [P, GH * TT])
        ones = sb("ones", [P, DH])
        q = sb("q", [P, QR, GH, W], F32R)
        k = sb("k", [P, 2, GH, KC * KE], F32R)
        v = sb("v", [P, 2, NKT, P])
        e = sb("e", [P, 2, GH, W])
        peak = sb("peak", [P, len(UNITS)])
        top = sb("top", [P, GH * TT])
        neg_hi = sb("neg_hi", [P, GH * TT], F32R)
        neg = sb("neg", [P, P])
        den_t = sb("den_t", [P, W])
        inv = sb("inv", [P, W // DH])
        inv_b = sb("inv_b", [P, W])
        inv_t = sb("inv_t", [P, W])
        o = sb("o", [P, 2, W])
        small_in, set_up = sem("small_in"), sem("set_up")
        q_loaded = [sem(f"q_loaded{r}") for r in range(QR)]
        k_loaded, v_loaded = [sem("k_loaded0"), sem("k_loaded1")], [sem("v_loaded0"), sem("v_loaded1")]
        unit_done, unit_read = sem("unit_done"), sem("unit_read")
        top_done, neg_done, neg_ready = sem("top_done"), sem("neg_done"), sem("neg_ready")
        st_done, exp_done, tile_used = sem("st_done"), sem("exp_done"), sem("tile_used")
        inv_step, acc_read = sem("inv_step"), sem("acc_read")
        o_stored = [sem("o_stored0"), sem("o_stored1")]
        passed = sem("passed")
        block = ctx.enter_context(nc.Block())

        @block.sync
        def _(sp):
            for dst, src in ((ident[:], d["ident"]), (mask[:], d["mask"])):
                sp.dma_start(dst, src).then_inc(small_in, DMA)
            for s in o_stored:
                sp.sem_inc(s, DMA)

            def load_q(i, j, first=False):
                if not first:
                    sp.wait_ge(tile_used, (BODY * i + j - QR + 1) * NKT + 2)
                    sp.sem_inc(passed, 1)
                for row, part in enumerate((0, 0, 1)):
                    src = q_in[part].rearrange("b (g h r) t -> (b g) r h t", g=GROUPS, h=GH)
                    sp.dma_start(q[row * DH:(row + 1) * DH, j % QR].bitcast(F32),
                                 src[2 * i + j // CHUNKS, :, :, j % CHUNKS * W:(j % CHUNKS + 1) * W]
                                 ).then_inc(q_loaded[j % QR], DMA)

            def load_kv(i, g, first=False):
                if not first:
                    sp.wait_ge(tile_used, (BODY * i + (g - 1) * CHUNKS) * NKT + 2)
                    sp.sem_inc(passed, 1)
                for row, part in enumerate((0, 1, 0)):
                    src = k_in[part].rearrange("b (g h r) t -> (b g) r h t", g=GROUPS, h=GH)
                    sp.dma_start(k[row * DH:(row + 1) * DH, g % 2, :, 0:keys].bitcast(F32),
                                 src[2 * i + g]).then_inc(k_loaded[g % 2], DMA)
                sp.dma_start(v[0:KR, g % 2], v_in[(i + g // 2) // 2, :, bass.ds(((i + g // 2) % 2 * 2 + g % 2) * P, P)].rearrange("(t p) c -> p t c", p=KR)
                             ).then_inc(v_loaded[g % 2], DMA)

            def store_o(i, j):
                sp.wait_ge(acc_read, BODY * i + j + 2)
                sp.sem_inc(passed, 1)
                dst = o_out.rearrange("b (g p) t -> (b g) p t", p=P)
                sp.dma_start(dst[2 * i + j // CHUNKS, :, j % CHUNKS * W:(j % CHUNKS + 1) * W],
                             o[:, j % 2]).then_inc(o_stored[j % 2], DMA)

            def step(i, j, bodies_left):
                if j + QR - 1 < BODY * bodies_left:
                    load_q(i, j + QR - 1)
                if j % CHUNKS == 0 and j // CHUNKS + 1 < 2 * bodies_left:
                    load_kv(i, j // CHUNKS + 1)
                store_o(i, j)

            load_q(0, 0, True)
            load_kv(0, 0, True)
            for j in range(1, QR - 1):
                load_q(0, j, True)
            with sp.Fori(0, STEPS // BODY - 1) as i:
                for j in range(BODY):
                    step(i, j, 2)
            for j in range(BODY):
                step(STEPS // BODY - 1, j, 1)
            for s in o_stored:
                sp.wait_ge(s, DMA * (STEPS // 2 + 1))

        @block.tensor
        def _(pe):
            def score_unit(i, j, u):
                n, g = BODY * i + j, j // CHUNKS
                h, tiles, kc = UNITS[u]
                if u == 0:
                    pe.wait_ge(q_loaded[j % QR], 3 * DMA * (BODY // QR * i + j // QR + 1))
                    if j % CHUNKS == 0:
                        pe.wait_ge(k_loaded[g % 2], 3 * DMA * (i + g // 2 + 1))
                pe.wait_ge(unit_read, n * U + u + 1)
                for x, qt in enumerate(tiles):
                    mm = pe.matmul(sm[:, (j * U + u) % 2, x * KE:(x + 1) * KE], q[0:3 * DH, j % QR, h, qt * P:(qt + 1) * P],
                                   k[0:3 * DH, g % 2, h, kc * KE:(kc + 1) * KE], start=True, stop=True)
                mm.then_inc(unit_done, 1)

            def turn_peaks(i, j):
                n = BODY * i + j
                pe.wait_ge(neg_ready, 2 * (n + 1))
                pe.wait_ge(unit_read, n * U + U)
                pe.transpose(sm[:, (j * U + U - 1) % 2, 0:P], neg[:], ident[:]).then_inc(unit_done, 1)

            def score_tile(i, j, kt):
                n, g = BODY * i + j, j // CHUNKS
                if kt == 0:
                    pe.wait_ge(unit_read, (n + 1) * U + 2)
                for a in range(2):
                    pe.wait_ge(exp_done, (n * NKT + kt) * 2 + a + 1)
                    for h in (2 * a, 2 * a + 1):
                        mm = pe.matmul(st[0:KR, a, h % 2], k[:, g % 2, h, kt * P:kt * P + KR], q[:, j % QR, h], start=True, stop=True)
                    mm.then_inc(st_done, 1)

            def weigh(i, j, kt):
                n, g = BODY * i + j, j // CHUNKS
                if kt == 0:
                    pe.wait_ge(acc_read, n + 1)
                    if j % CHUNKS == 0:
                        pe.wait_ge(v_loaded[g % 2], DMA * (i + g // 2 + 1))
                pe.wait_ge(exp_done, (n * NKT + kt) * 2 + 4)
                for h in range(GH):
                    rows = slice(h * DH, (h + 1) * DH)
                    pe.matmul(acc[rows], v[0:KR, g % 2, kt, rows], e[0:KR, (j * NKT + kt) % 2, h],
                              start=(kt == 0), stop=(kt == NKT - 1), tile_position=(0, h * DH))
                for h in range(GH):
                    rows = slice(h * DH, (h + 1) * DH)
                    mm = pe.matmul(den[rows], ones[0:KR], e[0:KR, (j * NKT + kt) % 2, h],
                                   start=(kt == 0), stop=(kt == NKT - 1), tile_position=(0, h * DH))
                mm.then_inc(tile_used, 1)

            def step(i, j, bodies_left):
                ahead = j + AHEAD < BODY * bodies_left
                units = list(range(len(UNITS))) if ahead else []
                for kt in range(NKT):
                    score_tile(i, j, kt)
                    for u in units[kt * PER:(kt + 1) * PER]:
                        score_unit(i, j + AHEAD, u)
                    if kt == NKT - 2 and ahead:
                        turn_peaks(i, j + AHEAD)
                    if kt > 0:
                        weigh(i, j, kt - 1)
                weigh(i, j, NKT - 1)
                if NKT == 1 and ahead:
                    turn_peaks(i, j + AHEAD)

            pe.sem_inc(tile_used, 2)
            pe.wait_ge(small_in, 2 * DMA)
            pe.wait_ge(set_up, SETUP)
            for j in range(AHEAD):
                for u in range(len(UNITS)):
                    score_unit(0, j, u)
                turn_peaks(0, j)
            with pe.Fori(0, STEPS // BODY - 1) as i:
                for j in range(BODY):
                    step(i, j, 2)
            for j in range(BODY):
                step(STEPS // BODY - 1, j, 1)

        @block.scalar
        def _(act):
            def step(i, j):
                n = BODY * i + j
                for kt in range(NKT):
                    act.wait_ge(tile_used, n * NKT + kt + 1)
                    for a in range(2):
                        act.wait_ge(st_done, (n * NKT + kt) * 2 + a + 1)
                        act.activation(e[0:KR, (j * NKT + kt) % 2, 2 * a:2 * a + 2], st[0:KR, a], ACT.Exp, scale=SCALE).then_inc(exp_done, 1)

            act.sem_inc(exp_done, 2)
            with act.Fori(0, STEPS // BODY) as i:
                for j in range(BODY):
                    step(i, j)

        @block.vector
        def _(dve):
            def peaks(i, j):
                n = BODY * i + j
                for u, (h, tiles, kc) in enumerate(UNITS):
                    dve.wait_ge(unit_done, n * U + u + 1)
                    src = sm[:, (j * U + u) % 2, 0:len(tiles) * KE].rearrange("p (x k) -> p x k", k=KE)[:, :, 0:KW]
                    dst = peak[:, u:u + 1] if KC > 1 else top[:, h * TT:(h + 1) * TT]
                    dve.tensor_reduce(dst, src, AX.X, ALU.max).then_inc(unit_read, 1)
                dve.wait_ge(unit_read, n * U + len(UNITS) + 2)
                if KC > 1:
                    dve.tensor_reduce(top[:], peak[:].rearrange("p (x c) -> p x c", c=KC), AX.X, ALU.max).then_inc(top_done, 1)
                    dve.wait_ge(top_done, n + 1)
                dve.tensor_scalar(neg_hi[:], top[:], -1.0, None, ALU.mult).then_inc(neg_done, 1)
                dve.wait_ge(neg_done, n + 1)
                pair = neg[:, 3 * DH:P].rearrange("p (x s) -> p x s", s=2)
                dve.tensor_copy(pair[:, :, 0], neg_hi[:].bitcast(F32)).then_inc(neg_ready, 1)
                dve.scalar_tensor_tensor(out=pair[:, :, 1], in0=top[:], scalar=-1.0, in1=neg_hi[:].bitcast(F32),
                                         op0=ALU.mult, op1=ALU.subtract).then_inc(neg_ready, 1)
                dve.wait_ge(unit_done, (n + 1) * U)
                dve.tensor_tensor(q[3 * DH:P, j % QR].rearrange("p h (x w) -> p (h x) w", w=P),
                                  sm[3 * DH:P, (j * U + U - 1) % 2, 0:P].unsqueeze(1).to_broadcast([DH, GH * TT, P]),
                                  mask[3 * DH:P].unsqueeze(2).to_broadcast([DH, GH * TT, P]), ALU.mult).then_inc(unit_read, 1)

            def normalise(i, j):
                n = BODY * i + j
                dve.wait_ge(tile_used, (n + 1) * NKT + 2)
                dve.transpose(den_t[:], den[:]).then_inc(inv_step, 1)
                dve.wait_ge(inv_step, 4 * n + 1)
                dve.reciprocal(inv[:], den_t[:].rearrange("p (c r) -> p c r", r=DH)[:, :, 0]).then_inc(inv_step, 1)
                dve.wait_ge(inv_step, 4 * n + 2)
                dve.tensor_copy(inv_b[:].rearrange("p (c r) -> p c r", r=DH), inv[:].unsqueeze(2).to_broadcast([P, W // DH, DH])).then_inc(inv_step, 1)
                dve.wait_ge(inv_step, 4 * n + 3)
                dve.transpose(inv_t[:], inv_b[:]).then_inc(inv_step, 1)
                dve.wait_ge(inv_step, 4 * n + 4)
                dve.wait_ge(o_stored[j % 2], DMA * (BODY // 2 * i + j // 2 + 1))
                dve.tensor_tensor(o[:, j % 2], acc[:], inv_t[:], ALU.mult).then_inc(acc_read, 1)

            def step(i, j, bodies_left):
                if j + AHEAD < BODY * bodies_left:
                    peaks(i, j + AHEAD)
                normalise(i, j)

            dve.sem_inc(unit_read, 2)
            dve.sem_inc(acc_read, 1)
            for part, value in ((k[3 * DH:P, 0].bitcast(F32), 1.0), (k[3 * DH:P, 1].bitcast(F32), 1.0), (ones[:], 1.0), (neg[:], 0.0)):
                dve.memset(part, value).then_inc(set_up, 1)
            if KE > KW:
                dve.memset(k[0:3 * DH, :, :, keys:].bitcast(F32), 0.0).then_inc(set_up, 1)
            dve.wait_ge(set_up, SETUP)
            dve.wait_ge(small_in, 2 * DMA)
            for j in range(AHEAD):
                peaks(0, j)
            with dve.Fori(0, STEPS // BODY - 1) as i:
                for j in range(BODY):
                    step(i, j, 2)
            for j in range(BODY):
                step(STEPS // BODY - 1, j, 1)


def mlp(nc, d, u_in, x_in, gate, out):
    with nc.cleanup_on_exit(), ExitStack() as ctx:
        sb = lambda n, s, t=F32: ctx.enter_context(nc.sbuf_tensor("mlp_" + n, s, t))
        sem = lambda n: nc.alloc_semaphore("mlp_" + n)
        ph = ctx.enter_context(nc.psum_tensor("mlp_ph", [P, 4, W], F32))
        py = ctx.enter_context(nc.psum_tensor("mlp_py", [P, TT, W], F32))
        w1 = sb("w1", [P, 2, KT, HID], F32R)
        w2 = sb("w2", [P, 2, HT, C], F32R)
        us = sb("us", [P, 2, 2, KT, W], F32R)
        x = sb("x", [P, TT, C])
        work = sb("work", [P, 4, W])
        gs = sb("gs", [P, 2, 2, W], F32R)
        grow = sb("grow", [P, B, C])
        brow = sb("brow", [P, B, C])
        b1 = sb("b1", [P, HT])
        gelu, gated = work[:, 0:2], work[:, 2:4]
        small_in, stage_in = sem("small_in"), [sem("stage_in0"), sem("stage_in1")]
        w_hi, w_lo, rows_done = sem("w_hi"), sem("w_lo"), sem("rows_done")
        u_loaded, x_loaded, biased = [sem("u_loaded0"), sem("u_loaded1")], sem("x_loaded"), sem("biased")
        hidden_done, gelu_done, g_hi, g_lo, used = sem("hidden_done"), sem("gelu_done"), sem("g_hi"), sem("g_lo"), sem("used")
        y_read, x_ready, stored = sem("y_read"), sem("x_ready"), sem("stored")
        passed = sem("passed")
        block = ctx.enter_context(nc.Block())
        stages = [x[:], work[:]]
        pieces = [(channels(d["L1_xcond_mlp_w1"])[:, :, c * C:(c + 1) * C], w1[:, :, :, c * C:(c + 1) * C]) for c in range(HID // C)] + \
                 [(channels(d["L1_xcond_mlp_w2"])[:, c * KT:(c + 1) * KT], w2[:, :, c * KT:(c + 1) * KT]) for c in range(HT // KT)]
        NP = len(pieces)
        SMALL = 1 + 2 * B

        @block.sync
        def _(sp):
            sp.sem_inc(stored, DMA)
            with nc.allow_non_contiguous_dma(reason="a short vector, once"):
                sp.dma_start(b1[:], column(d["L1_xcond_mlp_b1"])).then_inc(small_in, DMA)
            for b in range(B):
                sp.dma_start(brow[:, b], d["L1_xcond_mlp_b2"].partition_broadcast(P)).then_inc(small_in, DMA)
                sp.dma_start(grow[:, b], gate[b].partition_broadcast(P)).then_inc(small_in, DMA)
            for k, (src, _) in enumerate(pieces):
                if k >= 2:
                    sp.wait_ge(w_lo, k - 1)
                sp.dma_start(stages[k % 2], src).then_inc(stage_in[k % 2], DMA)

            def load_u(i, b, first=False):
                if not first:
                    sp.wait_ge(used, (2 * i + b - 1) * HT + 2)
                    sp.sem_inc(passed, 1)
                for part in range(2):
                    sp.dma_start(us[:, b, part].bitcast(F32), u_in[part, b, :, bass.ds(i * W, W)].rearrange("(t p) w -> p t w", p=P)).then_inc(u_loaded[b], DMA)

            def chunk(i, b, left):
                sp.wait_ge(stored, DMA * (2 * i + b + 1))
                sp.sem_inc(passed, 1)
                sp.dma_start(x[:], x_in[b, bass.ds(i * W, W), :].rearrange("(t p) c -> p t c", p=P)).then_inc(x_loaded, DMA)
                if left > 1:
                    load_u(*chunk_after(i, b))
                sp.wait_ge(x_ready, (2 * i + b + 1) * TT)
                sp.sem_inc(passed, 1)
                sp.dma_start(out[b, bass.ds(i * W, W), :].rearrange("(t p) c -> p t c", p=P), x[:]).then_inc(stored, DMA)

            load_u(0, 0, True)
            sp.wait_ge(w_lo, NP)
            with sp.Fori(0, CHUNKS - 1) as i:
                for b in range(B):
                    chunk(i, b, 3)
            for b in range(B):
                chunk(CHUNKS - 1, b, B - b)
            sp.wait_ge(stored, DMA * (B * CHUNKS + 1))

        @block.tensor
        def _(pe):
            def hidden(i, b, m):
                n = 2 * i + b
                if m == 0:
                    pe.wait_ge(u_loaded[b], 2 * DMA * (i + 1))
                pe.wait_ge(gelu_done, n * HT + m + 1)
                for t in range(KT):
                    for s, (pm, pw) in enumerate(PARTS):
                        mm = pe.matmul(ph[:, m % 4], w1[:, pw, t, m * P:(m + 1) * P], us[:, b, pm, t],
                                       start=(t == 0 and s == 0), stop=(t == KT - 1 and s == 2))
                mm.then_inc(hidden_done, 1)

            def output(i, b, m):
                n = 2 * i + b
                if m == 0:
                    pe.wait_ge(y_read, n * TT + 1)
                pe.wait_ge(g_lo, n * HT + m + 1)
                for tt in range(TT):
                    for s, (pm, pw) in enumerate(PARTS):
                        mm = pe.matmul(py[:, tt], gs[:, m % 2, pw, tt * P:(tt + 1) * P], w2[:, pm, m],
                                       start=(m == 0 and s == 0), stop=(m == HT - 1 and s == 2))
                mm.then_inc(used, 1)

            pe.sem_inc(used, 2)
            pe.wait_ge(w_lo, NP)
            with pe.Fori(0, CHUNKS) as i:
                for b in range(B):
                    for m in range(HT + 1):
                        if m < HT:
                            hidden(i, b, m)
                        if m > 0:
                            output(i, b, m - 1)

        @block.scalar
        def _(act):
            act.sem_inc(gelu_done, 4)
            for k, (_, dst) in enumerate(pieces):
                act.wait_ge(stage_in[k % 2], DMA * (k // 2 + 1))
                act.activation(dst[:, 0], stages[k % 2], ACT.Copy).then_inc(w_hi, 1)
            act.wait_ge(small_in, DMA * SMALL)
            act.wait_ge(w_lo, NP)
            with act.Fori(0, CHUNKS) as i:
                for b in range(B):
                    n = 2 * i + b
                    for m in range(HT):
                        act.wait_ge(used, n * HT + m + 1)
                        act.wait_ge(hidden_done, n * HT + m + 1)
                        act.activation(gelu[:, m % 2], ph[:, m % 4], ACT.Gelu_apprx_tanh, bias=b1[:, m:m + 1]).then_inc(gelu_done, 1)

        @block.vector
        def _(dve):
            dve.sem_inc(y_read, 1)
            for k, (_, dst) in enumerate(pieces):
                dve.wait_ge(w_hi, k + 1)
                dve.tensor_tensor(dst[:, 1], stages[k % 2], dst[:, 0].bitcast(F32), ALU.subtract).then_inc(w_lo, 1)
            dve.wait_ge(small_in, DMA * SMALL)
            with dve.Fori(0, CHUNKS) as i:
                for b in range(B):
                    n = 2 * i + b
                    for m in range(HT):
                        dve.wait_ge(gelu_done, n * HT + m + 5)
                        dve.wait_ge(used, n * HT + m + 1)
                        dve.tensor_copy(gs[:, m % 2, 0], gelu[:, m % 2]).then_inc(g_hi, 1)
                        dve.wait_ge(g_hi, n * HT + m + 1)
                        dve.tensor_tensor(gs[:, m % 2, 1], gelu[:, m % 2], gs[:, m % 2, 0].bitcast(F32), ALU.subtract).then_inc(g_lo, 1)
                    dve.wait_ge(used, (n + 1) * HT + 2)
                    dve.wait_ge(biased, n + 1)
                    for tt in range(TT):
                        dve.tensor_tensor(gated[:, tt % 2], py[:, tt], grow[:, b], ALU.mult).then_inc(y_read, 1)
                        dve.wait_ge(y_read, n * TT + tt + 2)
                        dve.tensor_tensor(x[:, tt], x[:, tt], gated[:, tt % 2], ALU.add).then_inc(x_ready, 1)

        @block.gpsimd
        def _(pool):
            pool.wait_ge(small_in, DMA * SMALL)
            pool.tensor_tensor(brow[:], brow[:], grow[:], ALU.mult).then_inc(rows_done, 1)
            pool.wait_ge(rows_done, 1)
            with pool.Fori(0, CHUNKS) as i:
                for b in range(B):
                    pool.wait_ge(x_loaded, DMA * (2 * i + b + 1))
                    pool.tensor_tensor(x[:], x[:], brow[:, b].unsqueeze(1).to_broadcast([P, TT, C]), ALU.add).then_inc(biased, 1)


def build(nc, d, out):
    def dram(name, shape, t=F32):
        return nc.dram_tensor("s_" + name, shape, t, kind="Internal").ap()

    q, k = dram("q", [2, B, C, T]), dram("k", [2, B, C, T])
    v, o = dram("v", [B, T, C]), dram("o", [B, C, T])
    x1, x2, x3 = dram("x1", [B, T, C]), dram("x2", [B, T, C]), dram("x3", [B, T, C])
    u = dram("u", [2, B, C, T])
    gates = dram("gates", [2, B, C])
    kv = [(dram(f"k{a}", [2, B, C, S]), dram(f"v{a}", [B, S, C])) for a in range(2)]
    with nc.sbuf_tensor("mod", [P, MODS, B], F32) as mod:
        def vector_of(tile):
            return lambda b, t: mod[:, tile + t, b:b + 1]

        w = lambda name, c: d[name][:, c * C:(c + 1) * C]
        vec = lambda name, c: d[name][c * C:(c + 1) * C]
        conditioning(nc, d, mod, gates, kv)
        chunk_pass(nc, d, "p1", d["x"], None, None, None, None, None, 1e-5, vector_of(0), vector_of(4),
                   [(d["L0_xcond_Wq"], d["L0_xcond_bq"], q)], None)
        attention(nc, d, "a1", q, kv[0][0], kv[0][1], o, S)
        chunk_pass(nc, d, "p2", d["x"], x1, o, d["L0_xcond_Wp"], d["L0_xcond_bp"], None, 1e-6, vector_of(20), vector_of(16),
                   [(w("L1_xcond_qkv_w", 0), vec("L1_xcond_qkv_b", 0), q), (w("L1_xcond_qkv_w", 1), vec("L1_xcond_qkv_b", 1), k)],
                   (w("L1_xcond_qkv_w", 2), vec("L1_xcond_qkv_b", 2), v))
        attention(nc, d, "a2", q, k, v, o, T)
        chunk_pass(nc, d, "p3", x1, x2, o, d["L1_xcond_self_o_w"], d["L1_xcond_self_o_b"], gates[0], 1e-6,
                   lambda b, t: mod[:, 40 + t, 0:1], lambda b, t: mod[:, 40 + t, 1:2],
                   [(d["L1_xcond_q_w"], d["L1_xcond_q_b"], q)], None)
        attention(nc, d, "a3", q, kv[1][0], kv[1][1], o, S)
        chunk_pass(nc, d, "p4", x2, x3, o, d["L1_xcond_cross_o_w"], d["L1_xcond_cross_o_b"], None, 1e-6, vector_of(32), vector_of(28),
                   [], None, plain=u)
        mlp(nc, d, u, x3, gates[1], out)


def kernel(**inputs):
    import concourse.bacc as bacc
    from concourse.bass_utils import run_bass_kernel_spmd

    nc = bacc.Bacc("TRN2", target_bir_lowering=False, num_devices=1)
    arrays = {f"in_{name}": np.ascontiguousarray(a) for name, a in inputs.items()}
    arrays["in_ident"] = np.eye(P, dtype=np.float32)
    arrays["in_mask"] = np.zeros((P, GH * TT), np.float32)
    for x in range(GH * TT):
        arrays["in_mask"][3 * DH + 2 * x:3 * DH + 2 * x + 2, x] = 1.0
    d = {k[3:]: nc.dram_tensor(k, a.shape, mybir.dt.from_np(a.dtype), kind="ExternalInput").ap() for k, a in arrays.items()}
    out = nc.dram_tensor("out", (B, T, C), F32, kind="ExternalOutput").ap()
    build(nc, d, out)
    r = run_bass_kernel_spmd(nc, [arrays], core_ids=[0])
    return r.results[0]["out"]
```

```python
from contextlib import ExitStack

import numpy as np

import concourse.bass as bass
from concourse import mybir

F32 = mybir.dt.float32
F32R = mybir.dt.float32r
ALU = mybir.AluOpType
ACT = mybir.ActivationFunctionType
AX = mybir.AxisListType

P = 128
B, T, C = 2, 2048, 512
S = 77
HEADS, DH = 16, 32
HID = 4 * C
KT = C // P
HT = HID // P
W = 512
CHUNKS = T // W
TT = W // P
GH = P // DH
GROUPS = HEADS // GH
SCALE = DH ** -0.5
PARTS = [(0, 0), (0, 1), (1, 0)]
DMA = 16
MODS = (2 + 2 + 6 + 1) * KT


def channels(ap):
    return ap.rearrange("(t p) n -> p t n", p=P)


def column(ap):
    return ap.rearrange("(t p) -> p t", p=P)


def chunk_after(i, b):
    return (i, 1) if b == 0 else (i + 1, 0)


def conditioning(nc, d, mod, gates, kv):
    NS, NA = 2 * C // P, 6 * C // P
    with nc.cleanup_on_exit(), ExitStack() as ctx:
        sb = lambda n, s, t=F32: ctx.enter_context(nc.sbuf_tensor("cn_" + n, s, t))
        sem = lambda n: nc.alloc_semaphore("cn_" + n)
        ps = ctx.enter_context(nc.psum_tensor("cn_ps", [P, 8, W], F32))
        ident = sb("ident", [P, P])
        cond = sb("cond", [P, KT, B])
        act_c = sb("act_c", [P, KT, B])
        act_row = sb("act_row", [P, KT, B, P])
        ctx_tok = sb("ctx_tok", [S, B, C])
        ctx_n = sb("ctx_n", [S, B, C])
        wss = sb("wss", [P, 2, KT, 2 * C])
        ada = sb("ada", [P, KT, 6 * C])
        wkv = sb("wkv", [P, 2, KT, 2 * C])
        bias = sb("bias", [P, 2 * NS + NA])
        kbias = sb("kbias", [P, 2, KT])
        vbias = sb("vbias", [S, 2, C])
        gbias = sb("gbias", [P, 2, C])
        gate_row = sb("gate_row", [P, 2, B, C])
        stats = sb("stats", [S, B, 6])
        mv = sb("mv", [S, B, 2])
        rstd = sb("rstd", [S, B])
        epst = sb("epst", [S, 1])
        ctxT = sb("ctxT", [P, 2, B, KT, S])
        kf = sb("kf", [P, 2, B, KT, S])
        khi = sb("khi", [P, 2, B, KT, S], F32R)
        klo = sb("klo", [P, 2, B, KT, S], F32R)
        vf = sb("vf", [S, 2, B, C])
        small_in, wss_in, ada_in, wkv_in = sem("small_in"), sem("wss_in"), sem("ada_in"), sem("wkv_in")
        silu_done, row_done, mods_done, mod_out = sem("silu_done"), sem("row_done"), sem("mods_done"), sem("mod_out")
        var_done, sqrt_done, norm_done = sem("var_done"), sem("sqrt_done"), sem("norm_done")
        turned, ctx_out, eps_set = sem("turned"), sem("ctx_out"), sem("eps_set")
        k_done, v_done, k_out, split, v_out, g_done, g_out, stored = (sem(n) for n in (
            "k_done", "v_done", "k_out", "split", "v_out", "g_done", "g_out", "stored"))
        dve_step = sem("dve_step")
        block = ctx.enter_context(nc.Block())
        SMALL = 15

        @block.sync
        def _(sp):
            with nc.allow_non_contiguous_dma(reason="short vectors, once"):
                for b in range(B):
                    sp.dma_start(cond[:, :, b], column(d["cond_1024"][b])).then_inc(small_in, DMA)
                sp.dma_start(ident[:], d["ident"]).then_inc(small_in, DMA)
                sp.dma_start(ctx_tok[:], d["ctx_1024"].rearrange("b s c -> s b c")).then_inc(small_in, DMA)
                for o, n, name in ((0, NS, "L0_xcond_bss_q"), (NS, NS, "L0_xcond_bss_kv"), (2 * NS, NA, "L1_xcond_ada_b")):
                    sp.dma_start(bias[:, o:o + n], column(d[name])).then_inc(small_in, DMA)
                for a, name in enumerate(("L0_xcond_bkv", "L1_xcond_kv_b")):
                    sp.dma_start(kbias[:, a], column(d[name][0:C])).then_inc(small_in, DMA)
                    sp.dma_start(vbias[:, a], d[name][C:2 * C].partition_broadcast(S)).then_inc(small_in, DMA)
                for g in range(2):
                    sp.dma_start(gbias[:, g], d["L1_xcond_ada_b"][(3 * g + 2) * C:(3 * g + 3) * C].partition_broadcast(P)).then_inc(small_in, DMA)
                sp.dma_start(mod[:, 2 * NS + NA:2 * NS + NA + KT, 0], column(d["L1_xcond_norm2_g"])).then_inc(small_in, DMA)
                sp.dma_start(mod[:, 2 * NS + NA:2 * NS + NA + KT, 1], column(d["L1_xcond_norm2_b"])).then_inc(small_in, DMA)
            for a, name in enumerate(("L0_xcond_Wss_q", "L0_xcond_Wss_kv")):
                sp.dma_start(wss[:, a], channels(d[name])).then_inc(wss_in, DMA)
            for a, name in enumerate(("L0_xcond_Wkv", "L1_xcond_kv_w")):
                sp.dma_start(wkv[:, a], channels(d[name])).then_inc(wkv_in, DMA)
            sp.dma_start(ada[:], channels(d["L1_xcond_ada_w"])).then_inc(ada_in, DMA)
            sp.wait_ge(split, 2)
            sp.wait_ge(v_out, 2 * B)
            for a in range(2):
                for b in range(B):
                    for part, t in ((0, khi), (1, klo)):
                        sp.dma_start(kv[a][0][part, b].rearrange("(t p) s -> p t s", p=P), t[:, a, b].bitcast(F32)).then_inc(stored, DMA)
                    sp.dma_start(kv[a][1][b], vf[:, a, b]).then_inc(stored, DMA)
            sp.wait_ge(g_out, 2 * B)
            sp.dma_start(gates.rearrange("g b c -> (g b c)").rearrange("(o n) -> o n", o=1),
                         gate_row[0:1].rearrange("p g b c -> p (g b c)")).then_inc(stored, DMA)
            sp.wait_ge(stored, DMA * (2 * B * 3 + 1))

        @block.tensor
        def _(pe):
            pe.wait_ge(small_in, DMA * SMALL)
            for b in range(B):
                for t in range(KT):
                    mm = pe.transpose(ps[:, 5 + b, t * S:(t + 1) * S], ctx_tok[:, b, t * P:(t + 1) * P], ident[0:S, 0:S])
            mm.then_inc(turned, 1)
            pe.wait_ge(norm_done, 2)
            for b in range(B):
                for t in range(KT):
                    mm = pe.transpose(ps[:, 3 + b, t * S:(t + 1) * S], ctx_n[:, b, t * P:(t + 1) * P], ident[0:S, 0:S])
            mm.then_inc(turned, 1)
            pe.wait_ge(wss_in, DMA * 2)
            pe.wait_ge(silu_done, 1)
            for j in range(2 * NS):
                for t in range(KT):
                    mm = pe.matmul(ps[:, 0, j * B:(j + 1) * B], wss[:, j // NS, t, (j % NS) * P:(j % NS + 1) * P],
                                   act_c[:, t], start=(t == 0), stop=(t == KT - 1))
            mm.then_inc(mods_done, 1)
            pe.wait_ge(wkv_in, DMA * 2)
            for n, a in enumerate((1, 0)):
                pe.wait_ge(ctx_out, 1 if a == 1 else 1 + B)
                for b in range(B):
                    if n:
                        pe.wait_ge(k_out, b + 1)
                    for m in range(KT):
                        for t in range(KT):
                            mm = pe.matmul(ps[:, 1 + b, m * S:(m + 1) * S], wkv[:, a, t, m * P:(m + 1) * P],
                                           ctxT[:, a, b, t], start=(t == 0), stop=(t == KT - 1))
                    mm.then_inc(k_done, 1)
                    if n:
                        pe.wait_ge(v_out, b + 1)
                    for t in range(KT):
                        mm = pe.matmul(ps[0:S, 6 + b, :], ctxT[:, a, b, t], wkv[:, a, t, C:2 * C],
                                       start=(t == 0), stop=(t == KT - 1))
                    mm.then_inc(v_done, 1)
            pe.wait_ge(ada_in, DMA)
            pe.wait_ge(mod_out, 1)
            for j in range(NA):
                for t in range(KT):
                    mm = pe.matmul(ps[:, 0, j * B:(j + 1) * B], ada[:, t, j * P:(j + 1) * P],
                                   act_c[:, t], start=(t == 0), stop=(t == KT - 1))
            mm.then_inc(mods_done, 1)
            pe.wait_ge(row_done, 1)
            for g in range(2):
                for b in range(B):
                    n = g * B + b
                    if n == 3:
                        pe.wait_ge(mod_out, 2)
                    for t in range(KT):
                        mm = pe.matmul(ps[:, (3, 4, 5, 0)[n], :], act_row[:, t, b], ada[:, t, (3 * g + 2) * C:(3 * g + 3) * C],
                                       start=(t == 0), stop=(t == KT - 1))
                    mm.then_inc(g_done, 1)

        @block.scalar
        def _(act):
            act.wait_ge(small_in, DMA * SMALL)
            act.activation(act_c[:], cond[:], ACT.Silu).then_inc(silu_done, 1)
            act.wait_ge(var_done, 1)
            act.wait_ge(eps_set, 1)
            act.activation(rstd[:], mv[:, :, 1], ACT.Sqrt, bias=epst[:, 0:1]).then_inc(sqrt_done, 1)
            for n, a in enumerate((1, 0)):
                for b in range(B):
                    act.wait_ge(k_done, n * B + b + 1)
                    for m in range(KT):
                        ins = act.activation(kf[:, a, b, m], ps[:, 1 + b, m * S:(m + 1) * S], ACT.Identity,
                                             bias=kbias[:, a, m:m + 1])
                    ins.then_inc(k_out, 1)

        @block.vector
        def _(dve):
            dve.memset(epst[:], 1e-5).then_inc(eps_set, 1)
            dve.wait_ge(small_in, DMA * SMALL)
            steps = 0
            for b in range(B):
                ins = dve.bn_stats(stats[:, b], ctx_tok[:, b])
            ins.then_inc(dve_step, 1)
            dve.wait_ge(dve_step, 1)
            for b in range(B):
                ins = dve.bn_aggr(mv[:, b], stats[:, b])
            ins.then_inc(var_done, 1)
            dve.wait_ge(turned, 1)
            dve.tensor_copy(ctxT[:, 1], ps[:, 5:7, 0:KT * S].rearrange("p b (t s) -> p b t s", t=KT)).then_inc(ctx_out, 1)
            dve.wait_ge(sqrt_done, 1)
            dve.reciprocal(rstd[:], rstd[:]).then_inc(dve_step, 1)
            dve.wait_ge(dve_step, 2)
            for b in range(B):
                dve.tensor_scalar(ctx_n[:, b], ctx_tok[:, b], mv[:, b, 0:1], rstd[:, b:b + 1],
                                  ALU.subtract, ALU.mult).then_inc(norm_done, 1)
            dve.wait_ge(silu_done, 1)
            for t in range(KT):
                for b in range(B):
                    ins = dve.tensor_copy(act_row[:, t, b], act_c[:, t, b:b + 1].to_broadcast([P, P]))
            ins.then_inc(row_done, 1)
            dve.wait_ge(mods_done, 1)
            dve.tensor_tensor(mod[:, 0:2 * NS], ps[:, 0, 0:2 * NS * B].rearrange("p (j b) -> p j b", b=B),
                              bias[:, 0:2 * NS].unsqueeze(2).to_broadcast([P, 2 * NS, B]), ALU.add).then_inc(mod_out, 1)
            dve.wait_ge(mod_out, 1)
            for o in (0, NS):
                ins = dve.tensor_scalar(mod[:, o:o + KT], mod[:, o:o + KT], 1.0, None, ALU.add)
            ins.then_inc(dve_step, 1)
            dve.wait_ge(dve_step, 3)
            dve.wait_ge(turned, 2)
            for b in range(B):
                for t in range(KT):
                    ins = dve.tensor_scalar(ctxT[:, 0, b, t], ps[:, 3 + b, t * S:(t + 1) * S],
                                            mod[:, NS + t, b:b + 1], mod[:, NS + KT + t, b:b + 1], ALU.mult, ALU.add)
                ins.then_inc(ctx_out, 1)
            for n, a in enumerate((1, 0)):
                for b in range(B):
                    dve.wait_ge(v_done, n * B + b + 1)
                    dve.tensor_tensor(vf[:, a, b], ps[0:S, 6 + b, :], vbias[:, a], ALU.add).then_inc(v_out, 1)
            dve.wait_ge(k_out, 2 * B)
            dve.tensor_copy(khi[:], kf[:]).then_inc(split, 1)
            dve.wait_ge(split, 1)
            dve.tensor_tensor(klo[:].rearrange("p a b t s -> p (a b t s)"), kf[:].rearrange("p a b t s -> p (a b t s)"),
                              khi[:].bitcast(F32).rearrange("p a b t s -> p (a b t s)"), ALU.subtract).then_inc(split, 1)
            dve.wait_ge(mods_done, 2)
            dve.tensor_tensor(mod[:, 2 * NS:2 * NS + NA], ps[:, 0, 0:NA * B].rearrange("p (j b) -> p j b", b=B),
                              bias[:, 2 * NS:2 * NS + NA].unsqueeze(2).to_broadcast([P, NA, B]), ALU.add).then_inc(mod_out, 1)
            dve.wait_ge(mod_out, 2)
            for o in (KT, 4 * KT):
                dve.tensor_scalar(mod[:, 2 * NS + o:2 * NS + o + KT], mod[:, 2 * NS + o:2 * NS + o + KT], 1.0, None, ALU.add)
            for g in range(2):
                for b in range(B):
                    n = g * B + b
                    dve.wait_ge(g_done, n + 1)
                    dve.tensor_tensor(gate_row[:, g, b], ps[:, (3, 4, 5, 0)[n], :], gbias[:, g], ALU.add).then_inc(g_out, 1)


def chunk_pass(nc, d, name, x_in, x_out, o_in, w_out, b_out, gate, eps, scale, shift, projections, values, plain=None):
    NM = sum(KT for _ in projections)
    TILES = NM + (TT if values else 0)
    RING = 4
    OS = 2 if plain is not None else 1
    XC = 2 if gate is None else 0
    with nc.cleanup_on_exit(), ExitStack() as ctx:
        sb = lambda n, s, t=F32: ctx.enter_context(nc.sbuf_tensor(f"{name}_{n}", s, t))
        sem = lambda n: nc.alloc_semaphore(f"{name}_{n}")
        po = ctx.enter_context(nc.psum_tensor(name + "_po", [P, 2, W], F32))
        pt = ctx.enter_context(nc.psum_tensor(name + "_pt", [P, 2, W], F32))
        pp = ctx.enter_context(nc.psum_tensor(name + "_pp", [P, RING, W], F32))
        ident = sb("ident", [P, P])
        weights = ([w_out] if o_in is not None else []) + [w for w, _, _ in projections] + ([values[0]] if values else [])
        NWT = len(weights)
        wparts = sb("w", [P, max(NWT, 1), 2, KT, C], F32R)
        stage = sb("stage", [P, 2, KT, C])
        x = sb("x", [P, 2, TT, C])
        xn = sb("xn", [P, TT, C])
        u = sb("u", [P, KT, W])
        us = sb("us", [P, 2, 2, KT, W], F32R)
        stats = sb("stats", [P, TT, 6])
        mv = sb("mv", [P, TT, 2])
        rstd = sb("rstd", [P, TT])
        epst = sb("epst", [P, 1])
        if o_in is not None:
            o = sb("o", [P, KT, W])
            os_ = sb("os", [P, OS, 2, KT, W], F32R)
            orow = sb("orow", [P, C])
            brow = sb("brow", [P, B, C])
        if gate is not None:
            grow = sb("grow", [P, B, C])
            gated = sb("gated", [P, 2, C])
        if projections:
            out = sb("out", [P, RING, 2, W], F32R)
            pbias = sb("pbias", [P, NM])
        if values:
            vout = sb("vout", [P, 2, C])
            vrow = sb("vrow", [P, C])
        small_in, stage_in = sem("small_in"), [sem("stage_in0"), sem("stage_in1")]
        w_hi, w_lo, rows_ready, rows_done = sem("w_hi"), sem("w_lo"), sem("rows_ready"), sem("rows_done")
        x_in_s, o_loaded = [sem("x_in0"), sem("x_in1")], sem("o_in")
        x_stored = [sem("x_stored0"), sem("x_stored1")]
        biased, o_hi, o_lo, oproj_done = sem("biased"), sem("o_hi"), sem("o_lo"), sem("oproj_done")
        gated_done, x_ready = sem("gated_done"), sem("x_ready")
        stats_done, var_done, std_done, rstd_done, xn_done = (sem(n) for n in (
            "stats_done", "var_done", "std_done", "rstd_done", "xn_done"))
        turned, u_done, u_lo = sem("turned"), sem("u_done"), sem("u_lo")
        proj_done, proj_hi, proj_out = sem("proj_done"), sem("proj_hi"), sem("proj_out")
        out_stored = [sem(f"out_stored{r}") for r in range(RING)]
        v_stored = [sem("v_stored0"), sem("v_stored1")]
        passed, aggregating = sem("passed"), sem("aggregating")
        u_stored = [sem("u_stored0"), sem("u_stored1")]
        block = ctx.enter_context(nc.Block())
        small = [(ident[:], d["ident"])]
        if o_in is not None:
            small.append((orow[:], b_out.partition_broadcast(P)))
        if gate is not None:
            small += [(grow[:, b], gate[b].partition_broadcast(P)) for b in range(B)]
        if values:
            small.append((vrow[:], values[1].partition_broadcast(P)))
        m = 0
        for _, bias, _ in projections:
            small.append((pbias[:, m:m + KT], column(bias)))
            m += KT
        N = CHUNKS * B

        @block.sync
        def _(sp):
            with nc.allow_non_contiguous_dma(reason="short vectors, once"):
                for dst, src in small:
                    sp.dma_start(dst, src).then_inc(small_in, DMA)

            def load_weight(k):
                if k >= 2:
                    sp.wait_ge(w_lo, k - 1)
                sp.dma_start(stage[:, k % 2], channels(weights[k])).then_inc(stage_in[k % 2], DMA)

            def load_x(i, b, first=False):
                if not first:
                    sp.wait_ge(xn_done, (2 * (i - 1) + b + 1) * TT)
                    if x_out is not None:
                        sp.sem_inc(passed, 1)
                        sp.wait_ge(x_stored[b], DMA * i)
                    sp.sem_inc(passed, 1)
                sp.dma_start(x[:, b], x_in[b, bass.ds(i * W, W), :].rearrange("(t p) c -> p t c", p=P)).then_inc(x_in_s[b], DMA)

            def load_o(i, b):
                sp.wait_ge(o_lo, 2 * i + b + 1)
                sp.sem_inc(passed, 1)
                sp.dma_start(o[:], o_in[b, :, bass.ds(i * W, W)].rearrange("(t p) w -> p t w", p=P)).then_inc(o_loaded, DMA)

            def store_x(i, b):
                sp.wait_ge(x_ready, (2 * i + b + 1) * TT + XC)
                sp.sem_inc(passed, 1)
                sp.dma_start(x_out[b, bass.ds(i * W, W), :].rearrange("(t p) c -> p t c", p=P), x[:, b]).then_inc(x_stored[b], DMA)

            def store_outputs(i, b):
                for t in range(TILES):
                    sp.wait_ge(proj_out, (2 * i + b) * TILES + t + 1 + RING)
                    sp.sem_inc(passed, 1)
                    if t < NM:
                        dst = projections[t // KT][2]
                        sp.dma_start(dst[:, b, t % KT * P:(t % KT + 1) * P, bass.ds(i * W, W)].rearrange("s p w -> p s w"),
                                     out[:, t % RING].bitcast(F32)).then_inc(out_stored[t % RING], DMA)
                    else:
                        sp.dma_start(values[2][b, bass.ds(i * W + (t - NM) * P, P)], vout[:, t % 2]).then_inc(v_stored[t % 2], DMA)
                if plain is not None:
                    sp.wait_ge(u_lo, 2 * i + b + 2)
                    sp.sem_inc(passed, 1)
                    sp.dma_start(plain[0, b, :, bass.ds(i * W, W)].rearrange("(t p) w -> p t w", p=P), us[:, b, 0].bitcast(F32)).then_inc(u_stored[b], DMA)
                    sp.dma_start(plain[1, b, :, bass.ds(i * W, W)].rearrange("(t p) w -> p t w", p=P), us[:, b, 1].bitcast(F32)).then_inc(u_stored[b], DMA)

            def superstep(i, b, left):
                if left > 2:
                    if o_in is not None and plain is None:
                        load_o(i + 1, b)
                    load_x(i + 1, b)
                if left > 1 and x_out is not None:
                    store_x(*chunk_after(i, b))
                if plain is not None and left > 3:
                    load_o(*chunk_after(i + 1, b))
                store_outputs(i, b)

            for s in (out_stored if projections else []) + (v_stored if values else []):
                sp.sem_inc(s, DMA)
            for s in u_stored if plain is not None else []:
                sp.sem_inc(s, 2 * DMA)
            load_x(0, 0, True)
            if o_in is not None:
                load_o(0, 0)
            load_weight(0) if NWT else None
            load_x(0, 1, True)
            for k in range(1, NWT):
                load_weight(k)
            if o_in is not None:
                load_o(0, 1)
                store_x(0, 0)
                if plain is not None:
                    load_o(1, 0)
            with sp.Fori(0, CHUNKS - 2) as i:
                for b in range(B):
                    superstep(i, b, 4)
            for n in range(N - 2 * B, N):
                superstep(n // B, n % B, N - n)
            for b in range(2):
                if x_out is not None:
                    sp.wait_ge(x_stored[b], DMA * CHUNKS)
                if values:
                    sp.wait_ge(v_stored[b], DMA * (N * TT // 2 + 1))
                if plain is not None:
                    sp.wait_ge(u_stored[b], 2 * DMA * (CHUNKS + 1))
            if projections:
                for r in range(RING):
                    sp.wait_ge(out_stored[r], DMA * (N * NM // RING + 1))

        @block.tensor
        def _(pe):
            def split_matmul(out_ap, lhs, rhs):
                for t in range(KT):
                    for q, (pm, pw) in enumerate(PARTS):
                        mm = pe.matmul(out_ap, lhs(pw, t), rhs(pm, t), start=(t == 0 and q == 0),
                                       stop=(t == KT - 1 and q == 2))
                return mm

            def output_projection(i, b):
                n = 2 * i + b
                pe.wait_ge(o_lo, n + 2)
                for tt in range(TT):
                    pe.wait_ge(x_ready, n * TT + tt + 1) if gate is None else pe.wait_ge(gated_done, n * TT + tt + 1)
                    split_matmul(po[:, tt % 2], lambda s, t: os_[:, b % OS, s, t, tt * P:(tt + 1) * P],
                                 lambda s, t: wparts[:, 0, s, t]).then_inc(oproj_done, 1)

            def turn(i, b):
                n = 2 * i + b
                for t in range(KT):
                    pe.wait_ge(u_done, n * KT + t + 1)
                    for tt in range(TT):
                        if t == 0:
                            pe.wait_ge(xn_done, n * TT + tt + 1)
                        mm = pe.transpose(pt[:, t % 2, tt * P:(tt + 1) * P], xn[:, tt, t * P:(t + 1) * P], ident[:])
                    mm.then_inc(turned, 1)

            def project(i, b):
                n = 2 * i + b
                pe.wait_ge(u_lo, n + 2)
                for t in range(TILES):
                    pe.wait_ge(proj_out, n * TILES + t + 1)
                    w = NWT - len(projections) - (1 if values else 0) + t // KT
                    if t < NM:
                        mm = split_matmul(pp[:, t % RING], lambda s, k: wparts[:, w, s, k, t % KT * P:(t % KT + 1) * P],
                                          lambda s, k: us[:, b, s, k])
                    else:
                        mm = split_matmul(pp[:, t % RING], lambda s, k: us[:, b, s, k, (t - NM) * P:(t - NM + 1) * P],
                                          lambda s, k: wparts[:, w, s, k])
                    mm.then_inc(proj_done, 1)

            def superstep(i, b, left):
                if left > 1 and o_in is not None:
                    output_projection(*chunk_after(i, b))
                if plain is not None:
                    turn(i, b)
                if left > 1 and o_in is None:
                    turn(*chunk_after(i, b))
                if TILES:
                    project(i, b)
                if left > 1 and o_in is not None and plain is None:
                    turn(*chunk_after(i, b))

            pe.wait_ge(small_in, DMA * len(small))
            if NWT:
                pe.wait_ge(w_lo, NWT if o_in is None else 1)
            if o_in is not None:
                output_projection(0, 0)
            if plain is None:
                turn(0, 0)
            if NWT:
                pe.wait_ge(w_lo, NWT)
            with pe.Fori(0, CHUNKS - 1) as i:
                for b in range(B):
                    superstep(i, b, 3)
            for b in range(B):
                superstep(CHUNKS - 1, b, B - b)

        @block.scalar
        def _(act):
            def split_o(i, b):
                n = 2 * i + b
                act.wait_ge(o_loaded, DMA * (n + 1))
                if not isinstance(n, int) or n >= OS:
                    act.wait_ge(x_ready if gate is None else gated_done, (n - OS + 1) * TT + 2)
                act.activation(os_[:, b % OS, 0], o[:], ACT.Copy).then_inc(o_hi, 1)

            def std(i, b):
                act.wait_ge(var_done, 2 * i + b + 1)
                act.activation(rstd[:], mv[:, :, 1], ACT.Sqrt, bias=epst[:, 0:1]).then_inc(std_done, 1)

            def modulate(i, b):
                n = 2 * i + b
                for t in range(KT):
                    act.wait_ge(turned, n * KT + t + 1)
                    if t == 0:
                        act.wait_ge(u_lo, n + 1)
                        if plain is not None:
                            act.wait_ge(u_stored[b], 2 * DMA * (i + 1))
                    act.activation(us[:, b, 0, t], pt[:, t % 2], ACT.Identity, bias=shift(b, t), scale=scale(b, t))
                    act.activation(u[:, t], pt[:, t % 2], ACT.Identity, bias=shift(b, t), scale=scale(b, t)).then_inc(u_done, 1)

            def evacuate(i, b):
                n = 2 * i + b
                for t in range(NM):
                    act.wait_ge(proj_done, n * TILES + t + 1)
                    act.wait_ge(out_stored[t % RING], DMA * (n * (NM // RING) + t // RING + 1))
                    act.activation(out[:, t % RING, 0], pp[:, t % RING], ACT.Identity, bias=pbias[:, t:t + 1]).then_inc(proj_hi, 1)

            def superstep(i, b, left):
                if plain is not None:
                    if left > 2:
                        split_o(i + 1, b)
                    modulate(i, b)
                if o_in is None and left > 1:
                    modulate(*chunk_after(i, b))
                if o_in is not None and left > 1:
                    std(*chunk_after(i, b))
                    if plain is None and left > 2:
                        split_o(i + 1, b)
                if o_in is None and left > 2:
                    std(i + 1, b)
                evacuate(i, b)
                if o_in is not None and plain is None and left > 1:
                    modulate(*chunk_after(i, b))

            act.sem_inc(u_done, 2)
            if o_in is not None:
                split_o(0, 0)
            act.wait_ge(rows_ready, 1)
            for k in range(NWT):
                act.wait_ge(stage_in[k % 2], DMA * (k // 2 + 1))
                act.activation(wparts[:, k, 0], stage[:, k % 2], ACT.Copy).then_inc(w_hi, 1)
            std(0, 0)
            if plain is None:
                modulate(0, 0)
            if o_in is not None:
                split_o(0, 1)
            else:
                std(0, 1)
            with act.Fori(0, CHUNKS - 1) as i:
                for b in range(B):
                    superstep(i, b, 3)
            for b in range(B):
                superstep(CHUNKS - 1, b, B - b)

        @block.vector
        def _(dve):
            def split_o(i, b):
                n = 2 * i + b
                dve.wait_ge(o_hi, n + 1)
                dve.tensor_tensor(os_[:, b % OS, 1], o[:], os_[:, b % OS, 0].bitcast(F32), ALU.subtract).then_inc(o_lo, 1)

            def normalise(i, b, first=False):
                n = 2 * i + b
                dve.wait_ge(x_in_s[b], DMA * (i + 1))
                for tt in range(TT):
                    if o_in is not None:
                        dve.wait_ge(oproj_done, n * TT + tt + 1)
                        dve.wait_ge(biased, n + 1)
                        if gate is not None:
                            dve.tensor_tensor(gated[:, tt % 2], po[:, tt % 2], grow[:, b], ALU.mult).then_inc(gated_done, 1)
                            dve.wait_ge(gated_done, n * TT + tt + 3)
                            dve.tensor_tensor(x[:, b, tt], x[:, b, tt], gated[:, tt % 2], ALU.add).then_inc(x_ready, 1)
                            dve.wait_ge(x_ready, n * TT + tt + 1)
                        else:
                            dve.tensor_tensor(x[:, b, tt], po[:, tt % 2], x[:, b, tt], ALU.add).then_inc(x_ready, 1)
                            dve.wait_ge(x_ready, n * TT + tt + 3)
                    dve.bn_stats(stats[:, tt], x[:, b, tt]).then_inc(stats_done, 1)
                dve.wait_ge(stats_done, (n + 1) * TT)
                dve.sem_inc(aggregating, 1)
                for tt in range(TT):
                    ins = dve.bn_aggr(mv[:, tt], stats[:, tt])
                ins.then_inc(var_done, 1)
                dve.wait_ge(std_done, n + 1)
                dve.reciprocal(rstd[:], rstd[:]).then_inc(rstd_done, 1)
                dve.wait_ge(rstd_done, n + 1)
                if not first:
                    dve.wait_ge(turned, n * KT)
                for tt in range(TT):
                    dve.tensor_scalar(xn[:, tt], x[:, b, tt], mv[:, tt, 0:1], rstd[:, tt:tt + 1],
                                      ALU.subtract, ALU.mult).then_inc(xn_done, 1)

            def evacuate(i, b):
                n = 2 * i + b
                for t in range(NM):
                    dve.wait_ge(proj_hi, n * NM + t + 1)
                    dve.scalar_tensor_tensor(out=out[:, t % RING, 1], in0=pp[:, t % RING], scalar=pbias[:, t:t + 1],
                                             in1=out[:, t % RING, 0].bitcast(F32), op0=ALU.add, op1=ALU.subtract).then_inc(proj_out, 1)
                for t in range(NM, TILES):
                    dve.wait_ge(proj_done, n * TILES + t + 1)
                    dve.wait_ge(v_stored[t % 2], DMA * (n * (TT // 2) + (t - NM) // 2 + 1))
                    dve.tensor_tensor(vout[:, t % 2], pp[:, t % RING], vrow[:], ALU.add).then_inc(proj_out, 1)

            def split_u(i, b):
                n = 2 * i + b
                for t in range(KT):
                    dve.wait_ge(u_done, n * KT + t + 3)
                    ins = dve.tensor_tensor(us[:, b, 1, t], u[:, t], us[:, b, 0, t].bitcast(F32), ALU.subtract)
                ins.then_inc(u_lo, 1)

            def superstep(i, b, left):
                if plain is not None and left > 2:
                    split_o(i + 1, b)
                if o_in is None and left > 1:
                    split_u(*chunk_after(i, b))
                if o_in is not None and left > 1:
                    normalise(*chunk_after(i, b))
                    if plain is None and left > 2:
                        split_o(i + 1, b)
                if o_in is None and left > 2:
                    normalise(i + 1, b)
                evacuate(i, b)
                if plain is not None:
                    split_u(i, b)
                if o_in is not None and plain is None and left > 1:
                    split_u(*chunk_after(i, b))

            dve.memset(epst[:], eps).then_inc(rows_ready, 1)
            dve.sem_inc(proj_out, RING)
            dve.sem_inc(u_lo, 1)
            if o_in is not None:
                dve.sem_inc(o_lo, 1)
                dve.sem_inc(gated_done if gate is not None else x_ready, 2)
                split_o(0, 0)
            for k in range(NWT):
                dve.wait_ge(w_hi, k + 1)
                dve.tensor_tensor(wparts[:, k, 1], stage[:, k % 2], wparts[:, k, 0].bitcast(F32), ALU.subtract).then_inc(w_lo, 1)
            normalise(0, 0, True)
            if plain is None:
                split_u(0, 0)
            if o_in is not None:
                split_o(0, 1)
            else:
                normalise(0, 1)
            with dve.Fori(0, CHUNKS - 1) as i:
                for b in range(B):
                    superstep(i, b, 3)
            for b in range(B):
                superstep(CHUNKS - 1, b, B - b)

        if o_in is not None:
            @block.gpsimd
            def _(pool):
                pool.wait_ge(small_in, DMA * len(small))
                if gate is not None:
                    for b in range(B):
                        ins = pool.tensor_tensor(brow[:, b], orow[:], grow[:, b], ALU.mult)
                    ins.then_inc(rows_done, 1)
                    pool.wait_ge(rows_done, 1)

                def add_bias(i, b):
                    row = orow[:] if gate is None else brow[:, b]
                    pool.wait_ge(x_in_s[b], DMA * (i + 1))
                    pool.tensor_tensor(x[:, b], x[:, b], row.unsqueeze(1).to_broadcast([P, TT, C]), ALU.add).then_inc(biased, 1)

                with pool.Fori(0, CHUNKS) as i:
                    for b in range(B):
                        add_bias(i, b)


def attention(nc, d, name, q_in, k_in, v_in, o_out, keys):
    NKT = -(-keys // P)
    KR = keys // NKT
    KC = -(-keys // W)
    KW = keys // KC
    KE = KW + KW % 2
    if KC > 1:
        UNITS = [(h, [qt], kc) for h in range(GH) for qt in range(TT) for kc in range(KC)]
    else:
        UNITS = [(h, list(range(TT)), 0) for h in range(GH)]
    U = len(UNITS)
    QR = 4
    ER = 4
    POOLED = [t for t in range(NKT - 2) if t % 3 != 2] if NKT > 2 else []
    ADDS = max(len(POOLED) - 1, 0)
    STEPS = B * GROUPS * CHUNKS
    BODY = 2 * CHUNKS
    TURN = 8 if NKT > 1 else 4
    TILES = GH * NKT + 1
    RING = 3
    LATE = 1 if NKT > 1 else 2
    DIVIDE_AT = range(6, 14, 2) if NKT > 1 else range(4)
    SETUP = 3 + KW % 2
    with nc.cleanup_on_exit(), ExitStack() as ctx:
        sb = lambda n, s, t=F32: ctx.enter_context(nc.sbuf_tensor(f"{name}_{n}", s, t))
        sem = lambda n: nc.alloc_semaphore(f"{name}_{n}")
        sm = ctx.enter_context(nc.psum_tensor(name + "_sm", [P, RING, W], F32))
        st = ctx.enter_context(nc.psum_tensor(name + "_st", [P, RING, W], F32))
        acc = ctx.enter_context(nc.psum_tensor(name + "_acc", [P, 2, W], F32))
        ident = sb("ident", [P, P])
        mask = sb("mask", [P, GH])
        ones = sb("ones", [P, DH])
        q = sb("q", [P, QR, GH, W], F32R)
        k = sb("k", [P, 2, GH, KC * KE], F32R)
        v = sb("v", [P, 2, NKT, P])
        e = sb("e", [P, ER, GH, W])
        if POOLED:
            esum = sb("esum", [P, GH, W])
        peak = sb("peak", [P, U])
        top = sb("top", [P, GH * TT])
        neg_hi = sb("neg_hi", [P, GH * TT], F32R)
        neg = sb("neg", [P, TT, P])
        sums = sb("sums", [P, 2, 2, W])
        den_t = sb("den_t", [P, W])
        inv = sb("inv", [P, W // DH])
        inv_b = sb("inv_b", [P, W])
        inv_t = sb("inv_t", [P, 2, W])
        o = sb("o", [P, 2, W])
        small_in, set_up, pool_set_up = sem("small_in"), sem("set_up"), sem("pool_set_up")
        q_loaded = [sem(f"q_loaded{r}") for r in range(QR)]
        k_loaded, v_loaded = [sem("k_loaded0"), sem("k_loaded1")], [sem("v_loaded0"), sem("v_loaded1")]
        unit_done, unit_read = sem("unit_done"), sem("unit_read")
        top_done, neg_done, neg_ready = sem("top_done"), sem("neg_done"), sem("neg_ready")
        score_done, score_read, tile_used, e_added = sem("score_done"), sem("score_read"), sem("tile_used"), sem("e_added")
        divided, acc_read, scaled = sem("divided"), sem("acc_read"), sem("scaled")
        o_stored = [sem("o_stored0"), sem("o_stored1")]
        passed = sem("passed")
        block = ctx.enter_context(nc.Block())

        def exists(i, j):
            return not isinstance(i, int) or 0 <= BODY * i + j < STEPS

        def place(kt, h):
            return GH * kt + h + (GH * kt + h >= TURN)

        def number(i, j, p):
            return (BODY * i + j) * TILES + p + (p < TURN or exists(i, j + 1))

        def turned(i, j):
            return number(i, j - 1, TURN) if j else 0

        def bank_free(engine, i, j, p):
            near = p < 2 or (TURN < p <= TURN + RING and not exists(i, j + 1))
            engine.wait_ge(score_read, number(i, j, p) + near)

        def run(engine, step, late=0):
            for j in range(LATE):
                step(0, j)
            with engine.Fori(0, STEPS // BODY - 1) as i:
                for j in range(LATE, BODY + LATE):
                    step(i, j)
            for j in range(LATE, BODY + late):
                step(STEPS // BODY - 1, j)

        @block.sync
        def _(sp):
            for dst, src in ((ident[:], d["ident"]), (mask[:], d["mask"])):
                sp.dma_start(dst, src).then_inc(small_in, DMA)
            for s in o_stored:
                sp.sem_inc(s, DMA)

            def load_q(i, j):
                for row, part in enumerate((0, 0, 1)):
                    src = q_in[part].rearrange("b (g h r) t -> (b g) r h t", g=GROUPS, h=GH)
                    sp.dma_start(q[row * DH:(row + 1) * DH, j % QR].bitcast(F32),
                                 src[2 * i + j // CHUNKS, :, :, j % CHUNKS * W:(j % CHUNKS + 1) * W]
                                 ).then_inc(q_loaded[j % QR], DMA)

            def load_k(i, g):
                for row, part in enumerate((0, 1, 0)):
                    src = k_in[part].rearrange("b (g h r) t -> (b g) r h t", g=GROUPS, h=GH)
                    sp.dma_start(k[row * DH:(row + 1) * DH, g % 2, :, 0:keys].bitcast(F32),
                                 src[2 * i + g]).then_inc(k_loaded[g % 2], DMA)

            def load_v(i, g):
                sp.dma_start(v[0:KR, g % 2], v_in[(i + g // 2) // 2, :, bass.ds(((i + g // 2) % 2 * 2 + g % 2) * P, P)].rearrange("(t p) c -> p t c", p=KR)
                             ).then_inc(v_loaded[g % 2], DMA)

            def store_o(i, j):
                sp.wait_ge(scaled, BODY * i + j + 3)
                sp.sem_inc(passed, 1)
                dst = o_out.rearrange("b (g p) t -> (b g) p t", p=P)
                sp.dma_start(dst[2 * i + j // CHUNKS, :, j % CHUNKS * W:(j % CHUNKS + 1) * W],
                             o[:, j % 2]).then_inc(o_stored[j % 2], DMA)

            def step(i, j):
                if exists(i, j - 1) and exists(i, j + QR - 1):
                    sp.wait_ge(score_done, (BODY * i + j) * TILES + 1)
                    sp.sem_inc(passed, 1)
                if exists(i, j + QR - 1):
                    load_q(i, j + QR - 1)
                if j % CHUNKS == 0 and exists(i, j + CHUNKS):
                    load_k(i, j // CHUNKS + 1)
                    if exists(i, j - 1):
                        sp.wait_ge(tile_used, (BODY * i + j) * NKT + ER)
                        sp.sem_inc(passed, 1)
                    load_v(i, j // CHUNKS + 1)
                if exists(i, j - LATE):
                    store_o(i, j - LATE)

            load_q(0, 0)
            load_k(0, 0)
            load_v(0, 0)
            for j in range(1, QR - 1):
                load_q(0, j)
            run(sp, step, LATE)
            for s in o_stored:
                sp.wait_ge(s, DMA * (STEPS // 2 + 1))

        @block.tensor
        def _(pe):
            def score_unit(i, j, u):
                n, g = BODY * i + j, j // CHUNKS
                h, tiles, kc = UNITS[u]
                if u == 0:
                    pe.wait_ge(q_loaded[j % QR], 3 * DMA * (BODY // QR * i + j // QR + 1))
                    if j % CHUNKS == 0:
                        pe.wait_ge(k_loaded[g % 2], 3 * DMA * (i + g // 2 + 1))
                pe.wait_ge(unit_read, n * U + u + (2 if u == 0 else 0))
                for x, qt in enumerate(tiles):
                    mm = pe.matmul(sm[:, u % RING, x * KE:(x + 1) * KE], q[0:3 * DH, j % QR, h, qt * P:(qt + 1) * P],
                                   k[0:3 * DH, g % 2, h, kc * KE:(kc + 1) * KE], start=True, stop=True)
                mm.then_inc(unit_done, 1)

            def turn_peaks(i, j):
                pe.wait_ge(neg_ready, 2 * (BODY * i + j + 1))
                if j:
                    bank_free(pe, i, j - 1, TURN)
                for qt in range(TT):
                    mm = pe.transpose(st[:, TURN % RING if j else 0, qt * P:(qt + 1) * P], neg[:, qt], ident[:])
                mm.then_inc(score_done, 1)

            def score_tile(i, j, kt, h):
                g = j // CHUNKS
                if kt == 0 and h == 0:
                    pe.wait_ge(score_read, turned(i, j) + 3)
                    if j % CHUNKS == 0:
                        pe.wait_ge(pool_set_up, 1)
                bank_free(pe, i, j, place(kt, h))
                pe.matmul(st[0:KR, place(kt, h) % RING], k[:, g % 2, h, kt * P:kt * P + KR],
                          q[:, j % QR, h], start=True, stop=True).then_inc(score_done, 1)

            def weigh(i, j, kt):
                n, g = BODY * i + j, j // CHUNKS
                if kt == 0:
                    pe.wait_ge(acc_read, n + 1)
                    if j % CHUNKS == 0:
                        pe.wait_ge(v_loaded[g % 2], DMA * (i + g // 2 + 1))
                pe.wait_ge(score_read, number(i, j, place(kt, GH - 1)) + 3)
                for h in range(GH):
                    rows = slice(h * DH, (h + 1) * DH)
                    mm = pe.matmul(acc[rows, 0], v[0:KR, g % 2, kt, rows], e[0:KR, (j * NKT + kt) % ER, h],
                                   start=(kt == 0), stop=(kt == NKT - 1), tile_position=(0, h * DH))
                if kt in POOLED:
                    mm.then_inc(tile_used, 1)

            def add_up(i, j, kt):
                if kt in POOLED:
                    return
                first = min(t for t in range(NKT) if t not in POOLED)
                operands = [e[0:KR, (j * NKT + kt) % ER]]
                if POOLED and kt == NKT - 1:
                    pe.wait_ge(e_added, (BODY * i + j + 1) * ADDS)
                    operands.append(esum)
                for x, operand in enumerate(operands):
                    for h in range(GH):
                        mm = pe.matmul(acc[h * DH:(h + 1) * DH, 1], ones[0:KR], operand[:, h], start=(kt == first),
                                       stop=(kt == NKT - 1 and x == len(operands) - 1), tile_position=(0, h * DH))
                mm.then_inc(tile_used, 1)

            def step(i, j):
                turn, ahead = exists(i, j + 1), exists(i, j + 2)
                total = NKT * 8 + (NKT - len(POOLED) + (NKT > 1)) * 4
                units, weight = 0, 0
                for kt in range(NKT):
                    parts = [(1, score_tile, (i, j, kt, h)) for h in range(GH)] if exists(i, j) else []
                    w = (i, j, kt - 1) if kt else (i, j - 1, NKT - 1)
                    if exists(w[0], w[1]) and (kt == 0 or exists(i, j)):
                        products = [(4, weigh, w), ((w[2] not in POOLED) * (4 + 4 * (w[2] == NKT - 1 > 0)), add_up, w)]
                        parts = parts[:2] + products[:1] + parts[2:] + products[1:] if NKT > 1 else products + parts
                    if NKT == 1 and turn:
                        parts.append((0, turn_peaks, (i, j + 1)))
                    if kt == 1 and turn:
                        parts.append((0, turn_peaks, (i, j + 1)))
                    for part_weight, part, where in parts:
                        part(*where)
                        weight += part_weight
                        while ahead and units < U and units * total <= (weight - 1) * U:
                            score_unit(i, j + 2, units)
                            units += 1
                while ahead and units < U:
                    score_unit(i, j + 2, units)
                    units += 1

            pe.sem_inc(tile_used, ER)
            pe.wait_ge(small_in, 2 * DMA)
            pe.wait_ge(set_up, SETUP)
            for j in range(2):
                for u in range(U):
                    score_unit(0, j, u)
            turn_peaks(0, 0)
            run(pe, step, 1)

        @block.scalar
        def _(act):
            def spread(i, j):
                act.wait_ge(score_done, turned(i, j) + 1)
                act.activation(q[3 * DH:P, j % QR], st[3 * DH:P, TURN % RING if j else 0].unsqueeze(1).to_broadcast([DH, GH, W]),
                               ACT.Copy).then_inc(score_read, 1)

            def exponentials(i, j, kt):
                n = BODY * i + j
                act.wait_ge(tile_used, n * NKT + kt + 1)
                before = (kt - ER) % NKT
                if before in POOLED and (kt >= ER or exists(i, j - 1)):
                    act.wait_ge(e_added, (n - (kt < ER)) * ADDS + max(POOLED.index(before), 1))
                for h in range(GH):
                    act.wait_ge(score_done, number(i, j, place(kt, h)) + 1)
                    act.activation(e[0:KR, (j * NKT + kt) % ER, h], st[0:KR, place(kt, h) % RING], ACT.Exp,
                                   scale=SCALE).then_inc(score_read, 1)

            def fetch_sums(i, j):
                n = BODY * i + j
                act.wait_ge(tile_used, (n + 1) * NKT + ER)
                act.wait_ge(scaled, n + 1)
                act.activation(sums[:, j % 2], acc[:], ACT.Copy).then_inc(acc_read, 1)

            def step(i, j):
                if NKT == 1 and exists(i, j - 1):
                    fetch_sums(i, j - 1)
                for kt in range(NKT):
                    if exists(i, j):
                        exponentials(i, j, kt)
                    if NKT == 1 and exists(i, j + 1):
                        spread(i, j + 1)
                    if NKT > 1 and kt == 0 and exists(i, j - 1):
                        fetch_sums(i, j - 1)
                    if kt == 1 and exists(i, j + 1):
                        spread(i, j + 1)

            act.sem_inc(score_read, 2)
            act.sem_inc(acc_read, 1)
            act.wait_ge(set_up, SETUP)
            spread(0, 0)
            run(act, step, 1)

        @block.vector
        def _(dve):
            def peak_of_unit(i, j, u):
                h, tiles, _ = UNITS[u]
                if u == 0 and exists(i, j - 1):
                    dve.wait_ge(neg_ready, 2 * (BODY * i + j))
                dve.wait_ge(unit_done, (BODY * i + j) * U + u + 1)
                src = sm[:, u % RING, 0:len(tiles) * KE].rearrange("p (x k) -> p x k", k=KE)[:, :, 0:KW]
                dst = peak[:, u:u + 1] if KC > 1 else top[:, h * TT:(h + 1) * TT]
                dve.tensor_reduce(dst, src, AX.X, ALU.max).then_inc(unit_read, 1)

            def minus_peaks(i, j):
                n = BODY * i + j
                dve.wait_ge(unit_read, (n + 1) * U + 2)
                if KC > 1:
                    dve.tensor_reduce(top[:], peak[:].rearrange("p (x c) -> p x c", c=KC), AX.X, ALU.max).then_inc(top_done, 1)
                    dve.wait_ge(top_done, n + 1)
                dve.tensor_scalar(neg_hi[:], top[:], -1.0, None, ALU.mult).then_inc(neg_done, 1)
                dve.wait_ge(neg_done, n + 1)
                if exists(i, j - 1):
                    dve.wait_ge(score_done, turned(i, j - 1) + 1)
                by_head = lambda ap: ap.rearrange("p (h t) -> p h t", t=TT)
                parts = neg[:, :, 3 * DH:3 * DH + 2 * GH].rearrange("p t (h s) -> p h t s", s=2)
                dve.tensor_copy(parts[:, :, :, 0], by_head(neg_hi[:].bitcast(F32))).then_inc(neg_ready, 1)
                dve.scalar_tensor_tensor(out=parts[:, :, :, 1], in0=by_head(top[:]), scalar=-1.0, in1=by_head(neg_hi[:].bitcast(F32)),
                                         op0=ALU.mult, op1=ALU.subtract).then_inc(neg_ready, 1)

            def divide(i, j, part):
                n = BODY * i + j
                if part == 0:
                    dve.wait_ge(acc_read, n + 2)
                    ins = dve.transpose(den_t[:], sums[:, j % 2, 1])
                else:
                    dve.wait_ge(divided, 4 * n + part)
                if part == 1:
                    ins = dve.reciprocal(inv[:], den_t[:].rearrange("p (c r) -> p c r", r=DH)[:, :, 0])
                if part == 2:
                    ins = dve.tensor_copy(inv_b[:].rearrange("p (c r) -> p c r", r=DH), inv[:].unsqueeze(2).to_broadcast([P, W // DH, DH]))
                if part == 3:
                    dve.wait_ge(scaled, n + 1)
                    ins = dve.transpose(inv_t[:, j % 2], inv_b[:])
                ins.then_inc(divided, 1)

            def step(i, j):
                for u in range(U):
                    if exists(i, j + 2):
                        peak_of_unit(i, j + 2, u)
                    if u in DIVIDE_AT and exists(i, j - LATE):
                        divide(i, j - LATE, DIVIDE_AT.index(u))
                if exists(i, j + 2):
                    minus_peaks(i, j + 2)

            dve.sem_inc(unit_read, 2)
            dve.memset(ones[:], 1.0).then_inc(set_up, 1)
            dve.memset(neg[:], 0.0).then_inc(set_up, 1)
            if KE > KW:
                dve.memset(k[0:3 * DH, :, :, keys:].bitcast(F32), 0.0).then_inc(set_up, 1)
            dve.wait_ge(small_in, 2 * DMA)
            dve.tensor_copy(k[3 * DH:P, 0], mask[3 * DH:P].unsqueeze(2).to_broadcast([DH, GH, KC * KE])).then_inc(set_up, 1)
            dve.wait_ge(set_up, SETUP)
            for j in range(2):
                for u in range(U):
                    peak_of_unit(0, j, u)
                minus_peaks(0, j)
            run(dve, step, LATE)

        @block.gpsimd
        def _(pool):
            def add(i, j, x):
                n, slot = BODY * i + j, lambda x: (j * NKT + POOLED[x]) % ER
                pool.wait_ge(score_read, number(i, j, place(POOLED[x], GH - 1)) + 3)
                if x > 1:
                    pool.wait_ge(e_added, n * ADDS + x - 1)
                elif exists(i, j - 1):
                    pool.wait_ge(tile_used, n * NKT + ER)
                pool.tensor_tensor(esum[:], e[:, slot(0)] if x == 1 else esum[:], e[:, slot(x)], ALU.add).then_inc(e_added, 1)

            def scale(i, j):
                n = BODY * i + j
                pool.wait_ge(o_stored[j % 2], DMA * (BODY // 2 * i + j // 2 + 1))
                pool.wait_ge(divided, 4 * (n + 1))
                pool.tensor_tensor(o[:, j % 2], sums[:, j % 2, 0], inv_t[:, j % 2], ALU.mult).then_inc(scaled, 1)

            def step(i, j):
                if POOLED and exists(i, j):
                    for x in range(1, 3):
                        add(i, j, x)
                if exists(i, j - LATE):
                    scale(i, j - LATE)
                if POOLED and exists(i, j):
                    for x in range(3, len(POOLED)):
                        add(i, j, x)

            pool.sem_inc(scaled, 2)
            pool.wait_ge(small_in, 2 * DMA)
            pool.tensor_copy(k[3 * DH:P, 1], mask[3 * DH:P].unsqueeze(2).to_broadcast([DH, GH, KC * KE])).then_inc(pool_set_up, 1)
            run(pool, step, LATE)


def mlp(nc, d, u_in, x_in, gate, out):
    with nc.cleanup_on_exit(), ExitStack() as ctx:
        sb = lambda n, s, t=F32: ctx.enter_context(nc.sbuf_tensor("mlp_" + n, s, t))
        sem = lambda n: nc.alloc_semaphore("mlp_" + n)
        ph = ctx.enter_context(nc.psum_tensor("mlp_ph", [P, 4, W], F32))
        py = ctx.enter_context(nc.psum_tensor("mlp_py", [P, TT, W], F32))
        w1 = sb("w1", [P, 2, KT, HID], F32R)
        w2 = sb("w2", [P, 2, HT, C], F32R)
        us = sb("us", [P, 2, 2, KT, W], F32R)
        x = sb("x", [P, TT, C])
        work = sb("work", [P, 4, W])
        gs = sb("gs", [P, 2, 2, W], F32R)
        grow = sb("grow", [P, B, C])
        brow = sb("brow", [P, B, C])
        b1 = sb("b1", [P, HT])
        gelu, gated = work[:, 0:2], work[:, 2:4]
        small_in, stage_in = sem("small_in"), [sem("stage_in0"), sem("stage_in1")]
        w_hi, w_lo, rows_done = sem("w_hi"), sem("w_lo"), sem("rows_done")
        u_loaded, x_loaded, biased = [sem("u_loaded0"), sem("u_loaded1")], sem("x_loaded"), sem("biased")
        hidden_done, gelu_done, g_hi, g_lo, used = sem("hidden_done"), sem("gelu_done"), sem("g_hi"), sem("g_lo"), sem("used")
        y_read, x_ready, stored = sem("y_read"), sem("x_ready"), sem("stored")
        passed = sem("passed")
        block = ctx.enter_context(nc.Block())
        stages = [x[:], work[:]]
        pieces = [(channels(d["L1_xcond_mlp_w1"])[:, :, c * C:(c + 1) * C], w1[:, :, :, c * C:(c + 1) * C]) for c in range(HID // C)] + \
                 [(channels(d["L1_xcond_mlp_w2"])[:, c * KT:(c + 1) * KT], w2[:, :, c * KT:(c + 1) * KT]) for c in range(HT // KT)]
        NP = len(pieces)
        SMALL = 1 + 2 * B

        @block.sync
        def _(sp):
            sp.sem_inc(stored, DMA)
            with nc.allow_non_contiguous_dma(reason="a short vector, once"):
                sp.dma_start(b1[:], column(d["L1_xcond_mlp_b1"])).then_inc(small_in, DMA)
            for b in range(B):
                sp.dma_start(brow[:, b], d["L1_xcond_mlp_b2"].partition_broadcast(P)).then_inc(small_in, DMA)
                sp.dma_start(grow[:, b], gate[b].partition_broadcast(P)).then_inc(small_in, DMA)
            for k, (src, _) in enumerate(pieces):
                if k >= 2:
                    sp.wait_ge(w_lo, k - 1)
                sp.dma_start(stages[k % 2], src).then_inc(stage_in[k % 2], DMA)

            def load_u(i, b, first=False):
                if not first:
                    sp.wait_ge(used, (2 * i + b - 1) * HT + 2)
                    sp.sem_inc(passed, 1)
                for part in range(2):
                    sp.dma_start(us[:, b, part].bitcast(F32), u_in[part, b, :, bass.ds(i * W, W)].rearrange("(t p) w -> p t w", p=P)).then_inc(u_loaded[b], DMA)

            def chunk(i, b, left):
                sp.wait_ge(stored, DMA * (2 * i + b + 1))
                sp.sem_inc(passed, 1)
                sp.dma_start(x[:], x_in[b, bass.ds(i * W, W), :].rearrange("(t p) c -> p t c", p=P)).then_inc(x_loaded, DMA)
                if left > 1:
                    load_u(*chunk_after(i, b))
                sp.wait_ge(x_ready, (2 * i + b + 1) * TT)
                sp.sem_inc(passed, 1)
                sp.dma_start(out[b, bass.ds(i * W, W), :].rearrange("(t p) c -> p t c", p=P), x[:]).then_inc(stored, DMA)

            load_u(0, 0, True)
            sp.wait_ge(w_lo, NP)
            with sp.Fori(0, CHUNKS - 1) as i:
                for b in range(B):
                    chunk(i, b, 3)
            for b in range(B):
                chunk(CHUNKS - 1, b, B - b)
            sp.wait_ge(stored, DMA * (B * CHUNKS + 1))

        @block.tensor
        def _(pe):
            def hidden(i, b, m):
                n = 2 * i + b
                if m == 0:
                    pe.wait_ge(u_loaded[b], 2 * DMA * (i + 1))
                pe.wait_ge(gelu_done, n * HT + m + 1)
                for t in range(KT):
                    for s, (pm, pw) in enumerate(PARTS):
                        mm = pe.matmul(ph[:, m % 4], w1[:, pw, t, m * P:(m + 1) * P], us[:, b, pm, t],
                                       start=(t == 0 and s == 0), stop=(t == KT - 1 and s == 2))
                mm.then_inc(hidden_done, 1)

            def output(i, b, m):
                n = 2 * i + b
                if m == 0:
                    pe.wait_ge(y_read, n * TT + 1)
                pe.wait_ge(g_lo, n * HT + m + 1)
                for tt in range(TT):
                    for s, (pm, pw) in enumerate(PARTS):
                        mm = pe.matmul(py[:, tt], gs[:, m % 2, pw, tt * P:(tt + 1) * P], w2[:, pm, m],
                                       start=(m == 0 and s == 0), stop=(m == HT - 1 and s == 2))
                mm.then_inc(used, 1)

            pe.sem_inc(used, 2)
            pe.wait_ge(w_lo, NP)
            with pe.Fori(0, CHUNKS) as i:
                for b in range(B):
                    for m in range(HT + 1):
                        if m < HT:
                            hidden(i, b, m)
                        if m > 0:
                            output(i, b, m - 1)

        @block.scalar
        def _(act):
            act.sem_inc(gelu_done, 4)
            for k, (_, dst) in enumerate(pieces):
                act.wait_ge(stage_in[k % 2], DMA * (k // 2 + 1))
                act.activation(dst[:, 0], stages[k % 2], ACT.Copy).then_inc(w_hi, 1)
            act.wait_ge(small_in, DMA * SMALL)
            act.wait_ge(w_lo, NP)
            with act.Fori(0, CHUNKS) as i:
                for b in range(B):
                    n = 2 * i + b
                    for m in range(HT):
                        act.wait_ge(used, n * HT + m + 1)
                        act.wait_ge(hidden_done, n * HT + m + 1)
                        act.activation(gelu[:, m % 2], ph[:, m % 4], ACT.Gelu_apprx_tanh, bias=b1[:, m:m + 1]).then_inc(gelu_done, 1)

        @block.vector
        def _(dve):
            dve.sem_inc(y_read, 1)
            for k, (_, dst) in enumerate(pieces):
                dve.wait_ge(w_hi, k + 1)
                dve.tensor_tensor(dst[:, 1], stages[k % 2], dst[:, 0].bitcast(F32), ALU.subtract).then_inc(w_lo, 1)
            dve.wait_ge(small_in, DMA * SMALL)
            with dve.Fori(0, CHUNKS) as i:
                for b in range(B):
                    n = 2 * i + b
                    for m in range(HT):
                        dve.wait_ge(gelu_done, n * HT + m + 5)
                        dve.wait_ge(used, n * HT + m + 1)
                        dve.tensor_copy(gs[:, m % 2, 0], gelu[:, m % 2]).then_inc(g_hi, 1)
                        dve.wait_ge(g_hi, n * HT + m + 1)
                        dve.tensor_tensor(gs[:, m % 2, 1], gelu[:, m % 2], gs[:, m % 2, 0].bitcast(F32), ALU.subtract).then_inc(g_lo, 1)
                    dve.wait_ge(used, (n + 1) * HT + 2)
                    dve.wait_ge(biased, n + 1)
                    for tt in range(TT):
                        dve.tensor_tensor(gated[:, tt % 2], py[:, tt], grow[:, b], ALU.mult).then_inc(y_read, 1)
                        dve.wait_ge(y_read, n * TT + tt + 2)
                        dve.tensor_tensor(x[:, tt], x[:, tt], gated[:, tt % 2], ALU.add).then_inc(x_ready, 1)

        @block.gpsimd
        def _(pool):
            pool.wait_ge(small_in, DMA * SMALL)
            pool.tensor_tensor(brow[:], brow[:], grow[:], ALU.mult).then_inc(rows_done, 1)
            pool.wait_ge(rows_done, 1)
            with pool.Fori(0, CHUNKS) as i:
                for b in range(B):
                    pool.wait_ge(x_loaded, DMA * (2 * i + b + 1))
                    pool.tensor_tensor(x[:], x[:], brow[:, b].unsqueeze(1).to_broadcast([P, TT, C]), ALU.add).then_inc(biased, 1)


def build(nc, d, out):
    def dram(name, shape, t=F32):
        return nc.dram_tensor("s_" + name, shape, t, kind="Internal").ap()

    q, k = dram("q", [2, B, C, T]), dram("k", [2, B, C, T])
    v, o = dram("v", [B, T, C]), dram("o", [B, C, T])
    x1, x2, x3 = dram("x1", [B, T, C]), dram("x2", [B, T, C]), dram("x3", [B, T, C])
    u = dram("u", [2, B, C, T])
    gates = dram("gates", [2, B, C])
    kv = [(dram(f"k{a}", [2, B, C, S]), dram(f"v{a}", [B, S, C])) for a in range(2)]
    with nc.sbuf_tensor("mod", [P, MODS, B], F32) as mod:
        def vector_of(tile):
            return lambda b, t: mod[:, tile + t, b:b + 1]

        w = lambda name, c: d[name][:, c * C:(c + 1) * C]
        vec = lambda name, c: d[name][c * C:(c + 1) * C]
        conditioning(nc, d, mod, gates, kv)
        chunk_pass(nc, d, "p1", d["x"], None, None, None, None, None, 1e-5, vector_of(0), vector_of(4),
                   [(d["L0_xcond_Wq"], d["L0_xcond_bq"], q)], None)
        attention(nc, d, "a1", q, kv[0][0], kv[0][1], o, S)
        chunk_pass(nc, d, "p2", d["x"], x1, o, d["L0_xcond_Wp"], d["L0_xcond_bp"], None, 1e-6, vector_of(20), vector_of(16),
                   [(w("L1_xcond_qkv_w", 0), vec("L1_xcond_qkv_b", 0), q), (w("L1_xcond_qkv_w", 1), vec("L1_xcond_qkv_b", 1), k)],
                   (w("L1_xcond_qkv_w", 2), vec("L1_xcond_qkv_b", 2), v))
        attention(nc, d, "a2", q, k, v, o, T)
        chunk_pass(nc, d, "p3", x1, x2, o, d["L1_xcond_self_o_w"], d["L1_xcond_self_o_b"], gates[0], 1e-6,
                   lambda b, t: mod[:, 40 + t, 0:1], lambda b, t: mod[:, 40 + t, 1:2],
                   [(d["L1_xcond_q_w"], d["L1_xcond_q_b"], q)], None)
        attention(nc, d, "a3", q, kv[1][0], kv[1][1], o, S)
        chunk_pass(nc, d, "p4", x2, x3, o, d["L1_xcond_cross_o_w"], d["L1_xcond_cross_o_b"], None, 1e-6, vector_of(32), vector_of(28),
                   [], None, plain=u)
        mlp(nc, d, u, x3, gates[1], out)


def kernel(**inputs):
    import concourse.bacc as bacc
    from concourse.bass_utils import run_bass_kernel_spmd

    nc = bacc.Bacc("TRN2", target_bir_lowering=False, num_devices=1)
    arrays = {f"in_{name}": np.ascontiguousarray(a) for name, a in inputs.items()}
    arrays["in_ident"] = np.eye(P, dtype=np.float32)
    arrays["in_mask"] = np.zeros((P, GH), np.float32)
    for h in range(GH):
        arrays["in_mask"][3 * DH + 2 * h:3 * DH + 2 * h + 2, h] = 1.0
    d = {k[3:]: nc.dram_tensor(k, a.shape, mybir.dt.from_np(a.dtype), kind="ExternalInput").ap() for k, a in arrays.items()}
    out = nc.dram_tensor("out", (B, T, C), F32, kind="ExternalOutput").ap()
    build(nc, d, out)
    r = run_bass_kernel_spmd(nc, [arrays], core_ids=[0])
    return r.results[0]["out"]
```

```python
from contextlib import ExitStack

import numpy as np

import concourse.bass as bass
from concourse import mybir

F32 = mybir.dt.float32
F32R = mybir.dt.float32r
ALU = mybir.AluOpType
ACT = mybir.ActivationFunctionType
AX = mybir.AxisListType

P = 128
B, T, C = 2, 2048, 512
S = 77
HEADS, DH = 16, 32
HID = 4 * C
KT = C // P
HT = HID // P
W = 512
CHUNKS = T // W
TT = W // P
GH = P // DH
GROUPS = HEADS // GH
SCALE = DH ** -0.5
PARTS = [(0, 0), (0, 1), (1, 0)]
DMA = 16
MODS = (2 + 2 + 6 + 1) * KT


def channels(ap):
    return ap.rearrange("(t p) n -> p t n", p=P)


def column(ap):
    return ap.rearrange("(t p) -> p t", p=P)


class Weights:

    def __init__(self, nc, ctx, name, shape):
        self.raw = ctx.enter_context(nc.sbuf_tensor(name, [P] + shape, F32))
        size = 4 * int(np.prod(shape))
        self.lo = nc.alloc_sbuf_tensor_at(name + "_lo", [P] + shape, F32R, offset=nc.sbuf_base - size)


def chunk_after(i, b):
    return (i, 1) if b == 0 else (i + 1, 0)


def conditioning(nc, d, mod, gates, kv, preload):
    NS, NA = 2 * C // P, 6 * C // P
    with nc.cleanup_on_exit(), ExitStack() as ctx:
        sb = lambda n, s, t=F32: ctx.enter_context(nc.sbuf_tensor("cn_" + n, s, t))
        sem = lambda n: nc.alloc_semaphore("cn_" + n)
        ps = ctx.enter_context(nc.psum_tensor("cn_ps", [P, 8, W], F32))
        ident = sb("ident", [P, P])
        cond = sb("cond", [P, KT, B])
        act_c = sb("act_c", [P, KT, B])
        act_pad = sb("act_pad", [P, KT, DH])
        rows = sb("rows", [P, 3, C])
        ctx_tok = sb("ctx_tok", [S, B, C])
        ctx_n = sb("ctx_n", [S, B, C])
        wss = sb("wss", [P, 2, KT, 2 * C])
        ada = sb("ada", [P, KT, 6 * C])
        wkv = sb("wkv", [P, 2, KT, 2 * C])
        bias = sb("bias", [P, 2 * NS + NA])
        kbias = sb("kbias", [P, 2, KT])
        vbias = sb("vbias", [S, 2, C])
        gbias = sb("gbias", [P, 2, C])
        gate_row = sb("gate_row", [P, 2, C])
        stats = sb("stats", [S, B, 6])
        mv = sb("mv", [S, B, 2])
        rstd = sb("rstd", [S, B])
        epst = sb("epst", [S, 1])
        ctxT = sb("ctxT", [P, 2, B, KT, S])
        kf = sb("kf", [P, 2, B, KT, S])
        khi = sb("khi", [P, 2, B, KT, S], F32R)
        klo = sb("klo", [P, 2, B, KT, S], F32R)
        vf = sb("vf", [S, 2, B, C])
        small_in, wss_in, ada_in, wkv_in = sem("small_in"), sem("wss_in"), sem("ada_in"), sem("wkv_in")
        silu_done, pad_done, rows_done, rows_out = sem("silu_done"), sem("pad_done"), sem("rows_done"), sem("rows_out")
        mods_done, mod_out = sem("mods_done"), sem("mod_out")
        var_done, sqrt_done, norm_done = sem("var_done"), sem("sqrt_done"), sem("norm_done")
        turned, ctx_out, eps_set = sem("turned"), sem("ctx_out"), sem("eps_set")
        k_done, v_done, k_out, split, v_out, g_out, stored = (sem(n) for n in (
            "k_done", "v_done", "k_out", "split", "v_out", "g_out", "stored"))
        dve_step, pad_zero, preloaded = sem("dve_step"), sem("pad_zero"), sem("preloaded")
        block = ctx.enter_context(nc.Block())
        SMALL = 15
        GROUPS_OF_MODS = [(0, [0, 1, 2, 3]), (4, [0, 1, 2, 3]), (8, [0, 1])]

        @block.sync
        def _(sp):
            with nc.allow_non_contiguous_dma(reason="short vectors, once"):
                for b in range(B):
                    sp.dma_start(cond[:, :, b], column(d["cond_1024"][b])).then_inc(small_in, DMA)
                sp.dma_start(ident[:], d["ident"]).then_inc(small_in, DMA)
                sp.dma_start(ctx_tok[:], d["ctx_1024"].rearrange("b s c -> s b c")).then_inc(small_in, DMA)
                for o, n, name in ((0, NS, "L0_xcond_bss_q"), (NS, NS, "L0_xcond_bss_kv"), (2 * NS, NA, "L1_xcond_ada_b")):
                    sp.dma_start(bias[:, o:o + n], column(d[name])).then_inc(small_in, DMA)
                for a, name in enumerate(("L0_xcond_bkv", "L1_xcond_kv_b")):
                    sp.dma_start(kbias[:, a], column(d[name][0:C])).then_inc(small_in, DMA)
                    sp.dma_start(vbias[:, a], d[name][C:2 * C].partition_broadcast(S)).then_inc(small_in, DMA)
                for g in range(2):
                    sp.dma_start(gbias[:, g], d["L1_xcond_ada_b"][(3 * g + 2) * C:(3 * g + 3) * C].partition_broadcast(P)).then_inc(small_in, DMA)
                sp.dma_start(mod[:, 2 * NS + NA:2 * NS + NA + KT, 0], column(d["L1_xcond_norm2_g"])).then_inc(small_in, DMA)
                sp.dma_start(mod[:, 2 * NS + NA:2 * NS + NA + KT, 1], column(d["L1_xcond_norm2_b"])).then_inc(small_in, DMA)
            for a, name in enumerate(("L0_xcond_Wss_q", "L0_xcond_Wss_kv")):
                sp.dma_start(wss[:, a], channels(d[name])).then_inc(wss_in, DMA)
            for a, name in enumerate(("L0_xcond_Wkv", "L1_xcond_kv_w")):
                sp.dma_start(wkv[:, a], channels(d[name])).then_inc(wkv_in, DMA)
            sp.dma_start(ada[:], channels(d["L1_xcond_ada_w"])).then_inc(ada_in, DMA)
            for dst, src in preload:
                sp.dma_start(dst, src).then_inc(preloaded, DMA)
            sp.wait_ge(split, 2)
            sp.wait_ge(v_out, 2 * B)
            for a in range(2):
                for b in range(B):
                    for part, t in ((0, khi), (1, klo)):
                        sp.dma_start(kv[a][0][part, b].rearrange("(t p) s -> p t s", p=P), t[:, a, b].bitcast(F32)).then_inc(stored, DMA)
                    sp.dma_start(kv[a][1][b], vf[:, a, b]).then_inc(stored, DMA)
            sp.wait_ge(g_out, 2)
            for g, row in enumerate((2 * DH, DH)):
                sp.dma_start(gates[g], gate_row[row:row + B, g]).then_inc(stored, DMA)
            sp.wait_ge(stored, DMA * (2 * B * 3 + 2))
            sp.wait_ge(preloaded, DMA * len(preload))

        @block.tensor
        def _(pe):
            pe.wait_ge(small_in, DMA * SMALL)
            for b in range(B):
                for t in range(KT):
                    mm = pe.transpose(ps[:, 5 + b, t * S:(t + 1) * S], ctx_tok[:, b, t * P:(t + 1) * P], ident[0:S, 0:S])
            mm.then_inc(turned, 1)
            pe.wait_ge(norm_done, 2)
            for b in range(B):
                for t in range(KT):
                    mm = pe.transpose(ps[:, 3 + b, t * S:(t + 1) * S], ctx_n[:, b, t * P:(t + 1) * P], ident[0:S, 0:S])
            mm.then_inc(turned, 1)
            def mod_rows(group, bank):
                first, chunks = GROUPS_OF_MODS[group]
                for t in range(KT):
                    for x in chunks:
                        c = first + x
                        w = wss[:, c // 2, t, c % 2 * C:(c % 2 + 1) * C] if c < 4 else ada[:, t, (c - 4) * C:(c - 3) * C]
                        mm = pe.matmul(ps[x * DH:(x + 1) * DH, bank, :], act_pad[:, t], w, start=(t == 0), stop=(t == KT - 1),
                                       tile_position=(0, x * DH))
                mm.then_inc(rows_done, 1)

            def turn_rows(group, bank):
                used = len(GROUPS_OF_MODS[group][1]) * DH
                pe.wait_ge(rows_out, group + 1)
                for t in range(KT):
                    mm = pe.transpose(ps[:, bank, t * P:t * P + used], rows[0:used, group, t * P:(t + 1) * P], ident[0:used, 0:used])
                mm.then_inc(mods_done, 1)

            pe.wait_ge(wss_in, DMA * 2)
            pe.wait_ge(pad_done, 1)
            mod_rows(0, 0)
            turn_rows(0, 7)
            pe.wait_ge(wkv_in, DMA * 2)
            for n, a in enumerate((1, 0)):
                pe.wait_ge(ctx_out, 1 if a == 1 else 1 + B)
                for b in range(B):
                    if n:
                        pe.wait_ge(k_out, b + 1)
                    for m in range(KT):
                        for t in range(KT):
                            mm = pe.matmul(ps[:, 1 + b, m * S:(m + 1) * S], wkv[:, a, t, m * P:(m + 1) * P],
                                           ctxT[:, a, b, t], start=(t == 0), stop=(t == KT - 1))
                    mm.then_inc(k_done, 1)
                    if n == 0 and b == 1:
                        pe.wait_ge(mod_out, 1)
                    if n:
                        pe.wait_ge(v_out, b + 1)
                    for t in range(KT):
                        mm = pe.matmul(ps[0:S, 6 + b, :], ctxT[:, a, b, t], wkv[:, a, t, C:2 * C],
                                       start=(t == 0), stop=(t == KT - 1))
                    mm.then_inc(v_done, 1)
            pe.wait_ge(ada_in, DMA)
            mod_rows(1, 0)
            mod_rows(2, 3)
            turn_rows(1, 4)
            turn_rows(2, 5)

        @block.scalar
        def _(act):
            act.wait_ge(small_in, DMA * SMALL)
            act.activation(act_c[:], cond[:], ACT.Silu).then_inc(silu_done, 1)
            act.wait_ge(silu_done, 1)
            act.wait_ge(pad_zero, 1)
            act.activation(act_pad[:, :, 0:B], act_c[:], ACT.Copy).then_inc(pad_done, 1)
            act.wait_ge(var_done, 1)
            act.wait_ge(eps_set, 1)
            act.activation(rstd[:], mv[:, :, 1], ACT.Sqrt, bias=epst[:, 0:1]).then_inc(sqrt_done, 1)
            for n, a in enumerate((1, 0)):
                for b in range(B):
                    act.wait_ge(k_done, n * B + b + 1)
                    for m in range(KT):
                        ins = act.activation(kf[:, a, b, m], ps[:, 1 + b, m * S:(m + 1) * S], ACT.Identity,
                                             bias=kbias[:, a, m:m + 1])
                    ins.then_inc(k_out, 1)

        @block.vector
        def _(dve):
            dve.memset(act_pad[:], 0.0).then_inc(pad_zero, 1)
            dve.memset(epst[:], 1e-5).then_inc(eps_set, 1)
            dve.wait_ge(small_in, DMA * SMALL)
            steps = 0
            for b in range(B):
                ins = dve.bn_stats(stats[:, b], ctx_tok[:, b])
            ins.then_inc(dve_step, 1)
            dve.wait_ge(dve_step, 1)
            for b in range(B):
                ins = dve.bn_aggr(mv[:, b], stats[:, b])
            ins.then_inc(var_done, 1)
            dve.wait_ge(turned, 1)
            dve.tensor_copy(ctxT[:, 1], ps[:, 5:7, 0:KT * S].rearrange("p b (t s) -> p b t s", t=KT)).then_inc(ctx_out, 1)
            dve.wait_ge(sqrt_done, 1)
            dve.reciprocal(rstd[:], rstd[:]).then_inc(dve_step, 1)
            dve.wait_ge(dve_step, 2)
            for b in range(B):
                dve.tensor_scalar(ctx_n[:, b], ctx_tok[:, b], mv[:, b, 0:1], rstd[:, b:b + 1],
                                  ALU.subtract, ALU.mult).then_inc(norm_done, 1)

            def rows_to_sbuf(group, bank):
                used = len(GROUPS_OF_MODS[group][1]) * DH
                dve.wait_ge(rows_done, group + 1)
                dve.tensor_copy(rows[0:used, group], ps[0:used, bank, :]).then_inc(rows_out, 1)

            def add_bias(group, bank):
                first, chunks = GROUPS_OF_MODS[group]
                n = len(chunks)
                dve.wait_ge(mods_done, group + 1)
                for t in range(KT):
                    by_chunk = lambda ap: ap[:, first * KT:(first + n) * KT].rearrange("p (x t) b -> p t x b", t=KT)[:, t]
                    ins = dve.tensor_tensor(by_chunk(mod), ps[:, bank, t * P:t * P + n * DH].rearrange("p (x r) -> p x r", r=DH)[:, :, 0:B],
                                            by_chunk(bias[:].unsqueeze(2).to_broadcast([P, 2 * NS + NA, B])), ALU.add)
                ins.then_inc(mod_out, 1)

            rows_to_sbuf(0, 0)
            add_bias(0, 7)
            dve.wait_ge(mod_out, 1)
            for o in (0, NS):
                ins = dve.tensor_scalar(mod[:, o:o + KT], mod[:, o:o + KT], 1.0, None, ALU.add)
            ins.then_inc(dve_step, 1)
            dve.wait_ge(dve_step, 3)
            dve.wait_ge(turned, 2)
            for b in range(B):
                for t in range(KT):
                    ins = dve.tensor_scalar(ctxT[:, 0, b, t], ps[:, 3 + b, t * S:(t + 1) * S],
                                            mod[:, NS + t, b:b + 1], mod[:, NS + KT + t, b:b + 1], ALU.mult, ALU.add)
                ins.then_inc(ctx_out, 1)
            for n, a in enumerate((1, 0)):
                for b in range(B):
                    dve.wait_ge(v_done, n * B + b + 1)
                    dve.tensor_tensor(vf[:, a, b], ps[0:S, 6 + b, :], vbias[:, a], ALU.add).then_inc(v_out, 1)
            dve.wait_ge(k_out, 2 * B)
            dve.tensor_copy(khi[:], kf[:]).then_inc(split, 1)
            dve.wait_ge(split, 1)
            dve.tensor_tensor(klo[:].rearrange("p a b t s -> p (a b t s)"), kf[:].rearrange("p a b t s -> p (a b t s)"),
                              khi[:].bitcast(F32).rearrange("p a b t s -> p (a b t s)"), ALU.subtract).then_inc(split, 1)
            rows_to_sbuf(1, 0)
            rows_to_sbuf(2, 3)
            add_bias(1, 4)
            add_bias(2, 5)
            dve.wait_ge(mod_out, 3)
            for o in (KT, 4 * KT):
                dve.tensor_scalar(mod[:, 2 * NS + o:2 * NS + o + KT], mod[:, 2 * NS + o:2 * NS + o + KT], 1.0, None, ALU.add)
            dve.wait_ge(rows_out, 3)
            for g, row in enumerate((2 * DH, DH)):
                dve.tensor_tensor(gate_row[row:row + B, g], rows[row:row + B, 1 + g], gbias[row:row + B, g], ALU.add).then_inc(g_out, 1)


def chunk_pass(nc, d, name, x_in, x_out, o_in, b_out, gate, eps, scale, shift, projections, values, raw, plain=None,
               prefetch=None):
    NM = sum(KT for _ in projections)
    TILES = NM + (TT if values else 0)
    RING = 4
    OS = 2 if plain is not None else 1

    def turned_after(t):
        each = 1 if TILES >= 2 * KT else 2
        return [x for x in range(KT) if TILES - 1 - (KT - 1 - x) // each == t]

    XC = 2 if gate is None else 0
    with nc.cleanup_on_exit(), ExitStack() as ctx:
        sb = lambda n, s, t=F32: ctx.enter_context(nc.sbuf_tensor(f"{name}_{n}", s, t))
        sem = lambda n: nc.alloc_semaphore(f"{name}_{n}")
        po = ctx.enter_context(nc.psum_tensor(name + "_po", [P, 2, W], F32))
        pt = ctx.enter_context(nc.psum_tensor(name + "_pt", [P, 2, W], F32))
        pp = ctx.enter_context(nc.psum_tensor(name + "_pp", [P, RING, W], F32))
        ident = sb("ident", [P, P])
        NWT = raw.raw.shape[1]
        w_part_hi = sb("w", [P, NWT, KT, C], F32R)
        wparts = lambda k, part: raw.lo[:, k] if part else w_part_hi[:, k]
        x = sb("x", [P, 2, TT, C])
        xn = sb("xn", [P, TT, C])
        u = sb("u", [P, KT, W])
        us = sb("us", [P, 2, 2, KT, W], F32R)
        stats = sb("stats", [P, TT, 6])
        mv = sb("mv", [P, TT, 2])
        rstd = sb("rstd", [P, TT])
        epst = sb("epst", [P, 1])
        if o_in is not None:
            o = sb("o", [P, KT, W])
            os_ = sb("os", [P, OS, 2, KT, W], F32R)
            orow = sb("orow", [P, C])
            brow = sb("brow", [P, B, C])
        if gate is not None:
            grow = sb("grow", [P, B, C])
            gated = sb("gated", [P, 2, C])
        if projections:
            out = sb("out", [P, RING, 2, W], F32R)
            pbias = sb("pbias", [P, NM])
        if values:
            vout = sb("vout", [P, 2, C])
            vrow = sb("vrow", [P, C])
        small_in, prefetched = sem("small_in"), sem("prefetched")
        w_hi, w_lo, rows_ready, rows_done = sem("w_hi"), sem("w_lo"), sem("rows_ready"), sem("rows_done")
        x_in_s, o_loaded = [sem("x_in0"), sem("x_in1")], sem("o_in")
        x_stored = [sem("x_stored0"), sem("x_stored1")]
        biased, o_hi, o_lo, oproj_done = sem("biased"), sem("o_hi"), sem("o_lo"), sem("oproj_done")
        gated_done, x_ready = sem("gated_done"), sem("x_ready")
        stats_done, var_done, std_done, rstd_done, xn_done = (sem(n) for n in (
            "stats_done", "var_done", "std_done", "rstd_done", "xn_done"))
        turned, u_done, u_lo = sem("turned"), sem("u_done"), sem("u_lo")
        proj_done, proj_hi, proj_out = sem("proj_done"), sem("proj_hi"), sem("proj_out")
        out_stored = [sem(f"out_stored{r}") for r in range(RING)]
        v_stored = [sem("v_stored0"), sem("v_stored1")]
        passed, aggregating = sem("passed"), sem("aggregating")
        u_stored = [sem("u_stored0"), sem("u_stored1")]
        block = ctx.enter_context(nc.Block())
        small = [(ident[:], d["ident"])]
        if o_in is not None:
            small.append((orow[:], b_out.partition_broadcast(P)))
        if gate is not None:
            small += [(grow[:, b], gate[b].partition_broadcast(P)) for b in range(B)]
        if values:
            small.append((vrow[:], values[0].partition_broadcast(P)))
        m = 0
        for bias, _ in projections:
            small.append((pbias[:, m:m + KT], column(bias)))
            m += KT
        N = CHUNKS * B

        @block.sync
        def _(sp):
            def load_small():
                with nc.allow_non_contiguous_dma(reason="short vectors, once"):
                    for dst, src in small:
                        sp.dma_start(dst, src).then_inc(small_in, DMA)

            def load_x(i, b, first=False):
                if not first:
                    sp.wait_ge(xn_done, (2 * (i - 1) + b + 1) * TT)
                    if x_out is not None:
                        sp.sem_inc(passed, 1)
                        sp.wait_ge(x_stored[b], DMA * i)
                    sp.sem_inc(passed, 1)
                sp.dma_start(x[:, b], x_in[b, bass.ds(i * W, W), :].rearrange("(t p) c -> p t c", p=P)).then_inc(x_in_s[b], DMA)

            def load_o(i, b):
                sp.wait_ge(o_lo, 2 * i + b + 1)
                sp.sem_inc(passed, 1)
                sp.dma_start(o[:], o_in[b, :, bass.ds(i * W, W)].rearrange("(t p) w -> p t w", p=P)).then_inc(o_loaded, DMA)

            def store_x(i, b):
                sp.wait_ge(x_ready, (2 * i + b + 1) * TT + XC)
                sp.sem_inc(passed, 1)
                sp.dma_start(x_out[b, bass.ds(i * W, W), :].rearrange("(t p) c -> p t c", p=P), x[:, b]).then_inc(x_stored[b], DMA)

            def store_outputs(i, b):
                for t in range(TILES):
                    sp.wait_ge(proj_out, (2 * i + b) * TILES + t + 1 + RING)
                    sp.sem_inc(passed, 1)
                    if t < NM:
                        dst = projections[t // KT][1]
                        sp.dma_start(dst[:, b, t % KT * P:(t % KT + 1) * P, bass.ds(i * W, W)].rearrange("s p w -> p s w"),
                                     out[:, t % RING].bitcast(F32)).then_inc(out_stored[t % RING], DMA)
                    else:
                        sp.dma_start(values[1][b, bass.ds(i * W + (t - NM) * P, P)], vout[:, t % 2]).then_inc(v_stored[t % 2], DMA)
                if plain is not None:
                    sp.wait_ge(u_lo, 2 * i + b + 2)
                    sp.sem_inc(passed, 1)
                    sp.dma_start(plain[0, b, :, bass.ds(i * W, W)].rearrange("(t p) w -> p t w", p=P), us[:, b, 0].bitcast(F32)).then_inc(u_stored[b], DMA)
                    sp.dma_start(plain[1, b, :, bass.ds(i * W, W)].rearrange("(t p) w -> p t w", p=P), us[:, b, 1].bitcast(F32)).then_inc(u_stored[b], DMA)

            def superstep(i, b, left):
                if left > 2:
                    if o_in is not None and plain is None:
                        load_o(i + 1, b)
                    load_x(i + 1, b)
                if left > 1 and x_out is not None:
                    store_x(*chunk_after(i, b))
                if plain is not None and left > 3:
                    load_o(*chunk_after(i + 1, b))
                if prefetch is not None:
                    dst, src = prefetch[b]
                    n = dst.shape[1] // CHUNKS
                    src = channels(src)[:, bass.ds(i * n, n), :]
                    sp.dma_start(dst[:, bass.ds(i * n, n), :], src).then_inc(prefetched, DMA)
                store_outputs(i, b)

            for s in (out_stored if projections else []) + (v_stored if values else []):
                sp.sem_inc(s, DMA)
            for s in u_stored if plain is not None else []:
                sp.sem_inc(s, 2 * DMA)
            if o_in is not None:
                load_o(0, 0)
            load_x(0, 0, True)
            load_small()
            load_x(0, 1, True)
            if o_in is not None:
                load_o(0, 1)
                store_x(0, 0)
                if plain is not None:
                    load_o(1, 0)
            with sp.Fori(0, CHUNKS - 2) as i:
                for b in range(B):
                    superstep(i, b, 4)
            for n in range(N - 2 * B, N):
                superstep(n // B, n % B, N - n)
            if prefetch is not None:
                sp.wait_ge(prefetched, DMA * N)
            for b in range(2):
                if x_out is not None:
                    sp.wait_ge(x_stored[b], DMA * CHUNKS)
                if values:
                    sp.wait_ge(v_stored[b], DMA * (N * TT // 2 + 1))
                if plain is not None:
                    sp.wait_ge(u_stored[b], 2 * DMA * (CHUNKS + 1))
            if projections:
                for r in range(RING):
                    sp.wait_ge(out_stored[r], DMA * (N * NM // RING + 1))

        @block.tensor
        def _(pe):
            def split_matmul(out_ap, lhs, rhs):
                for t in range(KT):
                    for q, (pm, pw) in enumerate(PARTS):
                        mm = pe.matmul(out_ap, lhs(pw, t), rhs(pm, t), start=(t == 0 and q == 0),
                                       stop=(t == KT - 1 and q == 2))
                return mm

            def output_projection(i, b):
                n = 2 * i + b
                pe.wait_ge(o_lo, n + 2)
                for tt in range(TT):
                    pe.wait_ge(x_ready, n * TT + tt + 1) if gate is None else pe.wait_ge(gated_done, n * TT + tt + 1)
                    split_matmul(po[:, tt % 2], lambda s, t: os_[:, b % OS, s, t, tt * P:(tt + 1) * P],
                                 lambda s, t: wparts(0, s)[:, t]).then_inc(oproj_done, 1)

            def turn(i, b, tiles=range(KT)):
                n = 2 * i + b
                for t in tiles:
                    pe.wait_ge(u_done, n * KT + t + 1)
                    for tt in range(TT):
                        if t == 0:
                            pe.wait_ge(xn_done, n * TT + tt + 1)
                        mm = pe.transpose(pt[:, t % 2, tt * P:(tt + 1) * P], xn[:, tt, t * P:(t + 1) * P], ident[:])
                    mm.then_inc(turned, 1)

            def project(i, b, next_chunk=None):
                n = 2 * i + b
                pe.wait_ge(u_lo, n + 2)
                for t in range(TILES):
                    pe.wait_ge(proj_out, n * TILES + t + 1)
                    w = NWT - len(projections) - (1 if values else 0) + t // KT
                    if t < NM:
                        mm = split_matmul(pp[:, t % RING], lambda s, k: wparts(w, s)[:, k, t % KT * P:(t % KT + 1) * P],
                                          lambda s, k: us[:, b, s, k])
                    else:
                        mm = split_matmul(pp[:, t % RING], lambda s, k: us[:, b, s, k, (t - NM) * P:(t - NM + 1) * P],
                                          lambda s, k: wparts(w, s)[:, k])
                    mm.then_inc(proj_done, 1)
                    if next_chunk is not None:
                        turn(*next_chunk, turned_after(t))

            def superstep(i, b, left):
                if left > 1 and o_in is not None:
                    output_projection(*chunk_after(i, b))
                if plain is not None:
                    turn(i, b)
                if left > 1 and o_in is None:
                    turn(*chunk_after(i, b))
                if TILES:
                    project(i, b, chunk_after(i, b) if left > 1 and o_in is not None else None)

            pe.wait_ge(small_in, DMA * len(small))
            if NWT:
                pe.wait_ge(w_lo, NWT if o_in is None else 1)
            if o_in is not None:
                output_projection(0, 0)
            if plain is None:
                turn(0, 0)
            if NWT:
                pe.wait_ge(w_lo, NWT)
            with pe.Fori(0, CHUNKS - 1) as i:
                for b in range(B):
                    superstep(i, b, 3)
            for b in range(B):
                superstep(CHUNKS - 1, b, B - b)

        @block.scalar
        def _(act):
            def split_o(i, b):
                n = 2 * i + b
                act.wait_ge(o_loaded, DMA * (n + 1))
                if not isinstance(n, int) or n >= OS:
                    act.wait_ge(x_ready if gate is None else gated_done, (n - OS + 1) * TT + 2)
                act.activation(os_[:, b % OS, 0], o[:], ACT.Copy).then_inc(o_hi, 1)

            def std(i, b):
                act.wait_ge(var_done, 2 * i + b + 1)
                act.activation(rstd[:], mv[:, :, 1], ACT.Sqrt, bias=epst[:, 0:1]).then_inc(std_done, 1)

            def modulate(i, b, tiles=range(KT)):
                n = 2 * i + b
                for t in tiles:
                    act.wait_ge(turned, n * KT + t + 1)
                    if t == 0:
                        act.wait_ge(u_lo, n + 1)
                        if plain is not None:
                            act.wait_ge(u_stored[b], 2 * DMA * (i + 1))
                    act.activation(us[:, b, 0, t], pt[:, t % 2], ACT.Identity, bias=shift(b, t), scale=scale(b, t))
                    act.activation(u[:, t], pt[:, t % 2], ACT.Identity, bias=shift(b, t), scale=scale(b, t)).then_inc(u_done, 1)

            def evacuate(i, b, next_chunk=None):
                n = 2 * i + b
                for t in range(TILES):
                    if t >= NM:
                        if next_chunk is not None:
                            modulate(*next_chunk, turned_after(t))
                        continue
                    act.wait_ge(proj_done, n * TILES + t + 1)
                    act.wait_ge(out_stored[t % RING], DMA * (n * (NM // RING) + t // RING + 1))
                    act.activation(out[:, t % RING, 0], pp[:, t % RING], ACT.Identity, bias=pbias[:, t:t + 1]).then_inc(proj_hi, 1)
                    if next_chunk is not None:
                        modulate(*next_chunk, turned_after(t))

            def superstep(i, b, left):
                if plain is not None:
                    if left > 2:
                        split_o(i + 1, b)
                    modulate(i, b)
                if o_in is None and left > 1:
                    modulate(*chunk_after(i, b))
                if o_in is not None and left > 1:
                    std(*chunk_after(i, b))
                    if plain is None and left > 2:
                        split_o(i + 1, b)
                if o_in is None and left > 2:
                    std(i + 1, b)
                evacuate(i, b, chunk_after(i, b) if left > 1 and o_in is not None else None)

            act.sem_inc(u_done, 2)
            act.wait_ge(rows_ready, 1)
            for k in range(NWT):
                if k == 1 and o_in is not None:
                    split_o(0, 0)
                act.activation(w_part_hi[:, k], raw.raw[:, k], ACT.Copy).then_inc(w_hi, 1)
            if NWT == 1 and o_in is not None:
                split_o(0, 0)
            std(0, 0)
            if plain is None:
                modulate(0, 0)
            if o_in is not None:
                split_o(0, 1)
            else:
                std(0, 1)
            with act.Fori(0, CHUNKS - 1) as i:
                for b in range(B):
                    superstep(i, b, 3)
            for b in range(B):
                superstep(CHUNKS - 1, b, B - b)

        @block.vector
        def _(dve):
            def split_o(i, b):
                n = 2 * i + b
                dve.wait_ge(o_hi, n + 1)
                dve.tensor_tensor(os_[:, b % OS, 1], o[:], os_[:, b % OS, 0].bitcast(F32), ALU.subtract).then_inc(o_lo, 1)

            def normalise(i, b, first=False):
                n = 2 * i + b
                dve.wait_ge(x_in_s[b], DMA * (i + 1))
                for tt in range(TT):
                    if o_in is not None:
                        dve.wait_ge(oproj_done, n * TT + tt + 1)
                        dve.wait_ge(biased, n + 1)
                        if gate is not None:
                            dve.tensor_tensor(gated[:, tt % 2], po[:, tt % 2], grow[:, b], ALU.mult).then_inc(gated_done, 1)
                            dve.wait_ge(gated_done, n * TT + tt + 3)
                            dve.tensor_tensor(x[:, b, tt], x[:, b, tt], gated[:, tt % 2], ALU.add).then_inc(x_ready, 1)
                            dve.wait_ge(x_ready, n * TT + tt + 1)
                        else:
                            dve.tensor_tensor(x[:, b, tt], po[:, tt % 2], x[:, b, tt], ALU.add).then_inc(x_ready, 1)
                            dve.wait_ge(x_ready, n * TT + tt + 3)
                    dve.bn_stats(stats[:, tt], x[:, b, tt]).then_inc(stats_done, 1)
                dve.wait_ge(stats_done, (n + 1) * TT)
                dve.sem_inc(aggregating, 1)
                for tt in range(TT):
                    ins = dve.bn_aggr(mv[:, tt], stats[:, tt])
                ins.then_inc(var_done, 1)
                dve.wait_ge(std_done, n + 1)
                dve.reciprocal(rstd[:], rstd[:]).then_inc(rstd_done, 1)
                dve.wait_ge(rstd_done, n + 1)
                if not first:
                    dve.wait_ge(turned, n * KT)
                for tt in range(TT):
                    dve.tensor_scalar(xn[:, tt], x[:, b, tt], mv[:, tt, 0:1], rstd[:, tt:tt + 1],
                                      ALU.subtract, ALU.mult).then_inc(xn_done, 1)

            def evacuate(i, b, next_chunk=None):
                n = 2 * i + b
                for t in range(TILES):
                    if t < NM:
                        dve.wait_ge(proj_hi, n * NM + t + 1)
                        dve.scalar_tensor_tensor(out=out[:, t % RING, 1], in0=pp[:, t % RING], scalar=pbias[:, t:t + 1],
                                                 in1=out[:, t % RING, 0].bitcast(F32), op0=ALU.add, op1=ALU.subtract).then_inc(proj_out, 1)
                    else:
                        dve.wait_ge(proj_done, n * TILES + t + 1)
                        dve.wait_ge(v_stored[t % 2], DMA * (n * (TT // 2) + (t - NM) // 2 + 1))
                        dve.tensor_tensor(vout[:, t % 2], pp[:, t % RING], vrow[:], ALU.add).then_inc(proj_out, 1)
                    if next_chunk is not None:
                        split_u(*next_chunk, turned_after(t))

            def split_u(i, b, tiles=range(KT)):
                n = 2 * i + b
                for t in tiles:
                    dve.wait_ge(u_done, n * KT + t + 3)
                    ins = dve.tensor_tensor(us[:, b, 1, t], u[:, t], us[:, b, 0, t].bitcast(F32), ALU.subtract)
                    if t == KT - 1:
                        ins.then_inc(u_lo, 1)

            def superstep(i, b, left):
                if plain is not None and left > 2:
                    split_o(i + 1, b)
                if o_in is None and left > 1:
                    split_u(*chunk_after(i, b))
                if o_in is not None and left > 1:
                    normalise(*chunk_after(i, b))
                    if plain is None and left > 2:
                        split_o(i + 1, b)
                if o_in is None and left > 2:
                    normalise(i + 1, b)
                evacuate(i, b, chunk_after(i, b) if left > 1 and o_in is not None else None)
                if plain is not None:
                    split_u(i, b)

            dve.memset(epst[:], eps).then_inc(rows_ready, 1)
            dve.sem_inc(proj_out, RING)
            dve.sem_inc(u_lo, 1)
            if o_in is not None:
                dve.sem_inc(o_lo, 1)
                dve.sem_inc(gated_done if gate is not None else x_ready, 2)
            for k in range(NWT):
                if k == 1 and o_in is not None:
                    split_o(0, 0)
                dve.wait_ge(w_hi, k + 1)
                dve.tensor_tensor(raw.lo[:, k], raw.raw[:, k], w_part_hi[:, k].bitcast(F32), ALU.subtract).then_inc(w_lo, 1)
            if NWT == 1 and o_in is not None:
                split_o(0, 0)
            normalise(0, 0, True)
            if plain is None:
                split_u(0, 0)
            if o_in is not None:
                split_o(0, 1)
            else:
                normalise(0, 1)
            with dve.Fori(0, CHUNKS - 1) as i:
                for b in range(B):
                    superstep(i, b, 3)
            for b in range(B):
                superstep(CHUNKS - 1, b, B - b)

        if o_in is not None:
            @block.gpsimd
            def _(pool):
                pool.wait_ge(small_in, DMA * len(small))
                if gate is not None:
                    for b in range(B):
                        ins = pool.tensor_tensor(brow[:, b], orow[:], grow[:, b], ALU.mult)
                    ins.then_inc(rows_done, 1)
                    pool.wait_ge(rows_done, 1)

                def add_bias(i, b):
                    row = orow[:] if gate is None else brow[:, b]
                    pool.wait_ge(x_in_s[b], DMA * (i + 1))
                    pool.tensor_tensor(x[:, b], x[:, b], row.unsqueeze(1).to_broadcast([P, TT, C]), ALU.add).then_inc(biased, 1)

                with pool.Fori(0, CHUNKS) as i:
                    for b in range(B):
                        add_bias(i, b)


def attention(nc, d, name, q_in, k_in, v_in, o_out, keys, preload):
    NKT = -(-keys // P)
    KR = keys // NKT
    KC = -(-keys // W)
    KW = keys // KC
    KE = KW + KW % 2
    if KC > 1:
        UNITS = [(h, [qt], kc) for h in range(GH) for qt in range(TT) for kc in range(KC)]
    else:
        UNITS = [(h, list(range(TT)), 0) for h in range(GH)]
    U = len(UNITS)
    QR = 4
    ER = 4
    POOLED = [t for t in range(NKT - 2) if t % 3 != 2] if NKT > 2 else []
    ADDS = max(len(POOLED) - 1, 0)
    STEPS = B * GROUPS * CHUNKS
    BODY = 2 * CHUNKS
    TURN_KT = max(NKT - 3, 0)
    TURN = GH * (TURN_KT + 1)
    HEAD = 14 if NKT > 1 else U
    TILES = GH * NKT + 1
    RING = 3
    LATE = 1 if NKT > 1 else 2
    DIVIDE_AT = range(6, 14, 2) if NKT > 1 else range(4)
    SETUP = 2 + KW % 2
    with nc.cleanup_on_exit(), ExitStack() as ctx:
        sb = lambda n, s, t=F32: ctx.enter_context(nc.sbuf_tensor(f"{name}_{n}", s, t))
        sem = lambda n: nc.alloc_semaphore(f"{name}_{n}")
        sm = ctx.enter_context(nc.psum_tensor(name + "_sm", [P, RING, W], F32))
        st = ctx.enter_context(nc.psum_tensor(name + "_st", [P, RING, W], F32))
        acc = ctx.enter_context(nc.psum_tensor(name + "_acc", [P, 2, W], F32))
        ident = sb("ident", [P, P])
        mask = sb("mask", [P, GH])
        ones = sb("ones", [P, DH])
        q = sb("q", [P, QR, GH, W], F32R)
        k = sb("k", [P, 2, GH, KC * KE], F32R)
        v = sb("v", [P, 2, NKT, P])
        e = sb("e", [P, ER, GH, W])
        if POOLED:
            esum = sb("esum", [P, GH, W])
        peak = sb("peak", [P, U])
        top = sb("top", [P, GH * TT])
        neg_hi = sb("neg_hi", [P, GH * TT], F32R)
        neg = sb("neg", [P, TT, P])
        rows = sb("rows", [P, 2, W])
        sums = sb("sums", [P, 2, 2, W])
        den_t = sb("den_t", [P, W])
        inv = sb("inv", [P, W // DH])
        inv_b = sb("inv_b", [P, W])
        inv_t = sb("inv_t", [P, 2, W])
        o = sb("o", [P, 2, W])
        small_in, set_up, act_set_up, pool_set_up = sem("small_in"), sem("set_up"), sem("act_set_up"), sem("pool_set_up")
        q_loaded = [sem(f"q_loaded{r}") for r in range(QR)]
        rows_ready = [sem(f"rows_ready{r}") for r in range(QR)]
        k_loaded, v_loaded = [sem("k_loaded0"), sem("k_loaded1")], [sem("v_loaded0"), sem("v_loaded1")]
        unit_done, unit_read = sem("unit_done"), sem("unit_read")
        top_done, neg_done, neg_ready = sem("top_done"), sem("neg_done"), sem("neg_ready")
        score_done, score_read, tile_used, e_added = sem("score_done"), sem("score_read"), sem("tile_used"), sem("e_added")
        divided, acc_read, scaled = sem("divided"), sem("acc_read"), sem("scaled")
        o_stored = [sem("o_stored0"), sem("o_stored1")]
        passed, preloaded = sem("passed"), sem("preloaded")
        block = ctx.enter_context(nc.Block())

        def exists(i, j):
            return not isinstance(i, int) or 0 <= BODY * i + j < STEPS

        def place(kt, h):
            return GH * kt + h + (GH * kt + h >= TURN)

        def number(i, j, p):
            return (BODY * i + j) * TILES + p + (p < TURN or exists(i, j + 1))

        def turned(i, j):
            return number(i, j - 1, TURN) if j else 0

        def bank_free(engine, i, j, p):
            near = p < 2 or (TURN < p <= TURN + RING and not exists(i, j + 1))
            engine.wait_ge(score_read, number(i, j, p) + near)

        def bank_of_unit(j, u):
            return (j % BODY + u) % RING

        def units_of_step(i, j):
            units = [(j + 1, u) for u in range(HEAD, U)] + [(j + 2, u) for u in range(HEAD)]
            return [(m, u) for m, u in units if exists(i, m)]

        def run(engine, step, first, late):
            for j in range(first):
                step(0, j)
            with engine.Fori(0, STEPS // BODY - 1) as i:
                for j in range(first, BODY + first):
                    step(i, j)
            for j in range(first, BODY + late):
                step(STEPS // BODY - 1, j)

        @block.sync
        def _(sp):
            for dst, src in ((ident[:], d["ident"]), (mask[:], d["mask"])):
                sp.dma_start(dst, src).then_inc(small_in, DMA)
            for s in o_stored:
                sp.sem_inc(s, DMA)

            def load_q(i, j):
                for row, part in enumerate((0, 0, 1)):
                    src = q_in[part].rearrange("b (g h r) t -> (b g) r h t", g=GROUPS, h=GH)
                    sp.dma_start(q[row * DH:(row + 1) * DH, j % QR].bitcast(F32),
                                 src[2 * i + j // CHUNKS, :, :, j % CHUNKS * W:(j % CHUNKS + 1) * W]
                                 ).then_inc(q_loaded[j % QR], DMA)

            def load_k(i, g):
                for row, part in enumerate((0, 1, 0)):
                    src = k_in[part].rearrange("b (g h r) t -> (b g) r h t", g=GROUPS, h=GH)
                    sp.dma_start(k[row * DH:(row + 1) * DH, g % 2, :, 0:keys].bitcast(F32),
                                 src[2 * i + g]).then_inc(k_loaded[g % 2], DMA)

            def load_v(i, g):
                sp.dma_start(v[0:KR, g % 2], v_in[(i + g // 2) // 2, :, bass.ds(((i + g // 2) % 2 * 2 + g % 2) * P, P)].rearrange("(t p) c -> p t c", p=KR)
                             ).then_inc(v_loaded[g % 2], DMA)

            def spread_rows(i, j):
                sp.wait_ge(score_read, turned(i, j) + 3)
                sp.dma_start(q[3 * DH:P, j % QR].bitcast(F32), rows[3 * DH:P, j % 2].unsqueeze(1).to_broadcast([DH, GH, W])
                             ).then_inc(rows_ready[j % QR], DMA)

            def store_o(i, j):
                sp.wait_ge(scaled, BODY * i + j + 3)
                sp.sem_inc(passed, 1)
                dst = o_out.rearrange("b (g p) t -> (b g) p t", p=P)
                sp.dma_start(dst[2 * i + j // CHUNKS, :, j % CHUNKS * W:(j % CHUNKS + 1) * W],
                             o[:, j % 2]).then_inc(o_stored[j % 2], DMA)

            def step(i, j):
                if exists(i, j - 1) and exists(i, j + QR - 1):
                    sp.wait_ge(score_done, (BODY * i + j) * TILES + 1)
                    sp.sem_inc(passed, 1)
                if exists(i, j + QR - 1):
                    load_q(i, j + QR - 1)
                if j % CHUNKS == 0 and exists(i, j + CHUNKS):
                    load_k(i, j // CHUNKS + 1)
                    if exists(i, j - 1):
                        sp.wait_ge(tile_used, (BODY * i + j) * NKT + ER)
                        sp.sem_inc(passed, 1)
                    load_v(i, j // CHUNKS + 1)
                if exists(i, j - LATE - 1):
                    store_o(i, j - LATE - 1)
                if exists(i, j + 1):
                    spread_rows(i, j + 1)
                if isinstance(i, int) and i > 0 and 0 <= j - (BODY - QR) < len(preload):
                    sp.dma_start(*preload[j - (BODY - QR)]).then_inc(preloaded, DMA)

            load_q(0, 0)
            load_k(0, 0)
            load_v(0, 0)
            for j in range(1, QR - 1):
                load_q(0, j)
            spread_rows(0, 0)
            run(sp, step, LATE + 1, LATE + 1)
            for s in o_stored:
                sp.wait_ge(s, DMA * (STEPS // 2 + 1))
            sp.wait_ge(preloaded, DMA * len(preload))

        @block.tensor
        def _(pe):
            def score_unit(i, j, u):
                n, g = BODY * i + j, j // CHUNKS
                h, tiles, kc = UNITS[u]
                if u == 0:
                    pe.wait_ge(q_loaded[j % QR], 3 * DMA * (BODY // QR * i + j // QR + 1))
                    if j % CHUNKS == 0:
                        pe.wait_ge(k_loaded[g % 2], 3 * DMA * (i + g // 2 + 1))
                pe.wait_ge(unit_read, n * U + u + (j % BODY == 0 and u < 2))
                for x, qt in enumerate(tiles):
                    mm = pe.matmul(sm[:, bank_of_unit(j, u), x * KE:(x + 1) * KE], q[0:3 * DH, j % QR, h, qt * P:(qt + 1) * P],
                                   k[0:3 * DH, g % 2, h, kc * KE:(kc + 1) * KE], start=True, stop=True)
                mm.then_inc(unit_done, 1)

            def turn_peaks(i, j):
                pe.wait_ge(neg_ready, 2 * (BODY * i + j + 1))
                if j:
                    bank_free(pe, i, j - 1, TURN)
                for qt in range(TT):
                    mm = pe.transpose(st[:, TURN % RING if j else 0, qt * P:(qt + 1) * P], neg[:, qt], ident[:])
                mm.then_inc(score_done, 1)

            def score_tile(i, j, kt, h):
                g = j // CHUNKS
                if kt == 0 and h == 0:
                    pe.wait_ge(rows_ready[j % QR], DMA * (BODY // QR * i + j // QR + 1))
                    if j % CHUNKS == 0:
                        pe.wait_ge(act_set_up, 1)
                        pe.wait_ge(pool_set_up, 1)
                bank_free(pe, i, j, place(kt, h))
                pe.matmul(st[0:KR, place(kt, h) % RING], k[:, g % 2, h, kt * P:kt * P + KR],
                          q[:, j % QR, h], start=True, stop=True).then_inc(score_done, 1)

            def weigh(i, j, kt):
                n, g = BODY * i + j, j // CHUNKS
                if kt == 0:
                    pe.wait_ge(acc_read, n + 1)
                    if j % CHUNKS == 0:
                        pe.wait_ge(v_loaded[g % 2], DMA * (i + g // 2 + 1))
                pe.wait_ge(score_read, number(i, j, place(kt, GH - 1)) + 3)
                for h in range(GH):
                    rows = slice(h * DH, (h + 1) * DH)
                    mm = pe.matmul(acc[rows, 0], v[0:KR, g % 2, kt, rows], e[0:KR, (j * NKT + kt) % ER, h],
                                   start=(kt == 0), stop=(kt == NKT - 1), tile_position=(0, h * DH))
                if kt in POOLED:
                    mm.then_inc(tile_used, 1)

            def add_up(i, j, kt):
                if kt in POOLED:
                    return
                first = min(t for t in range(NKT) if t not in POOLED)
                operands = [e[0:KR, (j * NKT + kt) % ER]]
                if POOLED and kt == NKT - 1:
                    pe.wait_ge(e_added, (BODY * i + j + 1) * ADDS)
                    operands.append(esum)
                for x, operand in enumerate(operands):
                    for h in range(GH):
                        mm = pe.matmul(acc[h * DH:(h + 1) * DH, 1], ones[0:KR], operand[:, h], start=(kt == first),
                                       stop=(kt == NKT - 1 and x == len(operands) - 1), tile_position=(0, h * DH))
                mm.then_inc(tile_used, 1)

            def step(i, j):
                turn = exists(i, j + 1)
                total = NKT * 8 + (NKT - len(POOLED) + (NKT > 1)) * 4
                units = units_of_step(i, j)
                given, weight = 0, 0
                for kt in range(NKT):
                    parts = [(1, score_tile, (i, j, kt, h)) for h in range(GH)] if exists(i, j) else []
                    w = (i, j, kt - 1) if kt else (i, j - 1, NKT - 1)
                    if exists(w[0], w[1]) and (kt == 0 or exists(i, j)):
                        products = [(4, weigh, w), ((w[2] not in POOLED) * (4 + 4 * (w[2] == NKT - 1 > 0)), add_up, w)]
                        parts = parts[:2] + products[:1] + parts[2:] + products[1:] if NKT > 1 else products + parts
                    if kt == TURN_KT and turn:
                        parts.append((0, turn_peaks, (i, j + 1)))
                    for part_weight, part, where in parts:
                        part(*where)
                        weight += part_weight
                        while given < len(units) and given * total <= (weight - 1) * U:
                            score_unit(i, *units[given])
                            given += 1
                for m, u in units[given:]:
                    score_unit(i, m, u)

            pe.sem_inc(tile_used, ER)
            pe.wait_ge(small_in, 2 * DMA)
            pe.wait_ge(set_up, SETUP)
            for u in range(U):
                score_unit(0, 0, u)
            turn_peaks(0, 0)
            for u in range(HEAD):
                score_unit(0, 1, u)
            run(pe, step, LATE, 1)

        @block.scalar
        def _(act):
            def take_rows(i, j):
                if exists(i, j - 2):
                    act.wait_ge(rows_ready[(j - 2) % QR], DMA * (BODY // QR * i + (j - 2) // QR + 1))
                act.wait_ge(score_done, turned(i, j) + 1)
                act.activation(rows[3 * DH:P, j % 2], st[3 * DH:P, TURN % RING if j else 0], ACT.Copy).then_inc(score_read, 1)

            def exponentials(i, j, kt):
                n = BODY * i + j
                act.wait_ge(tile_used, n * NKT + kt + 1)
                before = (kt - ER) % NKT
                if before in POOLED and (kt >= ER or exists(i, j - 1)):
                    act.wait_ge(e_added, (n - (kt < ER)) * ADDS + max(POOLED.index(before), 1))
                for h in range(GH):
                    act.wait_ge(score_done, number(i, j, place(kt, h)) + 1)
                    act.activation(e[0:KR, (j * NKT + kt) % ER, h], st[0:KR, place(kt, h) % RING], ACT.Exp,
                                   scale=SCALE).then_inc(score_read, 1)

            def fetch_sums(i, j):
                n = BODY * i + j
                act.wait_ge(tile_used, (n + 1) * NKT + ER)
                act.wait_ge(scaled, n + 1)
                act.activation(sums[:, j % 2], acc[:], ACT.Copy).then_inc(acc_read, 1)

            def step(i, j):
                if NKT == 1 and exists(i, j - 1):
                    fetch_sums(i, j - 1)
                for kt in range(NKT):
                    if exists(i, j):
                        exponentials(i, j, kt)
                    if NKT > 1 and kt == 0 and exists(i, j - 1):
                        fetch_sums(i, j - 1)
                    if kt == TURN_KT and exists(i, j + 1):
                        take_rows(i, j + 1)

            act.sem_inc(score_read, 2)
            act.sem_inc(acc_read, 1)
            act.wait_ge(small_in, 2 * DMA)
            act.activation(k[3 * DH:P, 0], mask[3 * DH:P].unsqueeze(2).to_broadcast([DH, GH, KC * KE]), ACT.Copy).then_inc(act_set_up, 1)
            take_rows(0, 0)
            run(act, step, LATE, 1)

        @block.vector
        def _(dve):
            def peak_of_unit(i, j, u):
                h, tiles, _ = UNITS[u]
                if u == 0 and exists(i, j - 1):
                    dve.wait_ge(neg_ready, 2 * (BODY * i + j))
                dve.wait_ge(unit_done, (BODY * i + j) * U + u + 1)
                src = sm[:, bank_of_unit(j, u), 0:len(tiles) * KE].rearrange("p (x k) -> p x k", k=KE)[:, :, 0:KW]
                dst = peak[:, u:u + 1] if KC > 1 else top[:, h * TT:(h + 1) * TT]
                dve.tensor_reduce(dst, src, AX.X, ALU.max).then_inc(unit_read, 1)

            def minus_peaks(i, j):
                n = BODY * i + j
                dve.wait_ge(unit_read, (n + 1) * U + 2)
                if KC > 1:
                    dve.tensor_reduce(top[:], peak[:].rearrange("p (x c) -> p x c", c=KC), AX.X, ALU.max).then_inc(top_done, 1)
                    dve.wait_ge(top_done, n + 1)
                dve.tensor_scalar(neg_hi[:], top[:], -1.0, None, ALU.mult).then_inc(neg_done, 1)
                dve.wait_ge(neg_done, n + 1)
                if exists(i, j - 1):
                    dve.wait_ge(score_done, turned(i, j - 1) + 1)
                by_head = lambda ap: ap.rearrange("p (h t) -> p h t", t=TT)
                parts = neg[:, :, 3 * DH:3 * DH + 2 * GH].rearrange("p t (h s) -> p h t s", s=2)
                dve.tensor_copy(parts[:, :, :, 0], by_head(neg_hi[:].bitcast(F32))).then_inc(neg_ready, 1)
                dve.scalar_tensor_tensor(out=parts[:, :, :, 1], in0=by_head(top[:]), scalar=-1.0, in1=by_head(neg_hi[:].bitcast(F32)),
                                         op0=ALU.mult, op1=ALU.subtract).then_inc(neg_ready, 1)

            def divide(i, j, part):
                n = BODY * i + j
                if part == 0:
                    dve.wait_ge(acc_read, n + 2)
                    ins = dve.transpose(den_t[:], sums[:, j % 2, 1])
                else:
                    dve.wait_ge(divided, 4 * n + part)
                if part == 1:
                    ins = dve.reciprocal(inv[:], den_t[:].rearrange("p (c r) -> p c r", r=DH)[:, :, 0])
                if part == 2:
                    ins = dve.tensor_copy(inv_b[:].rearrange("p (c r) -> p c r", r=DH), inv[:].unsqueeze(2).to_broadcast([P, W // DH, DH]))
                if part == 3:
                    dve.wait_ge(scaled, n + 1)
                    ins = dve.transpose(inv_t[:, j % 2], inv_b[:])
                ins.then_inc(divided, 1)

            def step(i, j):
                units = units_of_step(i, j)
                for x in range(U):
                    if x < len(units):
                        m, u = units[x]
                        peak_of_unit(i, m, u)
                        if u == U - 1:
                            minus_peaks(i, m)
                    if x in DIVIDE_AT and exists(i, j - LATE):
                        divide(i, j - LATE, DIVIDE_AT.index(x))

            dve.sem_inc(unit_read, 2)
            dve.memset(ones[:], 1.0).then_inc(set_up, 1)
            dve.memset(neg[:], 0.0).then_inc(set_up, 1)
            if KE > KW:
                dve.memset(k[0:3 * DH, :, :, keys:].bitcast(F32), 0.0).then_inc(set_up, 1)
            dve.wait_ge(set_up, SETUP)
            for m, u in [(0, u) for u in range(U)] + [(1, u) for u in range(HEAD)]:
                peak_of_unit(0, m, u)
                if u == U - 1:
                    minus_peaks(0, m)
            run(dve, step, LATE, LATE)

        @block.gpsimd
        def _(pool):
            def add(i, j, x):
                n, slot = BODY * i + j, lambda x: (j * NKT + POOLED[x]) % ER
                pool.wait_ge(score_read, number(i, j, place(POOLED[x], GH - 1)) + 3)
                if x > 1:
                    pool.wait_ge(e_added, n * ADDS + x - 1)
                elif exists(i, j - 1):
                    pool.wait_ge(tile_used, n * NKT + ER)
                pool.tensor_tensor(esum[:], e[:, slot(0)] if x == 1 else esum[:], e[:, slot(x)], ALU.add).then_inc(e_added, 1)

            def scale(i, j):
                n = BODY * i + j
                pool.wait_ge(o_stored[j % 2], DMA * (BODY // 2 * i + j // 2 + 1))
                pool.wait_ge(divided, 4 * (n + 1))
                pool.tensor_tensor(o[:, j % 2], sums[:, j % 2, 0], inv_t[:, j % 2], ALU.mult).then_inc(scaled, 1)

            def step(i, j):
                if POOLED and exists(i, j):
                    for x in range(1, 3):
                        add(i, j, x)
                if exists(i, j - LATE):
                    scale(i, j - LATE)
                if POOLED and exists(i, j):
                    for x in range(3, len(POOLED)):
                        add(i, j, x)

            pool.sem_inc(scaled, 2)
            pool.wait_ge(small_in, 2 * DMA)
            pool.tensor_copy(k[3 * DH:P, 1], mask[3 * DH:P].unsqueeze(2).to_broadcast([DH, GH, KC * KE])).then_inc(pool_set_up, 1)
            run(pool, step, LATE, LATE)


def mlp(nc, d, u_in, x_in, gate, raw1, raw2, out):
    with nc.cleanup_on_exit(), ExitStack() as ctx:
        sb = lambda n, s, t=F32: ctx.enter_context(nc.sbuf_tensor("mlp_" + n, s, t))
        sem = lambda n: nc.alloc_semaphore("mlp_" + n)
        ph = ctx.enter_context(nc.psum_tensor("mlp_ph", [P, 4, W], F32))
        py = ctx.enter_context(nc.psum_tensor("mlp_py", [P, TT, W], F32))
        w1_hi = sb("w1_hi", [P, KT, HID], F32R)
        w2_hi = sb("w2_hi", [P, HT, C], F32R)
        w1, w2 = (w1_hi, raw1.lo), (w2_hi, raw2.lo)
        us = sb("us", [P, 2, 2, KT, W], F32R)
        x = sb("x", [P, TT, C])
        gelu = sb("gelu", [P, 2, W])
        gated = sb("gated", [P, 2, W])
        gs = sb("gs", [P, 2, 2, W], F32R)
        grow = sb("grow", [P, B, C])
        brow = sb("brow", [P, B, C])
        b1 = sb("b1", [P, HT])
        small_in = sem("small_in")
        w_hi, w_lo, rows_done = sem("w_hi"), sem("w_lo"), sem("rows_done")
        u_loaded, x_loaded, biased = [sem("u_loaded0"), sem("u_loaded1")], sem("x_loaded"), sem("biased")
        hidden_done, gelu_done, g_hi, g_lo, used = sem("hidden_done"), sem("gelu_done"), sem("g_hi"), sem("g_lo"), sem("used")
        y_read, x_ready, stored = sem("y_read"), sem("x_ready"), sem("stored")
        passed = sem("passed")
        block = ctx.enter_context(nc.Block())
        pieces = [[t[:, c] for t in (w1_hi, raw1.lo, raw1.raw)] for c in range(KT)] + \
                 [[t[:, c * KT:(c + 1) * KT] for t in (w2_hi, raw2.lo, raw2.raw)] for c in range(HT // KT)]
        NP = len(pieces)
        SMALL = 1 + 2 * B

        @block.sync
        def _(sp):
            sp.sem_inc(stored, DMA)

            def load_small():
                with nc.allow_non_contiguous_dma(reason="a short vector, once"):
                    sp.dma_start(b1[:], column(d["L1_xcond_mlp_b1"])).then_inc(small_in, DMA)
                for b in range(B):
                    sp.dma_start(brow[:, b], d["L1_xcond_mlp_b2"].partition_broadcast(P)).then_inc(small_in, DMA)
                    sp.dma_start(grow[:, b], gate[b].partition_broadcast(P)).then_inc(small_in, DMA)

            def load_u(i, b, first=False):
                if not first:
                    sp.wait_ge(used, (2 * i + b - 1) * HT + 2)
                    sp.sem_inc(passed, 1)
                for part in range(2):
                    sp.dma_start(us[:, b, part].bitcast(F32), u_in[part, b, :, bass.ds(i * W, W)].rearrange("(t p) w -> p t w", p=P)).then_inc(u_loaded[b], DMA)

            def chunk(i, b, left):
                sp.wait_ge(stored, DMA * (2 * i + b + 1))
                sp.sem_inc(passed, 1)
                sp.dma_start(x[:], x_in[b, bass.ds(i * W, W), :].rearrange("(t p) c -> p t c", p=P)).then_inc(x_loaded, DMA)
                if left > 1:
                    load_u(*chunk_after(i, b))
                sp.wait_ge(x_ready, (2 * i + b + 1) * TT)
                sp.sem_inc(passed, 1)
                sp.dma_start(out[b, bass.ds(i * W, W), :].rearrange("(t p) c -> p t c", p=P), x[:]).then_inc(stored, DMA)

            load_u(0, 0, True)
            load_small()
            with sp.Fori(0, CHUNKS - 1) as i:
                for b in range(B):
                    chunk(i, b, 3)
            for b in range(B):
                chunk(CHUNKS - 1, b, B - b)
            sp.wait_ge(stored, DMA * (B * CHUNKS + 1))

        @block.tensor
        def _(pe):
            def hidden(i, b, m):
                n = 2 * i + b
                if m == 0:
                    pe.wait_ge(u_loaded[b], 2 * DMA * (i + 1))
                pe.wait_ge(gelu_done, n * HT + m + 1)
                for t in range(KT):
                    for s, (pm, pw) in enumerate(PARTS):
                        mm = pe.matmul(ph[:, m % 4], w1[pw][:, t, m * P:(m + 1) * P], us[:, b, pm, t],
                                       start=(t == 0 and s == 0), stop=(t == KT - 1 and s == 2))
                mm.then_inc(hidden_done, 1)

            def output(i, b, m):
                n = 2 * i + b
                if m == 0:
                    pe.wait_ge(w_lo, NP)
                    pe.wait_ge(y_read, n * TT + 1)
                pe.wait_ge(g_lo, n * HT + m + 1)
                for tt in range(TT):
                    for s, (pm, pw) in enumerate(PARTS):
                        mm = pe.matmul(py[:, tt], gs[:, m % 2, pw, tt * P:(tt + 1) * P], w2[pm][:, m],
                                       start=(m == 0 and s == 0), stop=(m == HT - 1 and s == 2))
                mm.then_inc(used, 1)

            pe.sem_inc(used, 2)
            pe.wait_ge(w_lo, KT)
            with pe.Fori(0, CHUNKS) as i:
                for b in range(B):
                    for m in range(HT + 1):
                        if m < HT:
                            hidden(i, b, m)
                        if m > 0:
                            output(i, b, m - 1)

        @block.scalar
        def _(act):
            act.sem_inc(gelu_done, 4)
            for hi, _, raw in pieces:
                act.activation(hi, raw, ACT.Copy).then_inc(w_hi, 1)
            act.wait_ge(small_in, DMA * SMALL)
            with act.Fori(0, CHUNKS) as i:
                for b in range(B):
                    n = 2 * i + b
                    for m in range(HT):
                        act.wait_ge(used, n * HT + m + 1)
                        act.wait_ge(hidden_done, n * HT + m + 1)
                        act.activation(gelu[:, m % 2], ph[:, m % 4], ACT.Gelu_apprx_tanh, bias=b1[:, m:m + 1]).then_inc(gelu_done, 1)

        @block.vector
        def _(dve):
            dve.sem_inc(y_read, 1)
            for k, (hi, lo, raw) in enumerate(pieces):
                dve.wait_ge(w_hi, k + 1)
                dve.tensor_tensor(lo, raw, hi.bitcast(F32), ALU.subtract).then_inc(w_lo, 1)
            dve.wait_ge(small_in, DMA * SMALL)
            with dve.Fori(0, CHUNKS) as i:
                for b in range(B):
                    n = 2 * i + b
                    for m in range(HT):
                        dve.wait_ge(gelu_done, n * HT + m + 5)
                        dve.wait_ge(used, n * HT + m + 1)
                        dve.tensor_copy(gs[:, m % 2, 0], gelu[:, m % 2]).then_inc(g_hi, 1)
                        dve.wait_ge(g_hi, n * HT + m + 1)
                        dve.tensor_tensor(gs[:, m % 2, 1], gelu[:, m % 2], gs[:, m % 2, 0].bitcast(F32), ALU.subtract).then_inc(g_lo, 1)
                    dve.wait_ge(used, (n + 1) * HT + 2)
                    dve.wait_ge(biased, n + 1)
                    for tt in range(TT):
                        dve.tensor_tensor(gated[:, tt % 2], py[:, tt], grow[:, b], ALU.mult).then_inc(y_read, 1)
                        dve.wait_ge(y_read, n * TT + tt + 2)
                        dve.tensor_tensor(x[:, tt], x[:, tt], gated[:, tt % 2], ALU.add).then_inc(x_ready, 1)

        @block.gpsimd
        def _(pool):
            pool.wait_ge(small_in, DMA * SMALL)
            pool.tensor_tensor(brow[:], brow[:], grow[:], ALU.mult).then_inc(rows_done, 1)
            pool.wait_ge(rows_done, 1)
            with pool.Fori(0, CHUNKS) as i:
                for b in range(B):
                    pool.wait_ge(x_loaded, DMA * (2 * i + b + 1))
                    pool.tensor_tensor(x[:], x[:], brow[:, b].unsqueeze(1).to_broadcast([P, TT, C]), ALU.add).then_inc(biased, 1)


def build(nc, d, out):
    def dram(name, shape, t=F32):
        return nc.dram_tensor("s_" + name, shape, t, kind="Internal").ap()

    q, k = dram("q", [2, B, C, T]), dram("k", [2, B, C, T])
    v, o = dram("v", [B, T, C]), dram("o", [B, C, T])
    x1, x2, x3 = dram("x1", [B, T, C]), dram("x2", [B, T, C]), dram("x3", [B, T, C])
    u = dram("u", [2, B, C, T])
    gates = dram("gates", [2, B, C])
    kv = [(dram(f"k{a}", [2, B, C, S]), dram(f"v{a}", [B, S, C])) for a in range(2)]
    w = lambda name, c: d[name][:, c * C:(c + 1) * C]
    vec = lambda name, c: d[name][c * C:(c + 1) * C]

    def raw_weights(name, *weights):
        room = Weights(nc, ctx, name, [len(weights), KT, C])
        return room, [(room.raw[:, x], channels(weight)) for x, weight in enumerate(weights)]

    with nc.sbuf_tensor("mod", [P, MODS, B], F32) as mod:
        def vector_of(tile):
            return lambda b, t: mod[:, tile + t, b:b + 1]

        with ExitStack() as ctx:
            raw, preload = raw_weights("raw_p1", d["L0_xcond_Wq"])
            conditioning(nc, d, mod, gates, kv, preload)
            chunk_pass(nc, d, "p1", d["x"], None, None, None, None, 1e-5, vector_of(0), vector_of(4),
                       [(d["L0_xcond_bq"], q)], None, raw)
        with ExitStack() as ctx:
            raw, preload = raw_weights("raw_p2", d["L0_xcond_Wp"], *[w("L1_xcond_qkv_w", c) for c in range(3)])
            attention(nc, d, "a1", q, kv[0][0], kv[0][1], o, S, preload)
            chunk_pass(nc, d, "p2", d["x"], x1, o, d["L0_xcond_bp"], None, 1e-6, vector_of(20), vector_of(16),
                       [(vec("L1_xcond_qkv_b", 0), q), (vec("L1_xcond_qkv_b", 1), k)], (vec("L1_xcond_qkv_b", 2), v), raw)
        with ExitStack() as ctx:
            raw, preload = raw_weights("raw_p3", d["L1_xcond_self_o_w"], d["L1_xcond_q_w"])
            attention(nc, d, "a2", q, k, v, o, T, preload)
            chunk_pass(nc, d, "p3", x1, x2, o, d["L1_xcond_self_o_b"], gates[0], 1e-6,
                       lambda b, t: mod[:, 40 + t, 0:1], lambda b, t: mod[:, 40 + t, 1:2], [(d["L1_xcond_q_b"], q)], None, raw)
        with ExitStack() as ctx:
            raw, preload = raw_weights("raw_p4", d["L1_xcond_cross_o_w"])
            attention(nc, d, "a3", q, kv[1][0], kv[1][1], o, S, preload)
            raw1 = Weights(nc, ctx, "raw_mlp1", [KT, HID])
            raw2 = Weights(nc, ctx, "raw_mlp2", [HT, C])
            chunk_pass(nc, d, "p4", x2, x3, o, d["L1_xcond_cross_o_b"], None, 1e-6, vector_of(32), vector_of(28),
                       [], None, raw, plain=u, prefetch=[(raw1.raw, d["L1_xcond_mlp_w1"]), (raw2.raw, d["L1_xcond_mlp_w2"])])
            mlp(nc, d, u, x3, gates[1], raw1, raw2, out)


def kernel(**inputs):
    import concourse.bacc as bacc
    from concourse.bass_utils import run_bass_kernel_spmd

    nc = bacc.Bacc("TRN2", target_bir_lowering=False, num_devices=1)
    arrays = {f"in_{name}": np.ascontiguousarray(a) for name, a in inputs.items()}
    arrays["in_ident"] = np.eye(P, dtype=np.float32)
    arrays["in_mask"] = np.zeros((P, GH), np.float32)
    for h in range(GH):
        arrays["in_mask"][3 * DH + 2 * h:3 * DH + 2 * h + 2, h] = 1.0
    d = {k[3:]: nc.dram_tensor(k, a.shape, mybir.dt.from_np(a.dtype), kind="ExternalInput").ap() for k, a in arrays.items()}
    out = nc.dram_tensor("out", (B, T, C), F32, kind="ExternalOutput").ap()
    build(nc, d, out)
    r = run_bass_kernel_spmd(nc, [arrays], core_ids=[0])
    return r.results[0]["out"]
```
